# Optimizing a Trainium2 kernel written in Bass

```python
import numpy as np
import jax
import jax.numpy as jnp

def _softmax(x, axis=-1):
    return jax.nn.softmax(x, axis=axis)

def _gelu(x):
    return jax.nn.gelu(x, approximate=True)

def _silu(x):
    return jax.nn.silu(x)

def _sigmoid(x):
    return jax.nn.sigmoid(x)

def _layernorm(x, axis=-1, eps=1e-05):
    m = jnp.mean(x, axis=axis, keepdims=True)
    v = jnp.var(x, axis=axis, keepdims=True)
    return (x - m) / jnp.sqrt(v + eps)

def _scatter_add(tgt, idx, src, axis=0):
    return tgt.at[idx].add(src)

def _segment_sum(src, seg, n):
    return jax.ops.segment_sum(src, seg, n)
kernel_name = 'mk_pixart_seq_d4_seqx_r4_83da0c'

def setup_inputs(seed: int=0):
    np.random.seed(seed)
    _w = jnp.asarray

    def _rec_inputs():
        import jax
        import jax.numpy as jnp
        _rk = jax.random.key(seed)
        x = 7.22e-05 + 1 * jax.random.normal(jax.random.fold_in(_rk, 1), (16, 128, 256), jnp.float32)
        _lenS = 128 - jax.random.randint(jax.random.fold_in(_rk, 7), (16,), 0, max(1, 128 // 4) + 1, jnp.int32)
        _lenS2 = 128 - jax.random.randint(jax.random.fold_in(_rk, 8), (16,), 0, max(1, 128 // 4) + 1, jnp.int32)
        cond_1024 = 0.000887014 + 1.03683 * jax.random.normal(jax.random.fold_in(_rk, 11), (16, 256), jnp.float32)
        _ctx_1024P = jax.random.normal(jax.random.fold_in(_rk, 12), (16, 16, 256), jnp.float32)
        _ctx_1024c = jax.random.dirichlet(jax.random.fold_in(_rk, 512), 0.3 * jnp.ones((16,), jnp.float32), (16, 128))
        _ctx_1024t = jnp.einsum('bsk,bkd->bsd', _ctx_1024c, _ctx_1024P)
        _ctx_1024t = _ctx_1024t * jax.lax.rsqrt(jnp.mean(jnp.square(_ctx_1024t)) + 1e-12) * 0.953939
        ctx_1024 = 0.00086875 + 0.999764 * (_ctx_1024t + 0.3 * jax.random.normal(jax.random.fold_in(_rk, 612), (16, 128, 256), jnp.float32))
        return (x, cond_1024, ctx_1024)
    x, cond_1024, ctx_1024 = _rec_inputs()

    def _L0_xcond_setup():
        import jax, jax.numpy as jnp
        import numpy as np
        C = 256
        H = 16
        D = C // H
        WIN = 128
        SHIFT = 64
        TOPK = 16
        HID = 1024
        EPS = 1e-06

        def _ln(x):
            x32 = x.astype(jnp.float32)
            m = x32.mean(-1, keepdims=True)
            v = jnp.mean((x32 - m) ** 2, axis=-1, keepdims=True)
            return ((x32 - m) * jax.lax.rsqrt(v + EPS)).astype(x.dtype)

        def _self_attn(h, w_qkv, b_qkv, w_so, b_so):
            B, L, _ = h.shape
            qkv = h @ w_qkv + b_qkv
            qkv = jnp.roll(qkv, -SHIFT, axis=1)
            nw = L // WIN
            qkv = qkv.reshape(B, nw, WIN, 3, H, D)
            q, k, v = (qkv[:, :, :, 0], qkv[:, :, :, 1], qkv[:, :, :, 2])
            scores = jnp.einsum('bnqhd,bnkhd->bnhqk', q, k) / jnp.sqrt(jnp.float32(D)).astype(h.dtype)
            attn = jax.nn.softmax(scores, axis=-1)
            o = jnp.einsum('bnhqk,bnkhd->bnqhd', attn, v).reshape(B, L, C)
            o = jnp.roll(o, SHIFT, axis=1)
            return o @ w_so + b_so

        def _topk_cross_attn(h, ctx, w_q, b_q, w_kv, b_kv, w_co, b_co):
            B, L, _ = h.shape
            Lc = ctx.shape[1]
            q = (h @ w_q + b_q).reshape(B, L, H, D)
            kv = (ctx @ w_kv + b_kv).reshape(B, Lc, 2, H, D)
            k, v = (kv[:, :, 0], kv[:, :, 1])
            scores = jnp.einsum('bqhd,bkhd->bhqk', q, k) / jnp.sqrt(jnp.float32(D)).astype(h.dtype)
            top_s, top_i = jax.lax.top_k(scores, TOPK)
            attn = jax.nn.softmax(top_s, axis=-1)
            v_bh = jnp.transpose(v, (0, 2, 1, 3))
            vg = jnp.take_along_axis(v_bh[:, :, None, :, :], top_i[..., None], axis=3)
            o = jnp.einsum('bhqk,bhqkd->bqhd', attn, vg).reshape(B, L, C)
            return o @ w_co + b_co

        def _swiglu(h, w_m1, b_m1, w_m2, b_m2):
            u = h @ w_m1 + b_m1
            a, b = (u[..., :HID], u[..., HID:])
            return jax.nn.silu(a) * b @ w_m2 + b_m2
        key = jax.random.key(seed)
        ks = jax.random.split(key, 24)
        s = 0.02
        inp = {'x': jax.random.normal(ks[0], (2, 1024, C), jnp.float32), 'mod': jax.random.normal(ks[1], (2, C), jnp.float32), 'context': jax.random.normal(ks[2], (2, 256, C), jnp.float32), 'w_ada': jax.random.normal(ks[3], (C, 9 * C), jnp.float32) * s, 'b_ada': jnp.zeros((9 * C,), jnp.float32), 'w_qkv': jax.random.normal(ks[4], (C, 3 * C), jnp.float32) * s, 'b_qkv': jnp.zeros((3 * C,), jnp.float32), 'w_so': jax.random.normal(ks[5], (C, C), jnp.float32) * s, 'b_so': jnp.zeros((C,), jnp.float32), 'w_q': jax.random.normal(ks[6], (C, C), jnp.float32) * s, 'b_q': jnp.zeros((C,), jnp.float32), 'w_kv': jax.random.normal(ks[7], (C, 2 * C), jnp.float32) * s, 'b_kv': jnp.zeros((2 * C,), jnp.float32), 'w_co': jax.random.normal(ks[8], (C, C), jnp.float32) * s, 'b_co': jnp.zeros((C,), jnp.float32), 'w_m1': jax.random.normal(ks[9], (C, 2 * HID), jnp.float32) * s, 'b_m1': jnp.zeros((2 * HID,), jnp.float32), 'w_m2': jax.random.normal(ks[10], (HID, C), jnp.float32) * s, 'b_m2': jnp.zeros((C,), jnp.float32)}
        return inp
    _L0_xcond_all = _L0_xcond_setup()
    _L0_xcond_in = {k: v for k, v in _L0_xcond_all.items() if k in ('w_ada', 'b_ada', 'w_qkv', 'b_qkv', 'w_so', 'b_so', 'w_q', 'b_q', 'w_kv', 'b_kv', 'w_co', 'b_co', 'w_m1', 'b_m1', 'w_m2', 'b_m2')}
    del _L0_xcond_all

    def _L1_xcond_setup():
        import jax, jax.numpy as jnp
        import numpy as np
        LN_EPS = 1e-06

        def _ln(x):
            mu = jnp.mean(x, axis=-1, keepdims=True)
            var = jnp.var(x, axis=-1, keepdims=True)
            return (x - mu) * jax.lax.rsqrt(var + LN_EPS)
        key = jax.random.key(seed)
        H, NH = (256, 16)
        B, N, S = (4, 256, 77)
        MLP = int(H * 4.0)
        ks = jax.random.split(key, 20)
        s = 1.0 / np.sqrt(H)
        return {'x': jax.random.normal(ks[0], (B, N, H), jnp.float32), 'c': jax.random.normal(ks[1], (B, H), jnp.float32), 'context': jax.random.normal(ks[2], (B, S, H), jnp.float32), 'W_mod': jax.random.normal(ks[3], (H, 6 * H), jnp.float32) * s, 'b_mod': jnp.zeros((6 * H,), jnp.float32), 'W_qkv': jax.random.normal(ks[4], (H, 3 * H), jnp.float32) * s, 'b_qkv': jnp.zeros((3 * H,), jnp.float32), 'W_proj': jax.random.normal(ks[5], (H, H), jnp.float32) * s, 'b_proj': jnp.zeros((H,), jnp.float32), 'W_qc': jax.random.normal(ks[6], (H, H), jnp.float32) * s, 'b_qc': jnp.zeros((H,), jnp.float32), 'W_kvc': jax.random.normal(ks[7], (H, 2 * H), jnp.float32) * s, 'b_kvc': jnp.zeros((2 * H,), jnp.float32), 'W_cproj': jax.random.normal(ks[8], (H, H), jnp.float32) * s, 'b_cproj': jnp.zeros((H,), jnp.float32), 'W_mlp1': jax.random.normal(ks[9], (H, MLP), jnp.float32) * s, 'b_mlp1': jnp.zeros((MLP,), jnp.float32), 'W_mlp2': jax.random.normal(ks[10], (MLP, H), jnp.float32) * (1.0 / np.sqrt(MLP)), 'b_mlp2': jnp.zeros((H,), jnp.float32)}
    _L1_xcond_all = _L1_xcond_setup()
    _L1_xcond_in = {k: v for k, v in _L1_xcond_all.items() if k in ('W_mod', 'b_mod', 'W_qkv', 'b_qkv', 'W_proj', 'b_proj', 'W_qc', 'b_qc', 'W_kvc', 'b_kvc', 'W_cproj', 'b_cproj', 'W_mlp1', 'b_mlp1', 'W_mlp2', 'b_mlp2')}
    del _L1_xcond_all

    def _L2_xcond_setup():
        import jax, jax.numpy as jnp
        import numpy as np
        D = 256
        H = 16
        HD = D // H
        MLP = 4 * D
        EPS = 1e-06
        SCALE = HD ** (-0.5)

        def _p(key, shape, s=0.02):
            return jax.random.normal(key, shape, dtype=jnp.float32) * s

        def _ln(x):
            mu = jnp.mean(x, axis=-1, keepdims=True)
            var = jnp.var(x, axis=-1, keepdims=True)
            return (x - mu) * jax.lax.rsqrt(var + EPS)

        def _heads(t):
            B, L, _ = t.shape
            return t.reshape(B, L, H, HD).transpose(0, 2, 1, 3)

        def _attend(q, k, v):
            attn = jnp.einsum('bhnd,bhsd->bhns', q, k) * SCALE
            attn = jax.nn.softmax(attn, axis=-1)
            o = jnp.einsum('bhns,bhsd->bhnd', attn, v)
            B, _, N, _ = q.shape
            return o.transpose(0, 2, 1, 3).reshape(B, N, D)
        key = jax.random.key(seed)
        ks = jax.random.split(key, 24)
        B, N, S = (4, 256, 77)
        return {'x': jax.random.normal(ks[0], (B, N, D), dtype=jnp.float32), 't_emb': jax.random.normal(ks[1], (B, D), dtype=jnp.float32), 'context': jax.random.normal(ks[2], (B, S, D), dtype=jnp.float32), 'adaln_w': _p(ks[3], (D, 6 * D)), 'adaln_b': _p(ks[4], (6 * D,)), 'qkv_w': _p(ks[5], (D, 3 * D)), 'qkv_b': _p(ks[6], (3 * D,)), 'sa_proj_w': _p(ks[7], (D, D)), 'sa_proj_b': _p(ks[8], (D,)), 'q_w': _p(ks[9], (D, D)), 'q_b': _p(ks[10], (D,)), 'kv_w': _p(ks[11], (D, 2 * D)), 'kv_b': _p(ks[12], (2 * D,)), 'ca_proj_w': _p(ks[13], (D, D)), 'ca_proj_b': _p(ks[14], (D,)), 'fc1_w': _p(ks[15], (D, MLP)), 'fc1_b': _p(ks[16], (MLP,)), 'fc2_w': _p(ks[17], (MLP, D)), 'fc2_b': _p(ks[18], (D,))}
    _L2_xcond_all = _L2_xcond_setup()
    _L2_xcond_in = {k: v for k, v in _L2_xcond_all.items() if k in ('adaln_w', 'adaln_b', 'qkv_w', 'qkv_b', 'sa_proj_w', 'sa_proj_b', 'q_w', 'q_b', 'kv_w', 'kv_b', 'ca_proj_w', 'ca_proj_b', 'fc1_w', 'fc1_b', 'fc2_w', 'fc2_b')}
    del _L2_xcond_all

    def _L3_xcond_setup():
        import jax, jax.numpy as jnp
        import numpy as np
        import math
        D_MODEL = 256
        N_HEADS = 16
        HEAD_DIM = D_MODEL // N_HEADS
        D_FF = 1024
        EPS = 1e-05
        ROPE_BASE = 10000.0

        def _rope(t):
            L, Dh = (t.shape[1], t.shape[-1])
            half = Dh // 2
            inv_freq = 1.0 / ROPE_BASE ** (jnp.arange(half, dtype=t.dtype) / half)
            ang = jnp.arange(L, dtype=t.dtype)[:, None] * inv_freq[None, :]
            cos = jnp.cos(ang)[None, :, None, :]
            sin = jnp.sin(ang)[None, :, None, :]
            t1, t2 = (t[..., :half], t[..., half:])
            return jnp.concatenate([t1 * cos - t2 * sin, t2 * cos + t1 * sin], axis=-1)

        def _adaln(x, emb, w, b):
            e = emb[:, 0, :]
            gb = e @ w.T + b
            gamma, beta = jnp.split(gb, 2, axis=-1)
            mu = x.mean(-1, keepdims=True)
            var = x.var(-1, keepdims=True)
            xn = (x - mu) * jax.lax.rsqrt(var + EPS)
            return xn * (1.0 + gamma[:, None, :]) + beta[:, None, :]

        def _attn(q, k, v):
            scale = 1.0 / math.sqrt(HEAD_DIM)
            scores = jnp.einsum('bqhd,bkhd->bhqk', q, k) * scale
            w = jax.nn.softmax(scores, axis=-1)
            out = jnp.einsum('bhqk,bkhd->bqhd', w, v)
            B, Lq = (out.shape[0], out.shape[1])
            return out.reshape(B, Lq, D_MODEL)
        key = jax.random.key(seed)
        ks = jax.random.split(key, 24)
        s = 0.02
        inp = {'x': jax.random.normal(ks[0], (2, 512, D_MODEL), jnp.float32), 'noise_emb': jax.random.normal(ks[1], (2, 1, D_MODEL), jnp.float32), 'context': jax.random.normal(ks[2], (2, 256, D_MODEL), jnp.float32), 'ln1_w': jax.random.normal(ks[3], (2 * D_MODEL, D_MODEL), jnp.float32) * s, 'ln1_b': jax.random.normal(ks[4], (2 * D_MODEL,), jnp.float32) * s, 'ln2_w': jax.random.normal(ks[5], (2 * D_MODEL, D_MODEL), jnp.float32) * s, 'ln2_b': jax.random.normal(ks[6], (2 * D_MODEL,), jnp.float32) * s, 'ln3_w': jax.random.normal(ks[7], (2 * D_MODEL, D_MODEL), jnp.float32) * s, 'ln3_b': jax.random.normal(ks[8], (2 * D_MODEL,), jnp.float32) * s, 'qkv_w': jax.random.normal(ks[9], (3 * D_MODEL, D_MODEL), jnp.float32) * s, 'sa_out_w': jax.random.normal(ks[10], (D_MODEL, D_MODEL), jnp.float32) * s, 'q_w': jax.random.normal(ks[11], (D_MODEL, D_MODEL), jnp.float32) * s, 'k_w': jax.random.normal(ks[12], (D_MODEL, D_MODEL), jnp.float32) * s, 'v_w': jax.random.normal(ks[13], (D_MODEL, D_MODEL), jnp.float32) * s, 'ca_out_w': jax.random.normal(ks[14], (D_MODEL, D_MODEL), jnp.float32) * s, 'ffn_w1': jax.random.normal(ks[15], (D_FF, D_MODEL), jnp.float32) * s, 'ffn_b1': jax.random.normal(ks[16], (D_FF,), jnp.float32) * s, 'ffn_w2': jax.random.normal(ks[17], (D_MODEL, D_FF), jnp.float32) * s, 'ffn_b2': jax.random.normal(ks[18], (D_MODEL,), jnp.float32) * s}
        return inp
    _L3_xcond_all = _L3_xcond_setup()
    _L3_xcond_in = {k: v for k, v in _L3_xcond_all.items() if k in ('ln1_w', 'ln1_b', 'ln2_w', 'ln2_b', 'ln3_w', 'ln3_b', 'qkv_w', 'sa_out_w', 'q_w', 'k_w', 'v_w', 'ca_out_w', 'ffn_w1', 'ffn_b1', 'ffn_w2', 'ffn_b2')}
    del _L3_xcond_all
    return {'x': x, 'cond_1024': cond_1024, 'ctx_1024': ctx_1024, 'L0_xcond_w_ada': _L0_xcond_in['w_ada'], 'L0_xcond_b_ada': _L0_xcond_in['b_ada'], 'L0_xcond_w_qkv': _L0_xcond_in['w_qkv'], 'L0_xcond_b_qkv': _L0_xcond_in['b_qkv'], 'L0_xcond_w_so': _L0_xcond_in['w_so'], 'L0_xcond_b_so': _L0_xcond_in['b_so'], 'L0_xcond_w_q': _L0_xcond_in['w_q'], 'L0_xcond_b_q': _L0_xcond_in['b_q'], 'L0_xcond_w_kv': _L0_xcond_in['w_kv'], 'L0_xcond_b_kv': _L0_xcond_in['b_kv'], 'L0_xcond_w_co': _L0_xcond_in['w_co'], 'L0_xcond_b_co': _L0_xcond_in['b_co'], 'L0_xcond_w_m1': _L0_xcond_in['w_m1'], 'L0_xcond_b_m1': _L0_xcond_in['b_m1'], 'L0_xcond_w_m2': _L0_xcond_in['w_m2'], 'L0_xcond_b_m2': _L0_xcond_in['b_m2'], 'L1_xcond_W_mod': _L1_xcond_in['W_mod'], 'L1_xcond_b_mod': _L1_xcond_in['b_mod'], 'L1_xcond_W_qkv': _L1_xcond_in['W_qkv'], 'L1_xcond_b_qkv': _L1_xcond_in['b_qkv'], 'L1_xcond_W_proj': _L1_xcond_in['W_proj'], 'L1_xcond_b_proj': _L1_xcond_in['b_proj'], 'L1_xcond_W_qc': _L1_xcond_in['W_qc'], 'L1_xcond_b_qc': _L1_xcond_in['b_qc'], 'L1_xcond_W_kvc': _L1_xcond_in['W_kvc'], 'L1_xcond_b_kvc': _L1_xcond_in['b_kvc'], 'L1_xcond_W_cproj': _L1_xcond_in['W_cproj'], 'L1_xcond_b_cproj': _L1_xcond_in['b_cproj'], 'L1_xcond_W_mlp1': _L1_xcond_in['W_mlp1'], 'L1_xcond_b_mlp1': _L1_xcond_in['b_mlp1'], 'L1_xcond_W_mlp2': _L1_xcond_in['W_mlp2'], 'L1_xcond_b_mlp2': _L1_xcond_in['b_mlp2'], 'L2_xcond_adaln_w': _L2_xcond_in['adaln_w'], 'L2_xcond_adaln_b': _L2_xcond_in['adaln_b'], 'L2_xcond_qkv_w': _L2_xcond_in['qkv_w'], 'L2_xcond_qkv_b': _L2_xcond_in['qkv_b'], 'L2_xcond_sa_proj_w': _L2_xcond_in['sa_proj_w'], 'L2_xcond_sa_proj_b': _L2_xcond_in['sa_proj_b'], 'L2_xcond_q_w': _L2_xcond_in['q_w'], 'L2_xcond_q_b': _L2_xcond_in['q_b'], 'L2_xcond_kv_w': _L2_xcond_in['kv_w'], 'L2_xcond_kv_b': _L2_xcond_in['kv_b'], 'L2_xcond_ca_proj_w': _L2_xcond_in['ca_proj_w'], 'L2_xcond_ca_proj_b': _L2_xcond_in['ca_proj_b'], 'L2_xcond_fc1_w': _L2_xcond_in['fc1_w'], 'L2_xcond_fc1_b': _L2_xcond_in['fc1_b'], 'L2_xcond_fc2_w': _L2_xcond_in['fc2_w'], 'L2_xcond_fc2_b': _L2_xcond_in['fc2_b'], 'L3_xcond_ln1_w': _L3_xcond_in['ln1_w'], 'L3_xcond_ln1_b': _L3_xcond_in['ln1_b'], 'L3_xcond_ln2_w': _L3_xcond_in['ln2_w'], 'L3_xcond_ln2_b': _L3_xcond_in['ln2_b'], 'L3_xcond_ln3_w': _L3_xcond_in['ln3_w'], 'L3_xcond_ln3_b': _L3_xcond_in['ln3_b'], 'L3_xcond_qkv_w': _L3_xcond_in['qkv_w'], 'L3_xcond_sa_out_w': _L3_xcond_in['sa_out_w'], 'L3_xcond_q_w': _L3_xcond_in['q_w'], 'L3_xcond_k_w': _L3_xcond_in['k_w'], 'L3_xcond_v_w': _L3_xcond_in['v_w'], 'L3_xcond_ca_out_w': _L3_xcond_in['ca_out_w'], 'L3_xcond_ffn_w1': _L3_xcond_in['ffn_w1'], 'L3_xcond_ffn_b1': _L3_xcond_in['ffn_b1'], 'L3_xcond_ffn_w2': _L3_xcond_in['ffn_w2'], 'L3_xcond_ffn_b2': _L3_xcond_in['ffn_b2']}

def reference(x, cond_1024, ctx_1024, L0_xcond_w_ada, L0_xcond_b_ada, L0_xcond_w_qkv, L0_xcond_b_qkv, L0_xcond_w_so, L0_xcond_b_so, L0_xcond_w_q, L0_xcond_b_q, L0_xcond_w_kv, L0_xcond_b_kv, L0_xcond_w_co, L0_xcond_b_co, L0_xcond_w_m1, L0_xcond_b_m1, L0_xcond_w_m2, L0_xcond_b_m2, L1_xcond_W_mod, L1_xcond_b_mod, L1_xcond_W_qkv, L1_xcond_b_qkv, L1_xcond_W_proj, L1_xcond_b_proj, L1_xcond_W_qc, L1_xcond_b_qc, L1_xcond_W_kvc, L1_xcond_b_kvc, L1_xcond_W_cproj, L1_xcond_b_cproj, L1_xcond_W_mlp1, L1_xcond_b_mlp1, L1_xcond_W_mlp2, L1_xcond_b_mlp2, L2_xcond_adaln_w, L2_xcond_adaln_b, L2_xcond_qkv_w, L2_xcond_qkv_b, L2_xcond_sa_proj_w, L2_xcond_sa_proj_b, L2_xcond_q_w, L2_xcond_q_b, L2_xcond_kv_w, L2_xcond_kv_b, L2_xcond_ca_proj_w, L2_xcond_ca_proj_b, L2_xcond_fc1_w, L2_xcond_fc1_b, L2_xcond_fc2_w, L2_xcond_fc2_b, L3_xcond_ln1_w, L3_xcond_ln1_b, L3_xcond_ln2_w, L3_xcond_ln2_b, L3_xcond_ln3_w, L3_xcond_ln3_b, L3_xcond_qkv_w, L3_xcond_sa_out_w, L3_xcond_q_w, L3_xcond_k_w, L3_xcond_v_w, L3_xcond_ca_out_w, L3_xcond_ffn_w1, L3_xcond_ffn_b1, L3_xcond_ffn_w2, L3_xcond_ffn_b2):
    import jax
    import jax.numpy as jnp

    def _L0_xcond_ref(x, mod, context, w_ada, b_ada, w_qkv, b_qkv, w_so, b_so, w_q, b_q, w_kv, b_kv, w_co, b_co, w_m1, b_m1, w_m2, b_m2):
        import jax, jax.numpy as jnp
        import numpy as np
        C = 256
        H = 16
        D = C // H
        WIN = 128
        SHIFT = 64
        TOPK = 16
        HID = 1024
        EPS = 1e-06

        def _ln(x):
            x32 = x.astype(jnp.float32)
            m = x32.mean(-1, keepdims=True)
            v = jnp.mean((x32 - m) ** 2, axis=-1, keepdims=True)
            return ((x32 - m) * jax.lax.rsqrt(v + EPS)).astype(x.dtype)

        def _self_attn(h, w_qkv, b_qkv, w_so, b_so):
            B, L, _ = h.shape
            qkv = h @ w_qkv + b_qkv
            qkv = jnp.roll(qkv, -SHIFT, axis=1)
            nw = L // WIN
            qkv = qkv.reshape(B, nw, WIN, 3, H, D)
            q, k, v = (qkv[:, :, :, 0], qkv[:, :, :, 1], qkv[:, :, :, 2])
            scores = jnp.einsum('bnqhd,bnkhd->bnhqk', q, k) / jnp.sqrt(jnp.float32(D)).astype(h.dtype)
            attn = jax.nn.softmax(scores, axis=-1)
            o = jnp.einsum('bnhqk,bnkhd->bnqhd', attn, v).reshape(B, L, C)
            o = jnp.roll(o, SHIFT, axis=1)
            return o @ w_so + b_so

        def _topk_cross_attn(h, ctx, w_q, b_q, w_kv, b_kv, w_co, b_co):
            B, L, _ = h.shape
            Lc = ctx.shape[1]
            q = (h @ w_q + b_q).reshape(B, L, H, D)
            kv = (ctx @ w_kv + b_kv).reshape(B, Lc, 2, H, D)
            k, v = (kv[:, :, 0], kv[:, :, 1])
            scores = jnp.einsum('bqhd,bkhd->bhqk', q, k) / jnp.sqrt(jnp.float32(D)).astype(h.dtype)
            top_s, top_i = jax.lax.top_k(scores, TOPK)
            attn = jax.nn.softmax(top_s, axis=-1)
            v_bh = jnp.transpose(v, (0, 2, 1, 3))
            vg = jnp.take_along_axis(v_bh[:, :, None, :, :], top_i[..., None], axis=3)
            o = jnp.einsum('bhqk,bhqkd->bqhd', attn, vg).reshape(B, L, C)
            return o @ w_co + b_co

        def _swiglu(h, w_m1, b_m1, w_m2, b_m2):
            u = h @ w_m1 + b_m1
            a, b = (u[..., :HID], u[..., HID:])
            return jax.nn.silu(a) * b @ w_m2 + b_m2
        m = jax.nn.silu(mod) @ w_ada + b_ada
        sh_msa, sc_msa, g_msa, sh_mca, sc_mca, g_mca, sh_mlp, sc_mlp, g_mlp = [m[:, i * C:(i + 1) * C][:, None, :] for i in range(9)]
        h = _ln(x) * (1 + sc_msa) + sh_msa
        h = _self_attn(h, w_qkv, b_qkv, w_so, b_so)
        x = x + h * g_msa
        h = _ln(x) * (1 + sc_mca) + sh_mca
        h = _topk_cross_attn(h, context, w_q, b_q, w_kv, b_kv, w_co, b_co)
        x = x + h * g_mca
        h = _ln(x) * (1 + sc_mlp) + sh_mlp
        h = _swiglu(h, w_m1, b_m1, w_m2, b_m2)
        x = x + h * g_mlp
        return x

    def _L1_xcond_ref(x, c, context, W_mod, b_mod, W_qkv, b_qkv, W_proj, b_proj, W_qc, b_qc, W_kvc, b_kvc, W_cproj, b_cproj, W_mlp1, b_mlp1, W_mlp2, b_mlp2):
        import jax, jax.numpy as jnp
        import numpy as np
        LN_EPS = 1e-06

        def _ln(x):
            mu = jnp.mean(x, axis=-1, keepdims=True)
            var = jnp.var(x, axis=-1, keepdims=True)
            return (x - mu) * jax.lax.rsqrt(var + LN_EPS)
        B, N, H = x.shape
        NH = 16
        hd = H // NH
        scale = hd ** (-0.5)
        c_proj = jax.nn.silu(c) @ W_mod + b_mod
        shift_a, scale_a, gate_a, shift_m, scale_m, gate_m = jnp.split(c_proj, 6, axis=-1)

        def modulate(t, shift, sc):
            return t * (1 + sc[:, None]) + shift[:, None]
        x_norm = modulate(_ln(x), shift_a, scale_a)
        qkv = x_norm @ W_qkv + b_qkv
        q, k, v = jnp.split(qkv, 3, axis=-1)
        q = q.reshape(B, N, NH, hd).transpose(0, 2, 1, 3)
        k = k.reshape(B, N, NH, hd).transpose(0, 2, 1, 3)
        v = v.reshape(B, N, NH, hd).transpose(0, 2, 1, 3)
        attn_w = jax.nn.softmax(jnp.einsum('bhqd,bhkd->bhqk', q, k) * scale, axis=-1)
        attn_out = jnp.einsum('bhqk,bhkd->bhqd', attn_w, v)
        attn_out = attn_out.transpose(0, 2, 1, 3).reshape(B, N, H)
        attn_out = attn_out @ W_proj + b_proj
        x = x + gate_a[:, None] * attn_out
        S = context.shape[1]
        q_c = _ln(x) @ W_qc + b_qc
        kv_c = _ln(context) @ W_kvc + b_kvc
        k_c, v_c = jnp.split(kv_c, 2, axis=-1)
        q_c = q_c.reshape(B, N, NH, hd).transpose(0, 2, 1, 3)
        k_c = k_c.reshape(B, S, NH, hd).transpose(0, 2, 1, 3)
        v_c = v_c.reshape(B, S, NH, hd).transpose(0, 2, 1, 3)
        c_attn_w = jax.nn.softmax(jnp.einsum('bhqd,bhsd->bhqs', q_c, k_c) * scale, axis=-1)
        c_attn_out = jnp.einsum('bhqs,bhsd->bhqd', c_attn_w, v_c)
        c_attn_out = c_attn_out.transpose(0, 2, 1, 3).reshape(B, N, H)
        c_attn_out = c_attn_out @ W_cproj + b_cproj
        x = x + c_attn_out
        x_norm2 = modulate(_ln(x), shift_m, scale_m)
        h = jax.nn.gelu(x_norm2 @ W_mlp1 + b_mlp1)
        h = h @ W_mlp2 + b_mlp2
        x = x + gate_m[:, None] * h
        return x

    def _L2_xcond_ref(x, t_emb, context, adaln_w, adaln_b, qkv_w, qkv_b, sa_proj_w, sa_proj_b, q_w, q_b, kv_w, kv_b, ca_proj_w, ca_proj_b, fc1_w, fc1_b, fc2_w, fc2_b):
        import jax, jax.numpy as jnp
        import numpy as np
        D = 256
        H = 16
        HD = D // H
        MLP = 4 * D
        EPS = 1e-06
        SCALE = HD ** (-0.5)

        def _p(key, shape, s=0.02):
            return jax.random.normal(key, shape, dtype=jnp.float32) * s

        def _ln(x):
            mu = jnp.mean(x, axis=-1, keepdims=True)
            var = jnp.var(x, axis=-1, keepdims=True)
            return (x - mu) * jax.lax.rsqrt(var + EPS)

        def _heads(t):
            B, L, _ = t.shape
            return t.reshape(B, L, H, HD).transpose(0, 2, 1, 3)

        def _attend(q, k, v):
            attn = jnp.einsum('bhnd,bhsd->bhns', q, k) * SCALE
            attn = jax.nn.softmax(attn, axis=-1)
            o = jnp.einsum('bhns,bhsd->bhnd', attn, v)
            B, _, N, _ = q.shape
            return o.transpose(0, 2, 1, 3).reshape(B, N, D)
        B, N, _ = x.shape
        S = context.shape[1]
        mod = jax.nn.silu(t_emb) @ adaln_w + adaln_b
        sh_sa, sc_sa, g_sa, sh_ff, sc_ff, g_ff = jnp.split(mod[:, None, :], 6, axis=-1)
        xm = _ln(x) * (1.0 + sc_sa) + sh_sa
        qkv = (xm @ qkv_w + qkv_b).reshape(B, N, 3, H, HD)
        q = qkv[:, :, 0].transpose(0, 2, 1, 3)
        k = qkv[:, :, 1].transpose(0, 2, 1, 3)
        v = qkv[:, :, 2].transpose(0, 2, 1, 3)
        x_sa = _attend(q, k, v) @ sa_proj_w + sa_proj_b
        x = x + g_sa * x_sa
        xn = _ln(x)
        q = _heads(xn @ q_w + q_b)
        kv = (context @ kv_w + kv_b).reshape(B, S, 2, H, HD)
        k = kv[:, :, 0].transpose(0, 2, 1, 3)
        v = kv[:, :, 1].transpose(0, 2, 1, 3)
        x_ca = _attend(q, k, v) @ ca_proj_w + ca_proj_b
        x = x + x_ca
        xm = _ln(x) * (1.0 + sc_ff) + sh_ff
        h = jax.nn.gelu(xm @ fc1_w + fc1_b, approximate=True)
        x_ff = h @ fc2_w + fc2_b
        x = x + g_ff * x_ff
        return x

    def _L3_xcond_ref(x, noise_emb, context, ln1_w, ln1_b, ln2_w, ln2_b, ln3_w, ln3_b, qkv_w, sa_out_w, q_w, k_w, v_w, ca_out_w, ffn_w1, ffn_b1, ffn_w2, ffn_b2):
        import jax, jax.numpy as jnp
        import numpy as np
        import math
        D_MODEL = 256
        N_HEADS = 16
        HEAD_DIM = D_MODEL // N_HEADS
        D_FF = 1024
        EPS = 1e-05
        ROPE_BASE = 10000.0

        def _rope(t):
            L, Dh = (t.shape[1], t.shape[-1])
            half = Dh // 2
            inv_freq = 1.0 / ROPE_BASE ** (jnp.arange(half, dtype=t.dtype) / half)
            ang = jnp.arange(L, dtype=t.dtype)[:, None] * inv_freq[None, :]
            cos = jnp.cos(ang)[None, :, None, :]
            sin = jnp.sin(ang)[None, :, None, :]
            t1, t2 = (t[..., :half], t[..., half:])
            return jnp.concatenate([t1 * cos - t2 * sin, t2 * cos + t1 * sin], axis=-1)

        def _adaln(x, emb, w, b):
            e = emb[:, 0, :]
            gb = e @ w.T + b
            gamma, beta = jnp.split(gb, 2, axis=-1)
            mu = x.mean(-1, keepdims=True)
            var = x.var(-1, keepdims=True)
            xn = (x - mu) * jax.lax.rsqrt(var + EPS)
            return xn * (1.0 + gamma[:, None, :]) + beta[:, None, :]

        def _attn(q, k, v):
            scale = 1.0 / math.sqrt(HEAD_DIM)
            scores = jnp.einsum('bqhd,bkhd->bhqk', q, k) * scale
            w = jax.nn.softmax(scores, axis=-1)
            out = jnp.einsum('bhqk,bkhd->bqhd', w, v)
            B, Lq = (out.shape[0], out.shape[1])
            return out.reshape(B, Lq, D_MODEL)
        B, L, D = x.shape
        L_ctx = context.shape[1]
        res = x
        xn = _adaln(x, noise_emb, ln1_w, ln1_b)
        qkv = xn @ qkv_w.T
        q, k, v = jnp.split(qkv, 3, axis=-1)
        q = _rope(q.reshape(B, L, N_HEADS, HEAD_DIM))
        k = _rope(k.reshape(B, L, N_HEADS, HEAD_DIM))
        v = v.reshape(B, L, N_HEADS, HEAD_DIM)
        sa = _attn(q, k, v) @ sa_out_w.T
        x = res + sa
        res = x
        xn = _adaln(x, noise_emb, ln2_w, ln2_b)
        q = _rope((xn @ q_w.T).reshape(B, L, N_HEADS, HEAD_DIM))
        k = _rope((context @ k_w.T).reshape(B, L_ctx, N_HEADS, HEAD_DIM))
        v = (context @ v_w.T).reshape(B, L_ctx, N_HEADS, HEAD_DIM)
        ca = _attn(q, k, v) @ ca_out_w.T
        x = res + ca
        res = x
        xn = _adaln(x, noise_emb, ln3_w, ln3_b)
        h = jax.nn.gelu(xn @ ffn_w1.T + ffn_b1, approximate=False)
        x = res + (h @ ffn_w2.T + ffn_b2)
        return x
    x = _L0_xcond_ref(x, cond_1024, ctx_1024, L0_xcond_w_ada, L0_xcond_b_ada, L0_xcond_w_qkv, L0_xcond_b_qkv, L0_xcond_w_so, L0_xcond_b_so, L0_xcond_w_q, L0_xcond_b_q, L0_xcond_w_kv, L0_xcond_b_kv, L0_xcond_w_co, L0_xcond_b_co, L0_xcond_w_m1, L0_xcond_b_m1, L0_xcond_w_m2, L0_xcond_b_m2)
    x = _L1_xcond_ref(x, cond_1024, ctx_1024, L1_xcond_W_mod, L1_xcond_b_mod, L1_xcond_W_qkv, L1_xcond_b_qkv, L1_xcond_W_proj, L1_xcond_b_proj, L1_xcond_W_qc, L1_xcond_b_qc, L1_xcond_W_kvc, L1_xcond_b_kvc, L1_xcond_W_cproj, L1_xcond_b_cproj, L1_xcond_W_mlp1, L1_xcond_b_mlp1, L1_xcond_W_mlp2, L1_xcond_b_mlp2)
    x = _L2_xcond_ref(x, cond_1024, ctx_1024, L2_xcond_adaln_w, L2_xcond_adaln_b, L2_xcond_qkv_w, L2_xcond_qkv_b, L2_xcond_sa_proj_w, L2_xcond_sa_proj_b, L2_xcond_q_w, L2_xcond_q_b, L2_xcond_kv_w, L2_xcond_kv_b, L2_xcond_ca_proj_w, L2_xcond_ca_proj_b, L2_xcond_fc1_w, L2_xcond_fc1_b, L2_xcond_fc2_w, L2_xcond_fc2_b)
    x = _L3_xcond_ref(x, cond_1024[:, None, :], ctx_1024, L3_xcond_ln1_w, L3_xcond_ln1_b, L3_xcond_ln2_w, L3_xcond_ln2_b, L3_xcond_ln3_w, L3_xcond_ln3_b, L3_xcond_qkv_w, L3_xcond_sa_out_w, L3_xcond_q_w, L3_xcond_k_w, L3_xcond_v_w, L3_xcond_ca_out_w, L3_xcond_ffn_w1, L3_xcond_ffn_b1, L3_xcond_ffn_w2, L3_xcond_ffn_b2)
    return x

_drawn_inputs = setup_inputs


def setup_inputs(seed=0):
    import zlib

    import numpy as np

    out = dict(_drawn_inputs(seed))
    spreads = {'L0_xcond_b_ada': (0.0, 0.388),
     'L0_xcond_b_qkv': (0.0, 0.8),
     'L0_xcond_b_so': (0.0, 0.362),
     'L0_xcond_b_q': (0.0, 0.8),
     'L0_xcond_b_kv': (0.0, 0.8),
     'L0_xcond_b_co': (0.0, 0.401),
     'L0_xcond_b_m1': (0.0, 0.8),
     'L0_xcond_b_m2': (0.0, 1.889),
     'L1_xcond_b_mod': (0.0, 0.551),
     'L1_xcond_b_qkv': (0.0, 0.8),
     'L1_xcond_b_proj': (0.0, 0.8),
     'L1_xcond_b_qc': (0.0, 2.0),
     'L1_xcond_b_kvc': (0.0, 0.8),
     'L1_xcond_b_cproj': (0.0, 0.8),
     'L1_xcond_b_mlp1': (0.0, 0.8),
     'L1_xcond_b_mlp2': (0.0, 0.8)}
    factors = {'L0_xcond_w_qkv': 8.0,
     'L0_xcond_w_so': 5.795,
     'L0_xcond_w_q': 7.219,
     'L0_xcond_w_kv': 3.878,
     'L0_xcond_w_co': 3.517,
     'L0_xcond_w_m1': 7.035,
     'L0_xcond_w_m2': 7.007,
     'L2_xcond_adaln_w': 2.907,
     'L2_xcond_adaln_b': 8.0,
     'L2_xcond_qkv_w': 6.045,
     'L2_xcond_qkv_b': 8.0,
     'L2_xcond_sa_proj_w': 5.942,
     'L2_xcond_sa_proj_b': 56.981,
     'L2_xcond_q_w': 64.0,
     'L2_xcond_q_b': 64.0,
     'L2_xcond_kv_b': 64.0,
     'L2_xcond_ca_proj_b': 31.632,
     'L2_xcond_fc1_w': 3.49,
     'L2_xcond_fc1_b': 37.514,
     'L2_xcond_fc2_w': 3.409,
     'L2_xcond_fc2_b': 58.015,
     'L3_xcond_ln1_b': 64.0,
     'L3_xcond_ln2_w': 51.986,
     'L3_xcond_ln2_b': 64.0,
     'L3_xcond_ln3_b': 64.0,
     'L3_xcond_q_w': 51.108,
     'L3_xcond_k_w': 50.261,
     'L3_xcond_ffn_b1': 64.0,
     'L3_xcond_ffn_b2': 100.792,
     'L1_xcond_W_qc': 3.402,
     'L2_xcond_kv_w': 8.0,
     'L2_xcond_ca_proj_w': 8.0,
     'L3_xcond_ln1_w': 8.0,
     'L3_xcond_ln3_w': 8.0,
     'L3_xcond_qkv_w': 8.0,
     'L3_xcond_sa_out_w': 8.0,
     'L3_xcond_v_w': 5.576,
     'L3_xcond_ca_out_w': 5.619,
     'L3_xcond_ffn_w1': 5.297,
     'L3_xcond_ffn_w2': 4.688}
    for name, (base, spread) in spreads.items():
        noise = np.random.default_rng([zlib.crc32(name.encode()), seed]).standard_normal(out[name].shape)
        drawn = base * np.exp(spread * noise) if base else spread * noise
        out[name] = jnp.asarray(drawn.astype(out[name].dtype))
    for name, factor in factors.items():
        out[name] = (out[name] * factor).astype(out[name].dtype)
    return out
```

```python
import concourse.bass as bass
from concourse import mybir
from contextlib import ExitStack

F32 = mybir.dt.float32
ALU = mybir.AluOpType
ACT = mybir.ActivationFunctionType
AX = mybir.AxisListType

P = 128
B = 16
T = 128
C = 256
KC = C // P
H = 16
D = C // H
G = 4
HG = H // G
DA = D + 1
GW = HG * DA
HID = 1024
FC = HID // P
TOPK = 16
LAYERS = 4
PAIRS = B // 2
QUADS = B // 4
START = 32
NEG = -3.0e38

W_Q, W_K, W_V, W_SO, W_XQ, W_XK, W_XV, W_XO = range(0, 8 * C, C)
WA = 8 * C

MOD0 = (0, 9, 15, 21)
NMOD = 27
LAYER = (
    dict(eps=1e-6, self_mod=(0, 1), self_gate=2, cross_mod=(3, 4), cross_gate=5, mlp_mod=(6, 7), mlp_gate=8,
         ctx_norm=False, topk=True, rope=False, swiglu=True, act=ACT.Silu, bias=True),
    dict(eps=1e-6, self_mod=(0, 1), self_gate=2, cross_mod=None, cross_gate=None, mlp_mod=(3, 4), mlp_gate=5,
         ctx_norm=True, topk=False, rope=False, swiglu=False, act=ACT.Gelu_apprx_tanh, bias=True),
    dict(eps=1e-6, self_mod=(0, 1), self_gate=2, cross_mod=None, cross_gate=None, mlp_mod=(3, 4), mlp_gate=5,
         ctx_norm=False, topk=False, rope=False, swiglu=False, act=ACT.Gelu_apprx_tanh, bias=True),
    dict(eps=1e-5, self_mod=(1, 0), self_gate=None, cross_mod=(3, 2), cross_gate=None, mlp_mod=(5, 4), mlp_gate=None,
         ctx_norm=False, topk=False, rope=True, swiglu=False, act=ACT.Gelu, bias=False),
)
EPS_COL = (0, 0, 0, 1)

BROW = (0, 28, 48, 68)
NBROW = 76
B_Q, B_K, B_V, B_XQ, B_XK, B_XV, B_F = 0, 2, 4, 6, 8, 10, 12

SELF, CROSS = 0, 1


def chunk_steps(a):
    steps = []
    n = 2 * G
    for t in range(n + 3):
        if t < n:
            steps.append(("scores", a, t))
        if 0 <= t - 2 < n:
            steps.append(("turn", a, t - 2))
        if 0 <= t - 3:
            steps.append(("values", a, t - 3))
        if t == G + 3:
            steps.append(("out_turn", a, 0))
        if t == G + 4:
            steps.append(("out_back", a, 0))
        if t == G + 5:
            steps.append(("out_proj", a, 0))
    return steps


STEPS = (
    [("x_turn", SELF, 0), ("k", SELF, 0), ("v", SELF, 0), ("q", SELF, 0)]
    + chunk_steps(SELF)
    + [("out_turn", SELF, 1), ("ctx_turn", CROSS, 0), ("out_back", SELF, 1), ("k", CROSS, 0),
       ("out_proj", SELF, 1), ("v", CROSS, 0), ("x_turn", CROSS, 0), ("q", CROSS, 0)]
    + chunk_steps(CROSS)
    + [("out_turn", CROSS, 1), ("out_back", CROSS, 1), ("out_proj", CROSS, 1)]
)

TAKER = dict(x_turn="act", ctx_turn="act", k="act", q="act", out_back="act", v="dve", out_turn="dve", out_proj="res")
USES = [s for s in STEPS if s[0] in TAKER]
WORK_BANKS = 3
assert len(USES) % WORK_BANKS == 0
N_USE = len(USES)
N_TAKE = {e: sum(TAKER[s[0]] == e for s in USES) for e in ("act", "dve", "res")}


def use_of(step):
    return USES.index(step)


def take_of(step):
    e = TAKER[step[0]]
    return [s for s in USES if TAKER[s[0]] == e].index(step)


def done(k):
    return k + (START + 1)


def freed(k, n):
    return k + (START + 1 - n)


def build(nc, dram, out):
    ctx = ExitStack()
    with ctx:
        def sb(name, shape, dt=F32):
            return ctx.enter_context(nc.sbuf_tensor(name, shape, dt))

        def sem(name):
            return ctx.enter_context(nc.semaphore(name))

        mods_dram = nc.dram_tensor("mods_dram", [B, NMOD * C], F32).ap()
        wa3_dram = nc.dram_tensor("wa3_dram", [C, WA], F32).ap()
        w13_dram = nc.dram_tensor("w13_dram", [C, HID], F32).ap()
        w23_dram = nc.dram_tensor("w23_dram", [HID, C], F32).ap()
        xa_dram = [nc.dram_tensor(f"xa{l}_dram", [B, T, C], F32).ap() for l in range(LAYERS)]
        xm_dram = [nc.dram_tensor(f"xm{l}_dram", [B, T, C], F32).ap() for l in range(LAYERS - 1)] + [out]
        x_src = [dram["x"]] + xm_dram[:-1]

        const = sb("const", [P, 3 * P + 2])
        ident = const[:, 0:P]
        rope_cos = const[:, P:2 * P]
        rope_sin = const[:, 2 * P:3 * P]
        eps = const[:, 3 * P:3 * P + 2]
        neghalf = sb("neghalf", [P, 4])
        wa = sb("wa", [P, KC, WA])
        wm = sb("wm", [P, 3 * 2048])
        bo = sb("bo", [P, 2, C])
        bm = sb("bm", [P, C])
        modT = sb("modT", [P, 2 * NMOD, B])
        brows = sb("brows", [NBROW, P])
        biasT = sb("biasT", [P, NBROW])
        cond = sb("cond", [B, 2, C])
        condT = sb("condT", [P, 2, KC, B])
        mrow = sb("mrow", [B, 2, 512])
        mbias = sb("mbias", [B, 9 * C])
        turned = sb("turned", [P, 2, 512])
        stats = sb("stats", [P, 4, 6])
        mv = sb("mv", [P, 4, 2])
        vare = sb("vare", [P, 4])
        rstd = sb("rstd", [P, 4])
        xin = sb("xin", [P, 2, C])
        x1 = sb("x1", [P, 2, C])
        x2 = sb("x2", [P, 2, C])
        cin = sb("cin", [P, 2, C])
        xn = sb("xn", [P, 2, C])
        cn = sb("cn", [P, 2, C])
        gate = sb("gate", [P, 2, 2, C])
        cur = sb("cur", [P, 2, 2, KC, 2])
        hT = sb("hT", [P, KC, 2, T])
        cT = sb("cT", [P, KC, 2, T])
        qT = sb("qT", [P, KC, 2, T])
        kT = sb("kT", [P, KC, 2, T])
        raw = sb("raw", [P, KC, 2, T])
        swapped = sb("swapped", [P, KC, 2, T])
        kblk = sb("kblk", [P, KC, 2, 8, T])
        vaug = sb("vaug", [P, 2, G, HG * (GW + DA)])
        mx = sb("mx", [P, 2, HG])
        prob = sb("prob", [P, 2, HG, T])
        probT = sb("probT", [P, 2, HG, T])
        left = sb("left", [P, HG, T])
        top = sb("top", [P, 2, HG, 8])
        negm = sb("negm", [P, HG])
        outT = sb("outT", [GW, G, T])
        rsum = sb("rsum", [P, H])
        on = sb("on", [P, H, D])
        oT = sb("oT", [P, KC, T])
        res = sb("res", [P, 2, C])
        mx_in = sb("mx_in", [P, 4, C])
        mres = sb("mres", [P, 4, C])
        mout = sb("mout", [P, 4, C])
        mxn = sb("mxn", [P, 4, C])
        mgate = sb("mgate", [P, 4, C])
        mcur = sb("mcur", [P, 2, KC, 4])
        fT = sb("fT", [P, KC, 4, T])
        act_a = sb("act_a", [P, 2, 512])
        hid = sb("hid", [P, FC, 512])

        kflat = kblk[:, :, :, :, :].rearrange("p a b c d -> p (a b c d)")
        ada0 = sb("ada0", [P, KC, 9 * C])
        ada = [ada0[:, :, :], kflat[:, 0:12 * C].rearrange("p (c n) -> p c n", c=KC)]
        raw_attn = hid[:, :, :].rearrange("p a b -> p (a b)").rearrange("p (r n) -> p r n", n=C)
        vflat = vaug[:, :, :, :].rearrange("p a b c -> p (a b c)")
        raw_w1 = ada0[:, :, :].rearrange("p c n -> p (c n)")[:, 0:8 * C].rearrange("p (r n) -> p r n", n=C)
        raw_w2 = vflat[:, 0:2 * HID].rearrange("p (r n) -> p r n", n=HID)
        raw_ln = wm[:, 0:12 * C].rearrange("p (r n) -> p r n", n=C)
        lnT = wm[:, 12 * C:24 * C].rearrange("p (c n) -> p c n", c=KC)

        bank = [ctx.enter_context(nc.psum_tensor(f"bank{i}", [P, 512], F32)) for i in range(8)]
        SC, PT, OB, WB = 0, 2, 4, 5

        s_const = sem("s_const")
        s_cond = sem("s_cond")
        s_brow = sem("s_brow")
        s_ada = [sem(f"s_ada{l}") for l in range(3)]
        s_rawln = sem("s_rawln")
        s_rawattn = sem("s_rawattn")
        s_raww1 = sem("s_raww1")
        s_raww2 = sem("s_raww2")
        s_mbias = sem("s_mbias")
        s_modst = [sem(f"s_modst{i}") for i in range(2)]
        s_w3st = [sem(f"s_w3st{i}") for i in range(2)]
        s_wa = sem("s_wa")
        s_wm = sem("s_wm")
        s_x = sem("s_x")
        s_ctx = sem("s_ctx")
        s_gate = [sem("s_gate_self"), sem("s_gate_cross")]
        s_spread = sem("s_spread")
        s_xast = sem("s_xast")
        s_mx = sem("s_mx")
        s_mres = sem("s_mres")
        s_mgate = sem("s_mgate")
        s_mst = sem("s_mst")
        s_zero = sem("s_zero")
        s_half = sem("s_half")
        s_silu = sem("s_silu")
        s_condT = sem("s_condT")
        s_condTs = sem("s_condTs")
        s_bT = sem("s_bT")
        s_bTs = sem("s_bTs")
        s_grp = sem("s_grp")
        s_grpout = sem("s_grpout")
        s_mchunk = sem("s_mchunk")
        s_mchout = sem("s_mchout")
        s_mturn = sem("s_mturn")
        s_mturned = sem("s_mturned")
        s_cur = sem("s_cur")
        s_var = sem("s_var")
        s_rstd = sem("s_rstd")
        s_vare = sem("s_vare")
        s_xn = sem("s_xn")
        s_cn = sem("s_cn")
        s_work = sem("s_work")
        s_tact = sem("s_tact")
        s_tdve = sem("s_tdve")
        s_rope = sem("s_rope")
        s_score = sem("s_score")
        s_shift = sem("s_shift")
        s_exp = sem("s_exp")
        s_negm = sem("s_negm")
        s_texp = sem("s_texp")
        s_turn = sem("s_turn")
        s_probT = sem("s_probT")
        s_val = sem("s_val")
        s_out = sem("s_out")
        s_res = sem("s_res")
        s_mxn = sem("s_mxn")
        s_mcur = sem("s_mcur")
        s_mT = sem("s_mT")
        s_mh = sem("s_mh")
        s_up = sem("s_up")
        s_upact = sem("s_upact")
        s_upmul = sem("s_upmul")
        s_down = sem("s_down")
        s_mo = sem("s_mo")
        s_link = sem("s_link")
        s_apart = sem("s_apart")

        STARTED = {
            "act": [s_tact, s_exp, s_texp, s_probT, s_out, s_mh, s_upact],
            "dve": [s_cur, s_var, s_xn, s_cn, s_tdve, s_rope, s_shift, s_negm, s_res, s_mxn, s_mcur, s_upmul, s_mo],
            "pe": [s_work, s_score, s_turn, s_val, s_mT, s_up, s_down],
            "pool": [s_rstd],
        }

        def ups(l):
            return 2 * FC if LAYER[l]["swiglu"] else FC

        def up0(l):
            return sum(ups(i) for i in range(l)) * QUADS

        def exps0(l):
            return 0 if l == 0 else PAIRS * 2 * G + (l - 1) * PAIRS * 4 * G

        def exp_of(l, it, a, i):
            per = 2 * G if LAYER[l]["topk"] else 4 * G
            return it * per + (exps0(l) + (2 * G * a) + i)

        def chunk_of(l, it, a, i):
            return it * (4 * G) + (l * PAIRS * 4 * G + 2 * G * a + i)

        def pair_of(l, it):
            return it + l * PAIRS

        def quad_of(l, it):
            return it + l * QUADS

        def vars_of(l, it, a):
            per = 3 if LAYER[l]["ctx_norm"] else 2
            before = sum((3 if LAYER[i]["ctx_norm"] else 2) * PAIRS + QUADS for i in range(l))
            order = {SELF: 0, "ctx": 1, CROSS: per - 1}[a]
            return it * per + (before + order)

        def vars_mlp(l, it):
            before = sum((3 if LAYER[i]["ctx_norm"] else 2) * PAIRS + QUADS for i in range(l))
            return it + (before + (3 if LAYER[l]["ctx_norm"] else 2) * PAIRS)

        def groups():
            out_rows = []
            for c in range(KC):
                for n in range(3):
                    out_rows.append(("ln", c, n))
            for c in range(KC):
                for n in range(4):
                    out_rows.append(("attn", c, n))
            for c in range(KC):
                for n in range(2):
                    out_rows.append(("w1", c, n))
            for f in range(0, FC, 2):
                out_rows.append(("w2", f, 0))
            return out_rows

        GROUPS = groups()
        MCHUNKS = ([(0, 512 * n, 512) for n in range(4)] + [(0, 2048, 256)] + [(1, 512 * n, 512) for n in range(3)]
                   + [(2, 512 * n, 512) for n in range(3)] + [(3, 512 * n, 512) for n in range(3)])

        w_of = [
            dict(qkv="L0_xcond_w_qkv", so="L0_xcond_w_so", q="L0_xcond_w_q", kv="L0_xcond_w_kv", co="L0_xcond_w_co",
                 w1="L0_xcond_w_m1", w2="L0_xcond_w_m2", bo="L0_xcond_b_so", bco="L0_xcond_b_co", b2="L0_xcond_b_m2"),
            dict(qkv="L1_xcond_W_qkv", so="L1_xcond_W_proj", q="L1_xcond_W_qc", kv="L1_xcond_W_kvc", co="L1_xcond_W_cproj",
                 w1="L1_xcond_W_mlp1", w2="L1_xcond_W_mlp2", bo="L1_xcond_b_proj", bco="L1_xcond_b_cproj",
                 b2="L1_xcond_b_mlp2"),
            dict(qkv="L2_xcond_qkv_w", so="L2_xcond_sa_proj_w", q="L2_xcond_q_w", kv="L2_xcond_kv_w", co="L2_xcond_ca_proj_w",
                 w1="L2_xcond_fc1_w", w2="L2_xcond_fc2_w", bo="L2_xcond_sa_proj_b", bco="L2_xcond_ca_proj_b",
                 b2="L2_xcond_fc2_b"),
        ]
        WA_N = [7, 7, 7, 1]
        WM_N = [3, 3, 3, 3]

        def rows(ap):
            return ap.rearrange("(c p) n -> p c n", p=P)

        block = ctx.enter_context(nc.Block())

        @block.sync
        def _(sp):
            def load_attn_weights(l):
                if l == 3:
                    sp.dma_start(wa[:, :, :], rows(wa3_dram)).then_inc(s_wa, 16)
                    return
                w = w_of[l]
                for name, at, n in (("qkv", W_Q, 3 * C), ("so", W_SO, C), ("q", W_XQ, C), ("kv", W_XK, 2 * C),
                                    ("co", W_XO, C)):
                    sp.dma_start(wa[:, :, at:at + n], rows(dram[w[name]])).then_inc(s_wa, 16)
                for a, name in enumerate(("bo", "bco")):
                    sp.dma_start(bo[:, a, :], dram[w[name]].partition_broadcast(P)).then_inc(s_wa, 16)

            def load_mlp_weights(l):
                n = HID * 2 if LAYER[l]["swiglu"] else HID
                w1 = w13_dram if l == 3 else dram[w_of[l]["w1"]]
                w2 = w23_dram if l == 3 else dram[w_of[l]["w2"]]
                b2 = dram["L3_xcond_ffn_b2"] if l == 3 else dram[w_of[l]["b2"]]
                sp.dma_start(wm[:, 0:KC * n].rearrange("p (c n) -> p c n", c=KC), rows(w1)).then_inc(s_wm, 16)
                sp.dma_start(wm[:, 4096:6144].rearrange("p (c n) -> p c n", c=FC), rows(w2)).then_inc(s_wm, 16)
                sp.dma_start(bm[:, :], b2.partition_broadcast(P)).then_inc(s_wm, 16)

            sp.sem_inc(s_xast, 16)
            sp.sem_inc(s_mst, 16)

            sp.dma_start(const[:, :], dram["tables"]).then_inc(s_const, 16)
            sp.dma_start(cond[:, 0, :], dram["cond_1024"]).then_inc(s_cond, 16)
            sp.dma_start(ada[0][:, :, 0:9 * C], rows(dram["L0_xcond_w_ada"])).then_inc(s_ada[0], 16)
            sp.dma_start(mbias[:, 0:9 * C], dram["L0_xcond_b_ada"].partition_broadcast(B)).then_inc(s_mbias, 16)
            sp.dma_start(raw_ln[:, 0:4, :], dram["L3_xcond_ln1_w"].rearrange("(r p) n -> p r n", p=P)).then_inc(s_rawln, 16)
            sp.dma_start(raw_ln[:, 4:8, :], dram["L3_xcond_ln2_w"].rearrange("(r p) n -> p r n", p=P)).then_inc(s_rawln, 16)
            sp.dma_start(raw_ln[:, 8:12, :], dram["L3_xcond_ln3_w"].rearrange("(r p) n -> p r n", p=P)).then_inc(s_rawln, 16)
            r = 0
            for name in ("L0_xcond_b_qkv", "L0_xcond_b_q", "L0_xcond_b_kv", "L0_xcond_b_m1",
                         "L1_xcond_b_qkv", "L1_xcond_b_qc", "L1_xcond_b_kvc", "L1_xcond_b_mlp1",
                         "L2_xcond_qkv_b", "L2_xcond_q_b", "L2_xcond_kv_b", "L2_xcond_fc1_b", "L3_xcond_ffn_b1"):
                n = dram[name].shape[0] // P
                sp.dma_start(brows[r:r + n, :], dram[name].rearrange("(r p) -> r p", p=P)).then_inc(s_brow, 16)
                r += n
            sp.dma_start(ada[1], rows(dram["L1_xcond_W_mod"])).then_inc(s_ada[1], 16)
            r = 0
            for name in ("qkv_w", "sa_out_w", "q_w", "k_w", "v_w", "ca_out_w"):
                src = dram["L3_xcond_" + name]
                n = src.shape[0] // P
                sp.dma_start(raw_attn[:, r:r + n, :], src.rearrange("(r p) n -> p r n", p=P)).then_inc(s_rawattn, 16)
                r += n
            sp.dma_start(raw_w2, dram["L3_xcond_ffn_w2"].rearrange("(r p) n -> p r n", p=P)).then_inc(s_raww2, 16)
            load_attn_weights(0)

            stored_w = [0, 0]
            for n, (l, at, w) in enumerate(MCHUNKS):
                sp.wait_ge(s_mchout, n + 1)
                sp.dma_start(mods_dram[:, MOD0[l] * C + at:MOD0[l] * C + at + w], mrow[:, n % 2, 0:w]).then_inc(s_modst[n % 2], 16)
                last = n + 1 < len(MCHUNKS) and MCHUNKS[n + 1][0] != l
                if last and l == 0:
                    sp.dma_start(ada[0][:, :, 0:6 * C], rows(dram["L2_xcond_adaln_w"])).then_inc(s_ada[2], 16)
                    sp.dma_start(mbias[:, 0:6 * C], dram["L1_xcond_b_mod"].partition_broadcast(B)).then_inc(s_mbias, 16)
                if last and l == 1:
                    sp.dma_start(mbias[:, 0:6 * C], dram["L2_xcond_adaln_b"].partition_broadcast(B)).then_inc(s_mbias, 16)
                if last and l == 2:
                    sp.dma_start(raw_w1, dram["L3_xcond_ffn_w1"].rearrange("(r p) n -> p r n", p=P)).then_inc(s_raww1, 16)
                    for i in range(3):
                        sp.dma_start(mbias[:, 2 * C * i:2 * C * (i + 1)],
                                     dram[f"L3_xcond_ln{i + 1}_b"].partition_broadcast(B)).then_inc(s_mbias, 16)
            for n, (kind, c, j) in enumerate(GROUPS):
                if kind == "ln":
                    continue
                sp.wait_ge(s_grpout, n + 1)
                src = turned[:, n % 2, :]
                if kind == "attn":
                    dst = wa3_dram[c * P:(c + 1) * P, 512 * j:512 * (j + 1)]
                elif kind == "w1":
                    dst = w13_dram[c * P:(c + 1) * P, 512 * j:512 * (j + 1)]
                else:
                    dst = w23_dram[c * P:(c + 2) * P, :].rearrange("(f p) n -> p f n", p=P)
                    src = src.rearrange("p (f n) -> p f n", f=2)
                sp.dma_start(dst, src).then_inc(s_w3st[n % 2], 16)
                stored_w[n % 2] += 1
            for i in range(2):
                sp.wait_ge(s_modst[i], 16 * (len(MCHUNKS) // 2))
                sp.wait_ge(s_w3st[i], 16 * stored_w[i])

            def pair(x):
                return x.rearrange("b t n -> t b n")

            def load_pair(l, it):
                g = pair_of(l, it)
                sp.wait_ge(s_res, freed(g * 4 + 1, 4))
                b = it * 2
                sp.dma_start(xin[:, :, :], pair(x_src[l][bass.ds(b, 2), :, :])).then_inc(s_x, 16)
                if LAYER[l]["self_gate"] is not None:
                    at = (MOD0[l] + LAYER[l]["self_gate"]) * C
                    sp.dma_start(gate[:, 0, :, :], mods_dram[bass.ds(b, 2), at:at + C].partition_broadcast(P)).then_inc(s_gate[SELF], 16)
                sp.wait_ge(s_work, freed(g * N_USE + use_of(("ctx_turn", CROSS, 0)), N_USE))
                sp.dma_start(cin[:, :, :], pair(dram["ctx_1024"][bass.ds(b, 2), :, :])).then_inc(s_ctx, 16)

            def attention_step(l, it, last):
                g = pair_of(l, it)
                for a in (SELF, CROSS):
                    if LAYER[l]["cross_gate"] is not None and a == CROSS:
                        sp.wait_ge(s_res, freed(g * 4 + 3, 4))
                        at = (MOD0[l] + LAYER[l]["cross_gate"]) * C
                        sp.dma_start(gate[:, 1, :, :], mods_dram[bass.ds(it * 2, 2), at:at + C].partition_broadcast(P))\
                            .then_inc(s_gate[CROSS], 16)
                    if LAYER[l]["rope"]:
                        sp.wait_ge(s_rope, done((it * 4) + 2 * a))
                    else:
                        sp.wait_ge(s_tact, done(g * N_TAKE["act"] + take_of(("k", a, 0))))
                    for h in range(P // D):
                        sp.dma_start(kblk[D * h:D * (h + 1), :, :, h, :].rearrange("p c s t -> p (c s) t"),
                                     kT[D * h:D * (h + 1), :, :, :].rearrange("p c s t -> p (c s) t")).then_inc(s_spread, 16)
                if not last:
                    load_pair(l, it + 1)
                sp.wait_ge(s_res, done(g * 4 + 3))
                sp.dma_start(pair(xa_dram[l][bass.ds(it * 2, 2), :, :]), x2[:, :, :]).then_inc(s_xast, 16)

            def load_quad_x(l, it):
                sp.wait_ge(s_mxn, freed(quad_of(l, it), 1))
                sp.dma_start(mx_in[:, :, :], pair(xa_dram[l][bass.ds(it * 4, 4), :, :])).then_inc(s_mx, 16)

            def load_quad_res(l, it):
                sp.wait_ge(s_mo, freed(quad_of(l, it) * 4 + 3, 4))
                sp.dma_start(mres[:, :, :], pair(xa_dram[l][bass.ds(it * 4, 4), :, :])).then_inc(s_mres, 16)
                if LAYER[l]["mlp_gate"] is not None:
                    at = (MOD0[l] + LAYER[l]["mlp_gate"]) * C
                    sp.dma_start(mgate[:, :, :], mods_dram[bass.ds(it * 4, 4), at:at + C].partition_broadcast(P))\
                        .then_inc(s_mgate, 16)

            def mlp_step(l, it, last):
                load_quad_res(l, it)
                if not last:
                    load_quad_x(l, it + 1)
                sp.wait_ge(s_mo, done(quad_of(l, it) * 4 + 3))
                sp.dma_start(pair(xm_dram[l][bass.ds(it * 4, 4), :, :]), mout[:, :, :]).then_inc(s_mst, 16)

            for l in range(LAYERS):
                if l > 0:
                    sp.wait_ge(s_mst, 16 * (QUADS * l + 1))
                load_pair(l, 0)
                if l > 0:
                    sp.wait_ge(s_down, done(4 * QUADS * l - 1))
                else:
                    sp.wait_ge(s_mchunk, len(MCHUNKS))
                load_mlp_weights(l)
                with sp.Fori(0, PAIRS - 1) as it:
                    attention_step(l, it, False)
                attention_step(l, PAIRS - 1, True)
                sp.wait_ge(s_xast, 16 * (PAIRS * (l + 1) + 1))
                load_quad_x(l, 0)
                if l + 1 < LAYERS:
                    load_attn_weights(l + 1)
                with sp.Fori(0, QUADS - 1) as it:
                    mlp_step(l, it, False)
                mlp_step(l, QUADS - 1, True)
            sp.wait_ge(s_mst, 16 * (QUADS * LAYERS + 1))

        @block.gpsimd
        def _(pool):
            for s in STARTED["pool"]:
                pool.sem_inc(s, START)
            nc.gpsimd.memset(neghalf[:, :], -0.5).then_inc(s_half, 1)
            pool.wait_ge(s_half, 1)
            pool.wait_ge(s_const, 16)

            def one(k, n, l):
                pool.wait_ge(s_var, done(k))
                e = eps[:, EPS_COL[l]:EPS_COL[l] + 1].to_broadcast([P, n])
                nc.gpsimd.tensor_tensor(vare[:, 0:n], mv[:, 0:n, 1], e, ALU.add).then_inc(s_vare, 1)
                pool.wait_ge(s_vare, k + 1)
                nc.gpsimd.tensor_tensor(rstd[:, 0:n], vare[:, 0:n], neghalf[:, 0:n], ALU.pow).then_inc(s_rstd, 1)

            for l in range(LAYERS):
                per = 3 if LAYER[l]["ctx_norm"] else 2
                first = vars_of(l, 0, SELF)
                with pool.Fori(0, PAIRS * per) as it:
                    one(it + first, 2, l)
                first = vars_mlp(l, 0)
                with pool.Fori(0, QUADS) as it:
                    one(it + first, 4, l)

        @block.scalar
        def _(act):
            for s in STARTED["act"]:
                act.sem_inc(s, START)
            act.wait_ge(s_cond, 16)
            nc.scalar.activation(cond[:, 1, :], cond[:, 0, :], ACT.Silu).then_inc(s_silu, 1)
            act.wait_ge(s_condT, 1)
            nc.scalar.activation(condT[:, :, :, :].rearrange("p a c b -> p (a c b)"), bank[0][:, 0:4 * B], ACT.Copy)\
                .then_inc(s_condTs, 1)
            blk = 0
            for n, (l, at, w) in enumerate(MCHUNKS):
                act.wait_ge(s_mturn, n + 1)
                k = w // P
                nc.scalar.activation(modT[:, blk:blk + k, :].rearrange("p k b -> p (k b)"),
                                     bank[4 + n % 2][:, 0:k * B], ACT.Copy).then_inc(s_mturned, 1)
                blk += k

            def take(l, it, step):
                act.wait_ge(s_work, done(pair_of(l, it) * N_USE + use_of(step)))
                return bank[WB + use_of(step) % WORK_BANKS]

            def attention_step(l, it):
                cfg = LAYER[l]
                g = pair_of(l, it)
                for step in STEPS:
                    kind, a, i = step
                    if kind == "x_turn":
                        src = take(l, it, step)
                        mod = cfg["self_mod"] if a == SELF else cfg["cross_mod"]
                        if mod is None:
                            nc.scalar.activation(hT[:, :, :, :].rearrange("p c s t -> p (c s t)"), src[:, :], ACT.Copy)\
                                .then_inc(s_tact, 1)
                        else:
                            if a == SELF:
                                act.wait_ge(s_cur, done(g))
                            for c in range(KC):
                                for s in range(2):
                                    ins = nc.scalar.activation(
                                        hT[:, c, s, :], src[:, (2 * c + s) * T:(2 * c + s + 1) * T], ACT.Identity,
                                        bias=cur[:, a, 0, c, s:s + 1], scale=cur[:, a, 1, c, s:s + 1])
                            ins.then_inc(s_tact, 1)
                    elif kind == "ctx_turn":
                        src = take(l, it, step)
                        nc.scalar.activation(cT[:, :, :, :].rearrange("p c s t -> p (c s t)"), src[:, :], ACT.Copy)\
                            .then_inc(s_tact, 1)
                    elif kind in "qk":
                        src = take(l, it, step)
                        if cfg["rope"]:
                            act.wait_ge(s_rope, freed(it * 4 + (2 * a + (kind == "q")), 1))
                            nc.scalar.activation(raw[:, :, :, :].rearrange("p c s t -> p (c s t)"), src[:, :], ACT.Copy)\
                                .then_inc(s_tact, 1)
                            continue
                        dst = qT if kind == "q" else kT
                        b0 = BROW[l] + {("q", SELF): B_Q, ("k", SELF): B_K, ("q", CROSS): B_XQ, ("k", CROSS): B_XK}[kind, a]
                        for c in range(KC):
                            ins = nc.scalar.activation(
                                dst[:, c, :, :].rearrange("p s t -> p (s t)"), src[:, c * 2 * T:(c + 1) * 2 * T],
                                ACT.Identity, bias=biasT[:, b0 + c:b0 + c + 1])
                        ins.then_inc(s_tact, 1)
                    elif kind == "scores":
                        k = chunk_of(l, it, a, i)
                        if cfg["topk"] and a == CROSS:
                            t = it * (2 * G) + i
                            act.wait_ge(s_negm, done(t))
                            act.wait_ge(s_turn, freed(k, 2))
                            for j in range(HG):
                                ins = nc.scalar.activation(prob[:, i % 2, j, :], bank[SC + i % 2][:, j * T:(j + 1) * T],
                                                           ACT.Exp, bias=negm[:, j:j + 1], scale=D ** -0.5)
                            ins.then_inc(s_texp, 1)
                        else:
                            act.wait_ge(s_shift, done(k))
                            p = prob[:, i % 2, :, :].rearrange("p h t -> p (h t)")
                            nc.scalar.activation(p, p, ACT.Exp, scale=D ** -0.5).then_inc(s_exp, 1)
                    elif kind == "turn":
                        k = chunk_of(l, it, a, i)
                        act.wait_ge(s_turn, done(k))
                        act.wait_ge(s_val, freed(k, 2))
                        nc.scalar.activation(probT[:, i % 2, :, :].rearrange("p h t -> p (h t)"), bank[PT + i % 2][:, :],
                                             ACT.Copy).then_inc(s_probT, 1)
                    elif kind == "values" and i % G == G - 1:
                        k = chunk_of(l, it, a, i)
                        act.wait_ge(s_val, done(k))
                        nc.scalar.activation(outT[:, :, :].rearrange("p g t -> p (g t)"), bank[OB][0:GW, :], ACT.Copy)\
                            .then_inc(s_out, 1)
                    elif kind == "out_back":
                        src = take(l, it, step)
                        if cfg["bias"]:
                            b0 = BROW[l] + (B_V if a == SELF else B_XV)
                            for c in range(KC):
                                ins = nc.scalar.activation(oT[:, c, :], src[:, c * T:(c + 1) * T], ACT.Identity,
                                                           bias=biasT[:, b0 + c:b0 + c + 1])
                        else:
                            ins = nc.scalar.activation(oT[:, :, :].rearrange("p c t -> p (c t)"), src[:, 0:KC * T], ACT.Copy)
                        ins.then_inc(s_tact, 1)

            def modulate(l, it):
                m = quad_of(l, it)
                act.wait_ge(s_mcur, done(m))
                for c in range(KC):
                    act.wait_ge(s_mT, done(m * KC + c))
                    for s in range(4):
                        ins = nc.scalar.activation(fT[:, c, s, :], bank[6 + c][:, s * T:(s + 1) * T], ACT.Identity,
                                                   bias=mcur[:, 0, c, s:s + 1], scale=mcur[:, 1, c, s:s + 1])
                ins.then_inc(s_mh, 1)

            def mlp_step(l, it, last):
                cfg = LAYER[l]
                b0 = BROW[l] + (B_F if l < 3 else 0)
                for f in range(FC):
                    if cfg["swiglu"]:
                        act.wait_ge(s_up, done(it * ups(l) + (up0(l) + 2 * f)))
                        act.wait_ge(s_upmul, freed(it * FC + f, 2))
                        nc.scalar.activation(act_a[:, f % 2, :], bank[2 * (f % 2)][:, :], cfg["act"],
                                             bias=biasT[:, b0 + f:b0 + f + 1]).then_inc(s_upact, 1)
                    else:
                        act.wait_ge(s_up, done(it * ups(l) + (up0(l) + f)))
                        nc.scalar.activation(hid[:, f, :], bank[f % 4][:, :], cfg["act"],
                                             bias=biasT[:, b0 + f:b0 + f + 1]).then_inc(s_upact, 1)
                if not last:
                    modulate(l, it + 1)

            act.wait_ge(s_bTs, 1)
            for l in range(LAYERS):
                with act.Fori(0, PAIRS) as it:
                    attention_step(l, it)
                modulate(l, 0)
                with act.Fori(0, QUADS - 1) as it:
                    mlp_step(l, it, False)
                mlp_step(l, QUADS - 1, True)

        @block.vector
        def _(dve):
            for s in STARTED["dve"]:
                dve.sem_inc(s, START)
            chain = dict(base=0, per=0, n=0, it=0)

            def link(ins):
                chain["n"] += 1
                ins.then_inc(s_link, 1)
                dve.wait_ge(s_link, chain["it"] * chain["per"] + (chain["base"] + chain["n"]))

            def enter(it, per):
                chain.update(it=it, per=per, n=0)

            def leave(times):
                assert chain["n"] == chain["per"], chain
                chain.update(base=chain["base"] + times * chain["per"], n=0, it=0, per=0)

            dve.wait_ge(s_bT, 1)
            nc.vector.tensor_copy(biasT[:, :], bank[1][:, 0:NBROW]).then_inc(s_bTs, 1)

            def group_out(n):
                kind, c, j = GROUPS[n]
                dve.wait_ge(s_grp, n + 1)
                if kind == "ln":
                    dst = lnT[:, c, 512 * j:512 * (j + 1)]
                else:
                    if n >= 8:
                        dve.wait_ge(s_w3st[n % 2], 16 * ((n - 6) // 2))
                    dst = turned[:, n % 2, :]
                nc.vector.tensor_copy(dst, bank[6 + n % 2][:, :]).then_inc(s_grpout, 1)

            def chunk_out(n):
                l, at, w = MCHUNKS[n]
                dve.wait_ge(s_mchunk, n + 1)
                dve.wait_ge(s_mbias, 16 * (l + 1 if l < 3 else 6))
                if n >= 2:
                    dve.wait_ge(s_modst[n % 2], 16 * (n // 2))
                    dve.wait_ge(s_mturn, n - 1)
                nc.vector.tensor_tensor(mrow[:, n % 2, 0:w], bank[2 + n % 2][0:B, 0:w], mbias[:, at:at + w], ALU.add)\
                    .then_inc(s_mchout, 1)

            for n in range(6):
                group_out(n)
            for n in range(len(MCHUNKS)):
                chunk_out(n)
            for n in range(6, len(GROUPS)):
                group_out(n)
            dve.wait_ge(s_grp, len(GROUPS))
            link(nc.vector.memset(kflat[:, :], 0.0))
            link(nc.vector.memset(vflat[:, :], 0.0))
            for s in range(2):
                for g in range(G):
                    ones = vaug[:, s, g, :].rearrange("p (h x) -> p h x", h=HG)[:, :, D:D + 1]
                    ins = nc.vector.memset(ones, 1.0)
            ins.then_inc(s_zero, 1)
            dve.wait_ge(s_zero, 1)
            leave_n = chain["n"]
            chain.update(base=leave_n, n=0)
            dve.wait_ge(s_mturned, len(MCHUNKS))

            def apart():
                dve.sem_inc(s_apart, 1)

            def normalise(k, x, dst, n):
                apart()
                for s in range(n):
                    ins = nc.vector.bn_stats(stats[:, s, :], x[:, s, :])
                link(ins)
                apart()
                for s in range(n):
                    ins = nc.vector.bn_aggr(mv[:, s, :], stats[:, s, :])
                ins.then_inc(s_var, 1)
                dve.wait_ge(s_var, done(k))
                dve.wait_ge(s_rstd, done(k))
                for s in range(n):
                    ins = nc.vector.tensor_scalar(dst[:, s, :], x[:, s, :], mv[:, s, 0:1], rstd[:, s:s + 1],
                                                  ALU.subtract, ALU.mult)
                return ins

            def take(l, it, step):
                dve.wait_ge(s_work, done(pair_of(l, it) * N_USE + use_of(step)))
                return bank[WB + use_of(step) % WORK_BANKS]

            def fetch_mods(l, it, dst, mod, n):
                sh, sc = (2 * (MOD0[l] + m) for m in mod)
                nc.vector.tensor_copy(dst[:, 0, :, :], modT[:, sh:sh + 2, bass.ds(it * n, n)])
                return nc.vector.tensor_scalar(dst[:, 1, :, :], modT[:, sc:sc + 2, bass.ds(it * n, n)], 1.0, None, ALU.add)

            def residual(src, bias, g, x, dst, i):
                r = res[:, i % 2, :]
                if bias is not None:
                    link(nc.vector.tensor_tensor(r, src, bias, ALU.add))
                    src = r
                if g is not None:
                    link(nc.vector.tensor_tensor(r, src, g, ALU.mult))
                    src = r
                return nc.vector.tensor_tensor(dst, src, x, ALU.add)

            def rotate(l, it, a, kind):
                cos = rope_cos.unsqueeze(1).to_broadcast([P, 4, T])
                sin = rope_sin.unsqueeze(1).to_broadcast([P, 4, T])
                dst = (qT if kind == "q" else kT)[:, :, :, :].rearrange("p c s t -> p (c s) t")
                v = raw[:, :, :, :].rearrange("p c s t -> p (c s) t")
                w = swapped[:, :, :, :].rearrange("p c s t -> p (c s) t")
                dve.wait_ge(s_tact, done(pair_of(l, it) * N_TAKE["act"] + take_of((kind, a, 0))))
                apart()
                link(nc.vector.stream_shuffle(w, v, [(p // D) * D + (p + D // 2) % D for p in range(32)]))
                link(nc.vector.tensor_tensor(w, w, sin, ALU.mult))
                link(nc.vector.tensor_tensor(dst, v, cos, ALU.mult))
                nc.vector.tensor_tensor(dst, dst, w, ALU.add).then_inc(s_rope, 1)

            def top_k(l, it, a, i):
                t = it * (2 * G) + i
                sc = bank[SC + i % 2]
                apart()
                for j in range(HG):
                    ins = nc.vector.max(top[:, 0, j, :], sc[:, j * T:(j + 1) * T])
                link(ins)
                nc.vector.tensor_scalar(negm[:, :], top[:, 0, :, 0], -(D ** -0.5), None, ALU.mult)
                for j in range(HG):
                    ins = nc.vector.match_replace(left[:, j, :], top[:, 0, j, :], sc[:, j * T:(j + 1) * T], NEG)
                ins.then_inc(s_negm, 1)
                dve.wait_ge(s_negm, done(t))
                apart()
                for j in range(HG):
                    ins = nc.vector.max(top[:, 1, j, :], left[:, j, :])
                link(ins)
                apart()
                for j in range(HG):
                    ins = nc.vector.match_replace(left[:, j, :], top[:, 1, j, :], left[:, j, :], NEG)
                link(ins)
                dve.wait_ge(s_texp, done(t))
                p = prob[:, i % 2, :, :].rearrange("p h t -> p (h t)")
                nc.vector.scalar_tensor_tensor(p, left[:, :, :].rearrange("p h t -> p (h t)"), NEG, p,
                                               ALU.is_equal, ALU.mult).then_inc(s_shift, 1)

            def attention_step(l, it):
                cfg = LAYER[l]
                g = pair_of(l, it)
                dve.wait_ge(s_tact, freed(g * N_TAKE["act"] + take_of(("x_turn", CROSS, 0)), N_TAKE["act"]))
                ins = fetch_mods(l, it, cur[:, SELF, :, :, :], cfg["self_mod"], 2)
                if cfg["cross_mod"] is not None:
                    ins = fetch_mods(l, it, cur[:, CROSS, :, :, :], cfg["cross_mod"], 2)
                ins.then_inc(s_cur, 1)
                dve.wait_ge(s_x, (g + 1) * 16)
                dve.wait_ge(s_work, freed(g * N_USE + use_of(("x_turn", CROSS, 0)), N_USE))
                normalise(vars_of(l, it, SELF), xin, xn, 2).then_inc(s_xn, 1)
                if cfg["ctx_norm"]:
                    dve.wait_ge(s_ctx, (g + 1) * 16)
                    normalise(vars_of(l, it, "ctx"), cin, cn, 2).then_inc(s_cn, 1)
                for step in STEPS:
                    kind, a, i = step
                    if kind == "x_turn" and a == CROSS:
                        dve.wait_ge(s_res, done(g * 4 + 1))
                        normalise(vars_of(l, it, CROSS), x1, xn, 2).then_inc(s_xn, 1)
                    elif kind in "qk" and cfg["rope"]:
                        rotate(l, it, a, kind)
                    elif kind == "v":
                        src = take(l, it, step)
                        for s in range(2):
                            ins = nc.vector.tensor_copy(
                                vaug[:, s, :, :].rearrange("p g (h x) -> p g h x", h=HG)[:, :, :, 0:D],
                                src[:, s * C:(s + 1) * C].rearrange("p (g h d) -> p g h d", g=G, h=HG))
                        ins.then_inc(s_tdve, 1)
                    elif kind == "scores":
                        k = chunk_of(l, it, a, i)
                        dve.wait_ge(s_score, done(k))
                        if cfg["topk"] and a == CROSS:
                            top_k(l, it, a, i)
                            continue
                        sc = bank[SC + i % 2][:, :].rearrange("p (h t) -> p h t", h=HG)
                        link(nc.vector.tensor_reduce(mx[:, i % 2, :], sc, AX.X, ALU.max))
                        dve.wait_ge(s_turn, freed(k, 2))
                        nc.vector.tensor_tensor(prob[:, i % 2, :, :], sc, mx[:, i % 2, :].unsqueeze(2).to_broadcast([P, HG, T]),
                                                ALU.subtract).then_inc(s_shift, 1)
                    elif kind == "out_turn":
                        src = take(l, it, step)[:, 0:G * GW].rearrange("p (h x) -> p h x", x=DA)
                        link(nc.vector.reciprocal(rsum[:, :], src[:, :, D]))
                        nc.vector.tensor_tensor(on[:, :, :], src[:, :, 0:D], rsum[:, :].unsqueeze(2).to_broadcast([P, H, D]),
                                                ALU.mult).then_inc(s_tdve, 1)
                    elif kind == "out_proj":
                        src = take(l, it, step)[:, 0:C]
                        gt = cfg["self_gate"] if a == SELF else cfg["cross_gate"]
                        if gt is not None and i == 0:
                            dve.wait_ge(s_gate[a], (g + 1) * 16)
                        if a == CROSS and i == 0:
                            dve.wait_ge(s_xast, (g + 1) * 16)
                        residual(src, bo[:, a, :] if cfg["bias"] else None, gate[:, a, i, :] if gt is not None else None,
                                 (xin if a == SELF else x1)[:, i, :], (x1 if a == SELF else x2)[:, i, :], i).then_inc(s_res, 1)

            def front(l, it):
                cfg = LAYER[l]
                m = quad_of(l, it)
                dve.wait_ge(s_mh, freed(m, 1))
                fetch_mods(l, it, mcur, cfg["mlp_mod"], 4).then_inc(s_mcur, 1)
                dve.wait_ge(s_mx, (m + 1) * 16)
                dve.wait_ge(s_mT, freed(m * KC + 1, KC))
                normalise(vars_mlp(l, it), mx_in, mxn, 4).then_inc(s_mxn, 1)

            def mlp_step(l, it, last):
                cfg = LAYER[l]
                m = quad_of(l, it)
                b0 = BROW[l] + (B_F if l < 3 else 0)
                if cfg["swiglu"]:
                    for f in range(FC):
                        dve.wait_ge(s_up, done(it * ups(l) + (up0(l) + 2 * f + 1)))
                        dve.wait_ge(s_upact, done(it * FC + f))
                        nc.vector.scalar_tensor_tensor(hid[:, f, :], bank[2 * (f % 2) + 1][:, :],
                                                       biasT[:, b0 + FC + f:b0 + FC + f + 1], act_a[:, f % 2, :],
                                                       ALU.add, ALU.mult).then_inc(s_upmul, 1)
                if not last:
                    front(l, it + 1)
                dve.wait_ge(s_mres, (m + 1) * 16)
                if cfg["mlp_gate"] is not None:
                    dve.wait_ge(s_mgate, (m + 1) * 16)
                dve.wait_ge(s_wm, 48 * (l + 1))
                dve.wait_ge(s_mst, (m + 1) * 16)
                for s in range(4):
                    dve.wait_ge(s_down, done(m * 4 + s))
                    residual(bank[4 + s % 2][:, 0:C], bm[:, :], mgate[:, s, :] if cfg["mlp_gate"] is not None else None,
                             mres[:, s, :], mout[:, s, :], s).then_inc(s_mo, 1)

            LINKS = DVE_LINKS
            for l in range(LAYERS):
                dve.wait_ge(s_wa, 16 * sum(WA_N[:l + 1]))
                with dve.Fori(0, PAIRS) as it:
                    enter(it, LINKS[l][0])
                    attention_step(l, it)
                leave(PAIRS)
                front(l, 0)
                chain.update(base=chain["base"] + chain["n"], n=0)
                with dve.Fori(0, QUADS - 1) as it:
                    enter(it, LINKS[l][1])
                    mlp_step(l, it, False)
                leave(QUADS - 1)
                mlp_step(l, QUADS - 1, True)
                chain.update(base=chain["base"] + chain["n"], n=0)

        @block.tensor
        def _(pe):
            for s in STARTED["pe"]:
                pe.sem_inc(s, START)
            mm, turn = nc.tensor.matmul, nc.tensor.transpose

            pe.wait_ge(s_const, 16)
            pe.wait_ge(s_silu, 1)
            for a in range(2):
                for c in range(KC):
                    ins = turn(bank[0][:, (2 * a + c) * B:(2 * a + c + 1) * B], cond[:, a, c * P:(c + 1) * P],
                               ident[0:B, 0:B])
            ins.then_inc(s_condT, 1)
            pe.wait_ge(s_brow, 16 * 13)
            turn(bank[1][:, 0:NBROW], brows[:, :], ident[0:NBROW, 0:NBROW]).then_inc(s_bT, 1)

            def group(n):
                kind, c, j = GROUPS[n]
                if n >= 2:
                    pe.wait_ge(s_grpout, n - 1)
                dst = bank[6 + n % 2]
                if kind == "w2":
                    for f in range(2):
                        for r in range(2):
                            ins = turn(dst[:, f * C + r * P:f * C + (r + 1) * P], raw_w2[:, r, (c + f) * P:(c + f + 1) * P], ident)
                else:
                    src = {"ln": raw_ln, "attn": raw_attn, "w1": raw_w1}[kind]
                    for b in range(4):
                        ins = turn(dst[:, b * P:(b + 1) * P], src[:, 4 * j + b, c * P:(c + 1) * P], ident)
                ins.then_inc(s_grp, 1)

            pe.wait_ge(s_rawln, 48)
            for n in range(6):
                group(n)
            pe.wait_ge(s_condTs, 1)

            def mod_chunk(n):
                l, at, w = MCHUNKS[n]
                if l < 3:
                    pe.wait_ge(s_ada[l], 16)
                else:
                    pe.wait_ge(s_grpout, 6)
                if n >= 2:
                    pe.wait_ge(s_mchout, n - 1)
                src = (ada[l % 2] if l < 3 else lnT)
                for c in range(KC):
                    ins = mm(bank[2 + n % 2][0:B, 0:w], condT[:, 0 if l == 3 else 1, c, :], src[:, c, at:at + w],
                             start=c == 0, stop=c == KC - 1)
                ins.then_inc(s_mchunk, 1)

            def mod_turn(n):
                l, at, w = MCHUNKS[n]
                pe.wait_ge(s_mchout, n + 1)
                if n >= 2:
                    pe.wait_ge(s_mturned, n - 1)
                for b in range(w // P):
                    ins = turn(bank[4 + n % 2][:, b * B:(b + 1) * B], mrow[:, n % 2, b * P:(b + 1) * P], ident[0:B, 0:B])
                ins.then_inc(s_mturn, 1)

            for n in range(len(MCHUNKS)):
                mod_chunk(n)
                if n >= 1:
                    mod_turn(n - 1)
            mod_turn(len(MCHUNKS) - 1)
            pe.wait_ge(s_rawattn, 96)
            pe.wait_ge(s_raww1, 16)
            pe.wait_ge(s_raww2, 16)
            for n in range(6, len(GROUPS)):
                group(n)
            pe.wait_ge(s_bTs, 1)
            pe.wait_ge(s_grpout, len(GROUPS))
            pe.wait_ge(s_mturned, len(MCHUNKS))
            pe.wait_ge(s_zero, 1)

            def weights(at, n):
                return lambda c: wa[:, c, at:at + n]

            def attention_step(l, it):
                cfg = LAYER[l]
                g = pair_of(l, it)
                for step in STEPS:
                    kind, a, i = step
                    if kind in TAKER:
                        u = use_of(step)
                        dst = bank[WB + u % WORK_BANKS]
                        before = USES[u - WORK_BANKS]
                        who = TAKER[before[0]]
                        ago = (u < WORK_BANKS) * N_TAKE[who]
                        pe.wait_ge(dict(act=s_tact, dve=s_tdve, res=s_res)[who], freed(g * N_TAKE[who] + take_of(before), ago))
                    if kind == "x_turn":
                        pe.wait_ge(s_xn, done(g * 2 + a))
                        for c in range(KC):
                            for s in range(2):
                                ins = turn(dst[:, (2 * c + s) * T:(2 * c + s + 1) * T], xn[:, s, c * P:(c + 1) * P], ident)
                        ins.then_inc(s_work, 1)
                    elif kind == "ctx_turn":
                        if cfg["ctx_norm"]:
                            pe.wait_ge(s_cn, done(it))
                        else:
                            pe.wait_ge(s_ctx, (g + 1) * 16)
                        src = cn if cfg["ctx_norm"] else cin
                        for c in range(KC):
                            for s in range(2):
                                ins = turn(dst[:, (2 * c + s) * T:(2 * c + s + 1) * T], src[:, s, c * P:(c + 1) * P], ident)
                        ins.then_inc(s_work, 1)
                    elif kind in "qkv":
                        turned_by = ("x_turn", a, 0) if a == SELF or kind == "q" else ("ctx_turn", a, 0)
                        pe.wait_ge(s_tact, done(g * N_TAKE["act"] + take_of(turned_by)))
                        src = hT if turned_by[0] == "x_turn" else cT
                        at = {("q", 0): W_Q, ("k", 0): W_K, ("v", 0): W_V, ("q", 1): W_XQ, ("k", 1): W_XK, ("v", 1): W_XV}[kind, a]
                        for m in range(2):
                            for c in range(KC):
                                if kind == "v":
                                    ins = mm(dst[:, m * C:(m + 1) * C], src[:, c, m, :], wa[:, c, at:at + C],
                                             start=c == 0, stop=c == KC - 1)
                                else:
                                    ins = mm(dst[:, m * 2 * T:(m + 1) * 2 * T], wa[:, c, at + m * P:at + (m + 1) * P],
                                             src[:, c, :, :].rearrange("p s t -> p (s t)"), start=c == 0, stop=c == KC - 1)
                        ins.then_inc(s_work, 1)
                    elif kind == "scores":
                        k = chunk_of(l, it, a, i)
                        s, grp = divmod(i, G)
                        c, half = divmod(grp, 2)
                        if i == 0:
                            pe.wait_ge(s_spread, (g * 2 + (a + 1)) * (16 * (P // D)))
                            if cfg["rope"]:
                                pe.wait_ge(s_rope, done(it * 4 + (2 * a + 1)))
                            else:
                                pe.wait_ge(s_tact, done(g * N_TAKE["act"] + take_of(("q", a, 0))))
                        pe.wait_ge(s_shift, freed(k, 2))
                        mm(bank[SC + i % 2][:, :], qT[:, c, s, :],
                           kblk[:, c, s, HG * half:HG * (half + 1), :].rearrange("p h t -> p (h t)"),
                           start=True, stop=True).then_inc(s_score, 1)
                    elif kind == "turn":
                        k = chunk_of(l, it, a, i)
                        if cfg["topk"] and a == CROSS:
                            pe.wait_ge(s_shift, done(k))
                        else:
                            pe.wait_ge(s_exp, done(exp_of(l, it, a, i)))
                        pe.wait_ge(s_probT, freed(k, 2))
                        for j in range(HG):
                            ins = turn(bank[PT + i % 2][:, j * T:(j + 1) * T], prob[:, i % 2, j, :], ident)
                        ins.then_inc(s_turn, 1)
                    elif kind == "values":
                        k = chunk_of(l, it, a, i)
                        s, grp = divmod(i, G)
                        if i == 0:
                            pe.wait_ge(s_tdve, done(g * N_TAKE["dve"] + take_of(("v", a, 0))))
                        if grp == 0:
                            pe.wait_ge(s_out, freed(g * 4 + (2 * a + s), 1))
                        pe.wait_ge(s_probT, done(k))
                        for j in range(HG):
                            ins = mm(bank[OB][0:GW, grp * T:(grp + 1) * T], vaug[:, s, grp, j * GW:(j + 1) * GW],
                                     probT[:, i % 2, j, :], start=j == 0, stop=j == HG - 1)
                        ins.then_inc(s_val, 1)
                    elif kind == "out_turn":
                        pe.wait_ge(s_out, done(g * 4 + (2 * a + i)))
                        for grp in range(G):
                            ins = turn(dst[:, grp * GW:(grp + 1) * GW], outT[:, grp, :], ident[0:GW, 0:GW])
                        ins.then_inc(s_work, 1)
                    elif kind == "out_back":
                        pe.wait_ge(s_tdve, done(g * N_TAKE["dve"] + take_of(("out_turn", a, i))))
                        for c in range(KC):
                            ins = turn(dst[:, c * T:(c + 1) * T],
                                       on[:, :, :].rearrange("p h d -> p (h d)")[:, c * P:(c + 1) * P], ident)
                        ins.then_inc(s_work, 1)
                    elif kind == "out_proj":
                        pe.wait_ge(s_tact, done(g * N_TAKE["act"] + take_of(("out_back", a, i))))
                        at = W_SO if a == SELF else W_XO
                        for c in range(KC):
                            ins = mm(dst[:, 0:C], oT[:, c, :], wa[:, c, at:at + C], start=c == 0, stop=c == KC - 1)
                        ins.then_inc(s_work, 1)

            def quad_turn(l, it):
                m = quad_of(l, it)
                pe.wait_ge(s_mxn, done(m))
                pe.wait_ge(s_mh, freed(m, 1))
                for c in range(KC):
                    for s in range(4):
                        ins = turn(bank[6 + c][:, s * T:(s + 1) * T], mxn[:, s, c * P:(c + 1) * P], ident)
                    ins.then_inc(s_mT, 1)

            def mlp_step(l, it, last):
                cfg = LAYER[l]
                m = quad_of(l, it)
                n = ups(l)
                w1 = wm[:, 0:KC * n * P].rearrange("p (c n) -> p c n", c=KC)
                w2 = wm[:, 4096:6144].rearrange("p (c n) -> p c n", c=FC)
                pe.wait_ge(s_mh, done(m))
                for j in range(n):
                    if cfg["swiglu"]:
                        f, lin = divmod(j, 2)
                        col = (f + lin * FC) * P
                        b = 2 * (f % 2) + lin
                        if lin:
                            pe.wait_ge(s_upmul, freed(it * FC + f, 2))
                        else:
                            pe.wait_ge(s_upact, freed(it * FC + f, 2))
                    else:
                        col = j * P
                        b = j % 4
                        pe.wait_ge(s_upact, freed(it * FC + (l * QUADS * FC + j), 4))
                    for c in range(KC):
                        ins = mm(bank[b][:, :], w1[:, c, col:col + P], fT[:, c, :, :].rearrange("p s t -> p (s t)"),
                                 start=c == 0, stop=c == KC - 1)
                    ins.then_inc(s_up, 1)
                if not last:
                    quad_turn(l, it + 1)
                if cfg["swiglu"]:
                    pe.wait_ge(s_upmul, done(it * FC + (FC - 1)))
                else:
                    pe.wait_ge(s_upact, done(it * FC + (l * QUADS * FC + FC - 1)))
                for s in range(4):
                    pe.wait_ge(s_mo, freed(m * 4 + s, 2))
                    for f in range(FC):
                        ins = mm(bank[4 + s % 2][:, 0:C], hid[:, f, s * T:(s + 1) * T], w2[:, f, :],
                                 start=f == 0, stop=f == FC - 1)
                    ins.then_inc(s_down, 1)

            for l in range(LAYERS):
                pe.wait_ge(s_wa, 16 * sum(WA_N[:l + 1]))
                pe.wait_ge(s_mo, START + 4 * QUADS * l)
                with pe.Fori(0, PAIRS) as it:
                    attention_step(l, it)
                pe.wait_ge(s_out, START + 4 * PAIRS * (l + 1))
                pe.wait_ge(s_tdve, START + N_TAKE["dve"] * PAIRS * (l + 1))
                pe.wait_ge(s_res, START + N_TAKE["res"] * PAIRS * (l + 1))
                quad_turn(l, 0)
                pe.wait_ge(s_wm, 48 * (l + 1))
                with pe.Fori(0, QUADS - 1) as it:
                    mlp_step(l, it, False)
                mlp_step(l, QUADS - 1, True)


DVE_LINKS = ((46, 9), (29, 9), (28, 9), (34, 5))


_INS = (
    ["x", "cond_1024", "ctx_1024"]
    + ["L0_xcond_" + n for n in ("w_ada b_ada w_qkv b_qkv w_so b_so w_q b_q w_kv b_kv w_co b_co w_m1 b_m1 w_m2 b_m2".split())]
    + ["L1_xcond_" + n for n in ("W_mod b_mod W_qkv b_qkv W_proj b_proj W_qc b_qc W_kvc b_kvc W_cproj b_cproj W_mlp1 b_mlp1 "
                                 "W_mlp2 b_mlp2".split())]
    + ["L2_xcond_" + n for n in ("adaln_w adaln_b qkv_w qkv_b sa_proj_w sa_proj_b q_w q_b kv_w kv_b ca_proj_w ca_proj_b "
                                 "fc1_w fc1_b fc2_w fc2_b".split())]
    + ["L3_xcond_" + n for n in ("ln1_w ln1_b ln2_w ln2_b ln3_w ln3_b qkv_w sa_out_w q_w k_w v_w ca_out_w ffn_w1 ffn_b1 "
                                 "ffn_w2 ffn_b2".split())]
)


def tables():
    import numpy as np

    half = D // 2
    inv_freq = (1.0 / np.float32(10000.0) ** (np.arange(half, dtype=np.float32) / np.float32(half))).astype(np.float32)
    ang = (np.arange(T, dtype=np.float32)[:, None] * inv_freq[None, :]).astype(np.float32)
    comp = np.arange(P) % D
    cos = np.cos(ang)[:, comp % half].T
    sin = np.sin(ang)[:, comp % half].T * np.where(comp < half, -1.0, 1.0)[:, None]
    eps = np.tile(np.array([[1e-6, 1e-5]]), (P, 1))
    return np.ascontiguousarray(np.concatenate([np.eye(P), cos, sin, eps], axis=1).astype(np.float32))


def kernel(**inputs):
    import numpy as _np
    import concourse.bacc as _bacc
    from concourse import mybir as _mybir
    from concourse.bass_utils import run_bass_kernel_spmd as _run

    nc = _bacc.Bacc("TRN2", target_bir_lowering=False, num_devices=1)
    arrays, dram = {}, {}
    for name in _INS:
        a = _np.ascontiguousarray(inputs[name])
        arrays[f"in_{name}_dram"] = a
        dram[name] = nc.dram_tensor(f"in_{name}_dram", a.shape, _mybir.dt.from_np(a.dtype), kind="ExternalInput").ap()
    t = tables()
    arrays["tables_dram"] = t
    dram["tables"] = nc.dram_tensor("tables_dram", t.shape, _mybir.dt.from_np(t.dtype), kind="ExternalInput").ap()
    out = nc.dram_tensor("out_dram", (B, T, C), F32, kind="ExternalOutput").ap()
    build(nc, dram, out)
    r = _run(nc, [arrays], core_ids=[0])
    return r.results[0]["out_dram"]
```

```python
import concourse.bass as bass
from concourse import mybir
from contextlib import ExitStack

F32 = mybir.dt.float32
ALU = mybir.AluOpType
ACT = mybir.ActivationFunctionType
AX = mybir.AxisListType

P = 128
B = 16
T = 128
C = 256
KC = C // P
H = 16
D = C // H
G = 4
HG = H // G
DA = D + 1
GW = HG * DA
HID = 1024
FC = HID // P
TOPK = 16
LAYERS = 4
PAIRS = B // 2
QUADS = B // 4
START = 32
NEG = -3.0e38

W_Q, W_K, W_V, W_SO, W_XQ, W_XK, W_XV, W_XO = range(0, 8 * C, C)
WA = 8 * C

MOD0 = (0, 9, 15, 21)
NMOD = 27
LAYER = (
    dict(eps=1e-6, self_mod=(0, 1), self_gate=2, cross_mod=(3, 4), cross_gate=5, mlp_mod=(6, 7), mlp_gate=8,
         ctx_norm=False, topk=True, rope=False, swiglu=True, act=ACT.Silu, bias=True),
    dict(eps=1e-6, self_mod=(0, 1), self_gate=2, cross_mod=None, cross_gate=None, mlp_mod=(3, 4), mlp_gate=5,
         ctx_norm=True, topk=False, rope=False, swiglu=False, act=ACT.Gelu_apprx_tanh, bias=True),
    dict(eps=1e-6, self_mod=(0, 1), self_gate=2, cross_mod=None, cross_gate=None, mlp_mod=(3, 4), mlp_gate=5,
         ctx_norm=False, topk=False, rope=False, swiglu=False, act=ACT.Gelu_apprx_tanh, bias=True),
    dict(eps=1e-5, self_mod=(1, 0), self_gate=None, cross_mod=(3, 2), cross_gate=None, mlp_mod=(5, 4), mlp_gate=None,
         ctx_norm=False, topk=False, rope=True, swiglu=False, act=ACT.Gelu, bias=False),
)
EPS_COL = (0, 0, 0, 1)

BROW = (0, 28, 48, 68)
NBROW = 76
B_Q, B_K, B_V, B_XQ, B_XK, B_XV, B_F = 0, 2, 4, 6, 8, 10, 12

SELF, CROSS = 0, 1
CHUNKS = ([(SELF, g, 1) for g in range(G)] + [(CROSS, g, 0) for g in range(G)]
          + [(SELF, G + g, 1) for g in range(G)] + [(CROSS, G + g, 0) for g in range(G)])


def chunk_steps():
    steps = []
    n = len(CHUNKS)
    for t in range(n + 1):
        if t < n:
            steps.append(("scores",) + CHUNKS[t])
        if 0 <= t - 2:
            steps.append(("turn",) + CHUNKS[t - 2])
        if t == n - 1:
            steps.append(("out_turn", SELF, 1, 1))
        if 0 <= t - 3:
            steps.append(("values",) + CHUNKS[t - 3])
        if t == n - 1:
            steps.append(("out_back", SELF, 1, 1))
        if t == n:
            steps.append(("out_proj", SELF, 1, 1))
        if t == n // 2:
            steps.append(("norm_ctx", CROSS, 0, 1))
        for block in range(2):
            a, off = CHUNKS[G * block][0], CHUNKS[G * block][2]
            if t == G * block + G + 3:
                steps.append(("out_turn", a, 0, off))
            if t == G * block + G + 4:
                steps.append(("out_back", a, 0, off))
            if t == G * block + G + 5:
                steps.append(("out_proj", a, 0, off))
    return steps


STEPS = (
    [("norm", SELF, 0, 1), ("turn", CROSS, 7, -1), ("values", CROSS, 6, -1), ("ctx_turn", CROSS, 0, 0),
     ("values", CROSS, 7, -1), ("x_turn", SELF, 0, 1), ("v", CROSS, 0, 0), ("k", SELF, 0, 1), ("k", CROSS, 0, 0),
     ("out_turn", CROSS, 1, -1), ("q", SELF, 0, 1), ("out_back", CROSS, 1, -1), ("v", SELF, 0, 1),
     ("out_proj", CROSS, 1, -1), ("keep", CROSS, 0, 0), ("x_turn", CROSS, 0, 0), ("q", CROSS, 0, 0)]
    + chunk_steps()
    + [("norm", CROSS, 0, 1)]
)
OFFSET = {s[:3]: s[3] for s in STEPS}
FIRST, LAST = -1, PAIRS


def steps_of(j):
    return [s for s in STEPS if not isinstance(j, int) or 0 <= j + s[3] < PAIRS]


def number(sel, l, pair, kind, a, i):
    off = OFFSET[kind, a, i]
    picked = [s for s in STEPS if sel(l, s)]

    def before(layer, j):
        all_before = sum(0 <= jj + s[3] < PAIRS for m in range(layer) for jj in range(FIRST, LAST + 1)
                         for s in STEPS if sel(m, s))
        return all_before + sum(0 <= jj + s[3] < PAIRS for jj in range(FIRST, j) for s in picked)

    step = (kind, a, i, off)
    if isinstance(pair, int):
        j = pair - off
        return before(l, j) + [s for s in picked if 0 <= j + s[3] < PAIRS].index(step)
    return pair * len(picked) + (before(l, 1) + picked.index(step) - (off + 1) * len(picked))


TAKER = dict(x_turn="act", ctx_turn="act", k="act", q="act", out_back="act", v="dve", out_turn="dve", out_proj="res")
USES = [s for s in STEPS if s[0] in TAKER]
N_USE = len(USES)
N_ACT = sum(TAKER[s[0]] == "act" for s in USES)
WORK_BANKS = 3
assert len(USES) % WORK_BANKS == 0


def is_use(l, s):
    return s[0] in TAKER


def is_taken_by(who):
    return lambda l, s: TAKER.get(s[0]) == who


def is_chunk(l, s):
    return s[0] == "scores"


def is_plain_chunk(l, s):
    return s[0] == "scores" and not (LAYER[l]["topk"] and s[1] == CROSS)


def is_topk_chunk(l, s):
    return s[0] == "scores" and LAYER[l]["topk"] and s[1] == CROSS


def is_output(l, s):
    return s[0] == "values" and s[2] % G == G - 1


def is_rotated(l, s):
    return s[0] in ("q", "k") and LAYER[l]["rope"]


def is_copy(l, s):
    return s[0] == "keep" or s[:2] == ("norm", SELF)


def is_token_norm(l, s):
    return s[0] == "norm"


def is_norm(l, s):
    return s[0] == "norm" or (s[0] == "norm_ctx" and LAYER[l]["ctx_norm"])


def work_bank(kind, a, i):
    return [u[:3] for u in USES].index((kind, a, i)) % WORK_BANKS


def use_before(j, step):
    mine = work_bank(*step[:3])
    todo = steps_of(j)
    todo = todo[:todo.index(step)]
    for back in range(3):
        for s in reversed(todo):
            if s[0] in TAKER and work_bank(*s[:3]) == mine:
                return -back, s
        if isinstance(j, int):
            todo = steps_of(j - back - 1) if j - back - 1 >= FIRST else []
        else:
            todo = STEPS
    return None


def done(k):
    return k + (START + 1)


def freed(k, n):
    return k + (START + 1 - n)


def build(nc, dram, out):
    ctx = ExitStack()
    with ctx:
        def sb(name, shape, dt=F32):
            return ctx.enter_context(nc.sbuf_tensor(name, shape, dt))

        def sem(name):
            return ctx.enter_context(nc.semaphore(name))

        mods_dram = nc.dram_tensor("mods_dram", [B, NMOD * C], F32).ap()
        wa3_dram = nc.dram_tensor("wa3_dram", [C, WA], F32).ap()
        w13_dram = nc.dram_tensor("w13_dram", [C, HID], F32).ap()
        w23_dram = nc.dram_tensor("w23_dram", [HID, C], F32).ap()
        xa_dram = [nc.dram_tensor(f"xa{l}_dram", [B, T, C], F32).ap() for l in range(LAYERS)]
        xm_dram = [nc.dram_tensor(f"xm{l}_dram", [B, T, C], F32).ap() for l in range(LAYERS - 1)] + [out]
        x_src = [dram["x"]] + xm_dram[:-1]

        const = sb("const", [P, 3 * P + 2])
        ident = const[:, 0:P]
        rope_cos = const[:, P:2 * P]
        rope_sin = const[:, 2 * P:3 * P]
        eps = const[:, 3 * P:3 * P + 2]
        neghalf = sb("neghalf", [P, 4])
        wa = sb("wa", [P, KC, WA])
        wm = sb("wm", [P, 3 * 2048])
        bo = sb("bo", [P, 2, C])
        bm = sb("bm", [P, C])
        modT = sb("modT", [P, 2 * NMOD, B])
        brows = sb("brows", [NBROW, P])
        biasT = sb("biasT", [P, NBROW])
        cond = sb("cond", [B, 2, C])
        condT = sb("condT", [P, 2, KC, B])
        stats = sb("stats", [P, 4, 6])
        mv = sb("mv", [P, 4, 2])
        vare = sb("vare", [P, 4])
        rstd = sb("rstd", [P, 4])
        xin = sb("xin", [P, 2, C])
        xself = sb("xself", [P, 2, C])
        x1 = sb("x1", [P, 2, C])
        x1cross = sb("x1cross", [P, 2, C])
        x2 = sb("x2", [P, 2, C])
        cin = sb("cin", [P, 2, C])
        xn = sb("xn", [P, 2, 2, C])
        cn = sb("cn", [P, 2, C])
        gate = sb("gate", [P, 2, 2, C])
        cur = sb("cur", [P, 2, 2, KC, 2])
        hT = sb("hT", [P, KC, 2, T])
        cT = sb("cT", [P, KC, 2, T])
        qT = sb("qT", [P, 2, KC, 2, T])
        kT = sb("kT", [P, 2, KC, 2, T])
        raw = sb("raw", [P, KC, 2, T])
        swapped = sb("swapped", [P, KC, 2, T])
        kblk = sb("kblk", [P, 2, KC, 2, 8, T])
        vaug = sb("vaug", [P, 2, 2, G, HG * (GW + DA)])
        mx = sb("mx", [P, 2, HG])
        prob = sb("prob", [P, 2, HG, T])
        probT = sb("probT", [P, 2, HG, T])
        left = sb("left", [P, HG, T])
        top = sb("top", [P, 2, HG, 8])
        negm = sb("negm", [P, HG])
        outT = sb("outT", [GW, G, T])
        rsum = sb("rsum", [P, H])
        on = sb("on", [P, H, D])
        oT = sb("oT", [P, KC, T])
        res = sb("res", [P, 2, C])
        quad = sb("quad", [P, 5, 4, C])
        mx_in, mres, mout, mxn, mgate = (quad[:, i, :, :] for i in range(5))
        mcur = sb("mcur", [P, 2, KC, 4])
        fT = sb("fT", [P, KC, 4, T])
        act_a = sb("act_a", [P, 2, 512])
        hid = sb("hid", [P, FC, 512])

        qflat = quad[:, :, :, :].rearrange("p i s n -> p (i s n)")
        mbias = qflat[0:B, 0:9 * C]
        mrow = qflat[0:B, 9 * C:13 * C].rearrange("p (i n) -> p i n", i=2)
        turned = qflat[:, 13 * C:17 * C].rearrange("p (i n) -> p i n", i=2)
        kflat = kblk[:, :, :, :, :, :].rearrange("p e a b c d -> p (e a b c d)")
        ada = [kflat[:, 0:18 * C].rearrange("p (c n) -> p c n", c=KC),
               kflat[:, 18 * C:30 * C].rearrange("p (c n) -> p c n", c=KC)]
        raw_attn = hid[:, :, :].rearrange("p a b -> p (a b)").rearrange("p (r n) -> p r n", n=C)
        vflat = vaug[:, :, :, :, :].rearrange("p e a b c -> p (e a b c)")
        raw_w1 = kflat[:, 0:8 * C].rearrange("p (r n) -> p r n", n=C)
        raw_w2 = vflat[:, 0:2 * HID].rearrange("p (r n) -> p r n", n=HID)
        raw_ln = wm[:, 0:12 * C].rearrange("p (r n) -> p r n", n=C)
        lnT = wm[:, 12 * C:24 * C].rearrange("p (c n) -> p c n", c=KC)

        bank = [ctx.enter_context(nc.psum_tensor(f"bank{i}", [P, 512], F32)) for i in range(8)]
        SC, PT, OB, WB = 0, 2, 4, 5

        s_const = sem("s_const")
        s_cond = sem("s_cond")
        s_brow = sem("s_brow")
        s_ada = [sem(f"s_ada{l}") for l in range(3)]
        s_rawln = sem("s_rawln")
        s_rawattn = sem("s_rawattn")
        s_raww1 = sem("s_raww1")
        s_raww2 = sem("s_raww2")
        s_mbias = sem("s_mbias")
        s_modst = [sem(f"s_modst{i}") for i in range(2)]
        s_w3st = [sem(f"s_w3st{i}") for i in range(2)]
        s_wa = sem("s_wa")
        s_wm = sem("s_wm")
        s_x = sem("s_x")
        s_ctx = sem("s_ctx")
        s_gate = [sem("s_gate_self"), sem("s_gate_cross")]
        s_spread = [sem("s_spread_self"), sem("s_spread_cross")]
        s_xast = sem("s_xast")
        s_mx = sem("s_mx")
        s_mres = sem("s_mres")
        s_mgate = sem("s_mgate")
        s_mst = sem("s_mst")
        s_zero = sem("s_zero")
        s_half = sem("s_half")
        s_silu = sem("s_silu")
        s_condT = sem("s_condT")
        s_condTs = sem("s_condTs")
        s_bT = sem("s_bT")
        s_bTs = sem("s_bTs")
        s_grp = sem("s_grp")
        s_grpout = sem("s_grpout")
        s_mchunk = sem("s_mchunk")
        s_mchout = sem("s_mchout")
        s_mturn = sem("s_mturn")
        s_mturned = sem("s_mturned")
        s_cur = [sem("s_cur_self"), sem("s_cur_cross")]
        s_var = sem("s_var")
        s_rstd = sem("s_rstd")
        s_vare = sem("s_vare")
        s_xn = sem("s_xn")
        s_cn = sem("s_cn")
        s_work = sem("s_work")
        s_tact = sem("s_tact")
        s_tdve = sem("s_tdve")
        s_rope = sem("s_rope")
        s_score = sem("s_score")
        s_shift = sem("s_shift")
        s_exp = sem("s_exp")
        s_negm = sem("s_negm")
        s_texp = sem("s_texp")
        s_turn = sem("s_turn")
        s_probT = sem("s_probT")
        s_val = sem("s_val")
        s_out = sem("s_out")
        s_kept = sem("s_kept")
        s_res = sem("s_res")
        s_mxn = sem("s_mxn")
        s_mcur = sem("s_mcur")
        s_mT = sem("s_mT")
        s_mh = sem("s_mh")
        s_up = sem("s_up")
        s_upact = sem("s_upact")
        s_upmul = sem("s_upmul")
        s_down = sem("s_down")
        s_mo = sem("s_mo")
        s_link = sem("s_link")
        s_apart = sem("s_apart")
        s_apart_sp = sem("s_apart_sp")

        STARTED = {
            "act": [s_tact, s_exp, s_texp, s_probT, s_out, s_mh, s_upact],
            "dve": [*s_cur, s_var, s_xn, s_cn, s_tdve, s_rope, s_shift, s_negm, s_res, s_mxn, s_mcur, s_upmul, s_mo],
            "pe": [s_work, s_score, s_turn, s_val, s_mT, s_up, s_down],
            "pool": [s_rstd],
        }

        def ups(l):
            return 2 * FC if LAYER[l]["swiglu"] else FC

        def up0(l):
            return sum(ups(i) for i in range(l)) * QUADS

        def pair_of(l, it):
            return it + l * PAIRS

        def quad_of(l, it):
            return it + l * QUADS

        def kept(l, j, a):
            return number(is_copy, l, j, *(("norm", SELF, 0) if a == SELF else ("keep", CROSS, 0))) + 1

        def norms(l):
            return PAIRS * sum(is_norm(l, s) for s in STEPS)

        def vars_of(l, pair, kind, a):
            return number(is_norm, l, pair, kind, a, 0) + l * QUADS

        def vars_mlp(l, it):
            return it + (sum(norms(i) for i in range(l + 1)) + l * QUADS)

        def groups():
            out_rows = []
            for c in range(KC):
                for n in range(3):
                    out_rows.append(("ln", c, n))
            for c in range(KC):
                for n in range(4):
                    out_rows.append(("attn", c, n))
            for c in range(KC):
                for n in range(2):
                    out_rows.append(("w1", c, n))
            for f in range(0, FC, 2):
                out_rows.append(("w2", f, 0))
            return out_rows

        GROUPS = groups()
        MCHUNKS = ([(0, 512 * n, 512) for n in range(4)] + [(0, 2048, 256)] + [(1, 512 * n, 512) for n in range(3)]
                   + [(2, 512 * n, 512) for n in range(3)] + [(3, 512 * n, 512) for n in range(3)])

        w_of = [
            dict(qkv="L0_xcond_w_qkv", so="L0_xcond_w_so", q="L0_xcond_w_q", kv="L0_xcond_w_kv", co="L0_xcond_w_co",
                 w1="L0_xcond_w_m1", w2="L0_xcond_w_m2", bo="L0_xcond_b_so", bco="L0_xcond_b_co", b2="L0_xcond_b_m2"),
            dict(qkv="L1_xcond_W_qkv", so="L1_xcond_W_proj", q="L1_xcond_W_qc", kv="L1_xcond_W_kvc", co="L1_xcond_W_cproj",
                 w1="L1_xcond_W_mlp1", w2="L1_xcond_W_mlp2", bo="L1_xcond_b_proj", bco="L1_xcond_b_cproj",
                 b2="L1_xcond_b_mlp2"),
            dict(qkv="L2_xcond_qkv_w", so="L2_xcond_sa_proj_w", q="L2_xcond_q_w", kv="L2_xcond_kv_w", co="L2_xcond_ca_proj_w",
                 w1="L2_xcond_fc1_w", w2="L2_xcond_fc2_w", bo="L2_xcond_sa_proj_b", bco="L2_xcond_ca_proj_b",
                 b2="L2_xcond_fc2_b"),
        ]
        WA_N = [7, 7, 7, 1]
        WM_N = [3, 3, 3, 3]

        def rows(ap):
            return ap.rearrange("(c p) n -> p c n", p=P)

        block = ctx.enter_context(nc.Block())

        @block.sync
        def _(sp):
            def load_attn_weights(l):
                if l == 3:
                    sp.dma_start(wa[:, :, :], rows(wa3_dram)).then_inc(s_wa, 16)
                    return
                w = w_of[l]
                for name, at, n in (("qkv", W_Q, 3 * C), ("so", W_SO, C), ("q", W_XQ, C), ("kv", W_XK, 2 * C),
                                    ("co", W_XO, C)):
                    sp.dma_start(wa[:, :, at:at + n], rows(dram[w[name]])).then_inc(s_wa, 16)
                for a, name in enumerate(("bo", "bco")):
                    sp.dma_start(bo[:, a, :], dram[w[name]].partition_broadcast(P)).then_inc(s_wa, 16)

            def load_mlp_weights(l):
                n = HID * 2 if LAYER[l]["swiglu"] else HID
                w1 = w13_dram if l == 3 else dram[w_of[l]["w1"]]
                w2 = w23_dram if l == 3 else dram[w_of[l]["w2"]]
                b2 = dram["L3_xcond_ffn_b2"] if l == 3 else dram[w_of[l]["b2"]]
                sp.dma_start(wm[:, 0:KC * n].rearrange("p (c n) -> p c n", c=KC), rows(w1)).then_inc(s_wm, 16)
                sp.dma_start(wm[:, 4096:6144].rearrange("p (c n) -> p c n", c=FC), rows(w2)).then_inc(s_wm, 16)
                sp.dma_start(bm[:, :], b2.partition_broadcast(P)).then_inc(s_wm, 16)

            sp.sem_inc(s_xast, 16)
            sp.sem_inc(s_mst, 16)

            sp.dma_start(const[:, :], dram["tables"]).then_inc(s_const, 16)
            sp.dma_start(cond[:, 0, :], dram["cond_1024"]).then_inc(s_cond, 16)
            sp.dma_start(ada[0][:, :, 0:9 * C], rows(dram["L0_xcond_w_ada"])).then_inc(s_ada[0], 16)
            sp.dma_start(mbias[:, 0:9 * C], dram["L0_xcond_b_ada"].partition_broadcast(B)).then_inc(s_mbias, 16)
            sp.dma_start(raw_ln[:, 0:4, :], dram["L3_xcond_ln1_w"].rearrange("(r p) n -> p r n", p=P)).then_inc(s_rawln, 16)
            sp.dma_start(raw_ln[:, 4:8, :], dram["L3_xcond_ln2_w"].rearrange("(r p) n -> p r n", p=P)).then_inc(s_rawln, 16)
            sp.dma_start(raw_ln[:, 8:12, :], dram["L3_xcond_ln3_w"].rearrange("(r p) n -> p r n", p=P)).then_inc(s_rawln, 16)
            r = 0
            for name in ("L0_xcond_b_qkv", "L0_xcond_b_q", "L0_xcond_b_kv", "L0_xcond_b_m1",
                         "L1_xcond_b_qkv", "L1_xcond_b_qc", "L1_xcond_b_kvc", "L1_xcond_b_mlp1",
                         "L2_xcond_qkv_b", "L2_xcond_q_b", "L2_xcond_kv_b", "L2_xcond_fc1_b", "L3_xcond_ffn_b1"):
                n = dram[name].shape[0] // P
                sp.dma_start(brows[r:r + n, :], dram[name].rearrange("(r p) -> r p", p=P)).then_inc(s_brow, 16)
                r += n
            sp.dma_start(ada[1], rows(dram["L1_xcond_W_mod"])).then_inc(s_ada[1], 16)
            r = 0
            for name in ("qkv_w", "sa_out_w", "q_w", "k_w", "v_w", "ca_out_w"):
                src = dram["L3_xcond_" + name]
                n = src.shape[0] // P
                sp.dma_start(raw_attn[:, r:r + n, :], src.rearrange("(r p) n -> p r n", p=P)).then_inc(s_rawattn, 16)
                r += n
            sp.dma_start(raw_w2, dram["L3_xcond_ffn_w2"].rearrange("(r p) n -> p r n", p=P)).then_inc(s_raww2, 16)
            load_attn_weights(0)

            stored_w = [0, 0]
            for n, (l, at, w) in enumerate(MCHUNKS):
                sp.wait_ge(s_mchout, n + 1)
                sp.dma_start(mods_dram[:, MOD0[l] * C + at:MOD0[l] * C + at + w], mrow[:, n % 2, 0:w]).then_inc(s_modst[n % 2], 16)
                last = n + 1 < len(MCHUNKS) and MCHUNKS[n + 1][0] != l
                if last and l == 0:
                    sp.dma_start(ada[0][:, :, 0:6 * C], rows(dram["L2_xcond_adaln_w"])).then_inc(s_ada[2], 16)
                    sp.dma_start(mbias[:, 0:6 * C], dram["L1_xcond_b_mod"].partition_broadcast(B)).then_inc(s_mbias, 16)
                if last and l == 1:
                    sp.dma_start(mbias[:, 0:6 * C], dram["L2_xcond_adaln_b"].partition_broadcast(B)).then_inc(s_mbias, 16)
                if last and l == 2:
                    sp.dma_start(raw_w1, dram["L3_xcond_ffn_w1"].rearrange("(r p) n -> p r n", p=P)).then_inc(s_raww1, 16)
                    for i in range(3):
                        sp.dma_start(mbias[:, 2 * C * i:2 * C * (i + 1)],
                                     dram[f"L3_xcond_ln{i + 1}_b"].partition_broadcast(B)).then_inc(s_mbias, 16)
            for n, (kind, c, j) in enumerate(GROUPS):
                if kind == "ln":
                    continue
                sp.wait_ge(s_grpout, n + 1)
                src = turned[:, n % 2, :]
                if kind == "attn":
                    dst = wa3_dram[c * P:(c + 1) * P, 512 * j:512 * (j + 1)]
                elif kind == "w1":
                    dst = w13_dram[c * P:(c + 1) * P, 512 * j:512 * (j + 1)]
                else:
                    dst = w23_dram[c * P:(c + 2) * P, :].rearrange("(f p) n -> p f n", p=P)
                    src = src.rearrange("p (f n) -> p f n", f=2)
                sp.dma_start(dst, src).then_inc(s_w3st[n % 2], 16)
                stored_w[n % 2] += 1
            for i in range(2):
                sp.wait_ge(s_modst[i], 16 * (len(MCHUNKS) // 2))
                sp.wait_ge(s_w3st[i], 16 * stored_w[i])

            def pair(x):
                return x.rearrange("b t n -> t b n")

            def apart():
                sp.sem_inc(s_apart_sp, 1)

            def load_x(l, j):
                if not isinstance(j, int) or j > 0:
                    sp.wait_ge(s_kept, kept(l, j - 1, SELF))
                elif l > 0:
                    sp.wait_ge(s_kept, kept(l - 1, PAIRS - 1, SELF))
                apart()
                sp.dma_start(xin[:, :, :], pair(x_src[l][bass.ds(j * 2, 2), :, :])).then_inc(s_x, 16)

            def load_ctx(l, j):
                sp.wait_ge(s_work, freed(number(is_use, l, j, "ctx_turn", CROSS, 0), N_USE))
                if LAYER[l]["ctx_norm"]:
                    apart()
                    sp.wait_ge(s_cn, freed(j, 1))
                apart()
                sp.dma_start(cin[:, :, :], pair(dram["ctx_1024"][bass.ds(j * 2, 2), :, :])).then_inc(s_ctx, 16)

            def load_gate(l, j, a):
                mod = LAYER[l]["self_gate" if a == SELF else "cross_gate"]
                if mod is None:
                    return
                sp.wait_ge(s_res, done(number(is_taken_by("res"), l, j - 1, "out_proj", a, 1)) if not isinstance(j, int) or j > 0
                           else START + 4 * PAIRS * l)
                apart()
                at = (MOD0[l] + mod) * C
                sp.dma_start(gate[:, a, :, :], mods_dram[bass.ds(j * 2, 2), at:at + C].partition_broadcast(P))\
                    .then_inc(s_gate[a], 16)

            def spread(l, j, a):
                if LAYER[l]["rope"]:
                    sp.wait_ge(s_rope, done(number(is_rotated, l, j, "k", a, 0)))
                else:
                    sp.wait_ge(s_tact, done(number(is_taken_by("act"), l, j, "k", a, 0)))
                for h in range(P // D):
                    sp.dma_start(kblk[D * h:D * (h + 1), a, :, :, h, :].rearrange("p c s t -> p (c s) t"),
                                 kT[D * h:D * (h + 1), a, :, :, :].rearrange("p c s t -> p (c s) t")).then_inc(s_spread[a], 16)

            def attention_step(l, j):
                def has(off):
                    return not isinstance(j, int) or 0 <= j + off < PAIRS
                if has(1):
                    spread(l, j + 1, SELF)
                if has(0):
                    spread(l, j, CROSS)
                if has(2):
                    load_x(l, j + 2)
                if has(1):
                    load_ctx(l, j + 1)
                if has(-1):
                    sp.wait_ge(s_res, done(number(is_taken_by("res"), l, j - 1, "out_proj", CROSS, 1)))
                    apart()
                    sp.dma_start(pair(xa_dram[l][bass.ds((j - 1) * 2, 2), :, :]), x2[:, :, :]).then_inc(s_xast, 16)
                if has(0):
                    load_gate(l, j, CROSS)
                if has(2):
                    load_gate(l, j + 2, SELF)

            def load_quad_x(l, it):
                sp.wait_ge(s_mxn, freed(quad_of(l, it), 1))
                sp.dma_start(mx_in[:, :, :], pair(xa_dram[l][bass.ds(it * 4, 4), :, :])).then_inc(s_mx, 16)

            def load_quad_res(l, it):
                sp.wait_ge(s_mo, freed(quad_of(l, it) * 4 + 3, 4))
                sp.dma_start(mres[:, :, :], pair(xa_dram[l][bass.ds(it * 4, 4), :, :])).then_inc(s_mres, 16)
                if LAYER[l]["mlp_gate"] is not None:
                    at = (MOD0[l] + LAYER[l]["mlp_gate"]) * C
                    sp.dma_start(mgate[:, :, :], mods_dram[bass.ds(it * 4, 4), at:at + C].partition_broadcast(P))\
                        .then_inc(s_mgate, 16)

            def mlp_step(l, it, last):
                load_quad_res(l, it)
                if not last:
                    load_quad_x(l, it + 1)
                sp.wait_ge(s_mo, done(quad_of(l, it) * 4 + 3))
                sp.dma_start(pair(xm_dram[l][bass.ds(it * 4, 4), :, :]), mout[:, :, :]).then_inc(s_mst, 16)

            for l in range(LAYERS):
                if l > 0:
                    sp.wait_ge(s_mst, 16 * (QUADS * l + 1))
                load_x(l, 0)
                load_gate(l, 0, SELF)
                if l > 0:
                    sp.wait_ge(s_down, done(4 * QUADS * l - 1))
                else:
                    sp.wait_ge(s_mchunk, len(MCHUNKS))
                load_mlp_weights(l)
                for j in (-1, 0):
                    attention_step(l, j)
                with sp.Fori(1, PAIRS - 2) as j:
                    attention_step(l, j)
                for j in (PAIRS - 2, PAIRS - 1, PAIRS):
                    attention_step(l, j)
                sp.wait_ge(s_xast, 16 * (PAIRS * (l + 1) + 1))
                load_quad_x(l, 0)
                if l + 1 < LAYERS:
                    load_attn_weights(l + 1)
                with sp.Fori(0, QUADS - 1) as it:
                    mlp_step(l, it, False)
                mlp_step(l, QUADS - 1, True)
            sp.wait_ge(s_mst, 16 * (QUADS * LAYERS + 1))

        @block.gpsimd
        def _(pool):
            for s in STARTED["pool"]:
                pool.sem_inc(s, START)
            nc.gpsimd.memset(neghalf[:, :], -0.5).then_inc(s_half, 1)
            pool.wait_ge(s_half, 1)
            pool.wait_ge(s_const, 16)

            def one(k, n, l):
                pool.wait_ge(s_var, done(k))
                e = eps[:, EPS_COL[l]:EPS_COL[l] + 1].to_broadcast([P, n])
                nc.gpsimd.tensor_tensor(vare[:, 0:n], mv[:, 0:n, 1], e, ALU.add).then_inc(s_vare, 1)
                pool.wait_ge(s_vare, k + 1)
                nc.gpsimd.tensor_tensor(rstd[:, 0:n], vare[:, 0:n], neghalf[:, 0:n], ALU.pow).then_inc(s_rstd, 1)

            for l in range(LAYERS):
                first = vars_mlp(l, 0) - norms(l)
                with pool.Fori(0, norms(l)) as it:
                    one(it + first, 2, l)
                first = vars_mlp(l, 0)
                with pool.Fori(0, QUADS) as it:
                    one(it + first, 4, l)

        @block.scalar
        def _(act):
            for s in STARTED["act"]:
                act.sem_inc(s, START)
            act.wait_ge(s_cond, 16)
            nc.scalar.activation(cond[:, 1, :], cond[:, 0, :], ACT.Silu).then_inc(s_silu, 1)
            act.wait_ge(s_condT, 1)
            nc.scalar.activation(condT[:, :, :, :].rearrange("p a c b -> p (a c b)"), bank[0][:, 0:4 * B], ACT.Copy)\
                .then_inc(s_condTs, 1)
            blk = 0
            for n, (l, at, w) in enumerate(MCHUNKS):
                act.wait_ge(s_mturn, n + 1)
                k = w // P
                nc.scalar.activation(modT[:, blk:blk + k, :].rearrange("p k b -> p (k b)"),
                                     bank[4 + n % 2][:, 0:k * B], ACT.Copy).then_inc(s_mturned, 1)
                blk += k

            def take(l, j, kind, a, i):
                act.wait_ge(s_work, done(number(is_use, l, j, kind, a, i)))
                return bank[WB + work_bank(kind, a, i)]

            def attention_step(l, it):
                cfg = LAYER[l]
                for kind, a, i, off in steps_of(it):
                    j = it + off
                    if kind == "x_turn":
                        src = take(l, j, kind, a, i)
                        mod = cfg["self_mod"] if a == SELF else cfg["cross_mod"]
                        if mod is None:
                            nc.scalar.activation(hT[:, :, :, :].rearrange("p c s t -> p (c s t)"), src[:, :], ACT.Copy)\
                                .then_inc(s_tact, 1)
                        else:
                            layers_before = sum(LAYER[m]["self_mod" if a == SELF else "cross_mod"] is not None for m in range(l))
                            act.wait_ge(s_cur[a], done(j + PAIRS * layers_before))
                            for c in range(KC):
                                for s in range(2):
                                    ins = nc.scalar.activation(
                                        hT[:, c, s, :], src[:, (2 * c + s) * T:(2 * c + s + 1) * T], ACT.Identity,
                                        bias=cur[:, a, 0, c, s:s + 1], scale=cur[:, a, 1, c, s:s + 1])
                            ins.then_inc(s_tact, 1)
                    elif kind == "ctx_turn":
                        src = take(l, j, kind, a, i)
                        nc.scalar.activation(cT[:, :, :, :].rearrange("p c s t -> p (c s t)"), src[:, :], ACT.Copy)\
                            .then_inc(s_tact, 1)
                    elif kind in ("q", "k"):
                        src = take(l, j, kind, a, i)
                        if cfg["rope"]:
                            act.wait_ge(s_rope, freed(number(is_rotated, l, j, kind, a, i), 1))
                            nc.scalar.activation(raw[:, :, :, :].rearrange("p c s t -> p (c s t)"), src[:, :], ACT.Copy)\
                                .then_inc(s_tact, 1)
                            continue
                        dst = qT if kind == "q" else kT
                        b0 = BROW[l] + {("q", SELF): B_Q, ("k", SELF): B_K, ("q", CROSS): B_XQ, ("k", CROSS): B_XK}[kind, a]
                        for c in range(KC):
                            ins = nc.scalar.activation(
                                dst[:, a, c, :, :].rearrange("p s t -> p (s t)"), src[:, c * 2 * T:(c + 1) * 2 * T],
                                ACT.Identity, bias=biasT[:, b0 + c:b0 + c + 1])
                        ins.then_inc(s_tact, 1)
                    elif kind == "scores":
                        k = number(is_chunk, l, j, kind, a, i)
                        if cfg["topk"] and a == CROSS:
                            t = number(is_topk_chunk, l, j, kind, a, i)
                            act.wait_ge(s_negm, done(t))
                            act.wait_ge(s_turn, freed(k, 2))
                            for h in range(HG):
                                ins = nc.scalar.activation(prob[:, i % 2, h, :], bank[SC + i % 2][:, h * T:(h + 1) * T],
                                                           ACT.Exp, bias=negm[:, h:h + 1], scale=D ** -0.5)
                            ins.then_inc(s_texp, 1)
                        else:
                            act.wait_ge(s_shift, done(k))
                            p = prob[:, i % 2, :, :].rearrange("p h t -> p (h t)")
                            nc.scalar.activation(p, p, ACT.Exp, scale=D ** -0.5).then_inc(s_exp, 1)
                    elif kind == "turn":
                        k = number(is_chunk, l, j, "scores", a, i)
                        act.wait_ge(s_turn, done(k))
                        act.wait_ge(s_val, freed(k, 2))
                        nc.scalar.activation(probT[:, i % 2, :, :].rearrange("p h t -> p (h t)"), bank[PT + i % 2][:, :],
                                             ACT.Copy).then_inc(s_probT, 1)
                    elif kind == "values" and i % G == G - 1:
                        k = number(is_chunk, l, j, "scores", a, i)
                        act.wait_ge(s_val, done(k))
                        nc.scalar.activation(outT[:, :, :].rearrange("p g t -> p (g t)"), bank[OB][0:GW, :], ACT.Copy)\
                            .then_inc(s_out, 1)
                    elif kind == "out_back":
                        src = take(l, j, kind, a, i)
                        if cfg["bias"]:
                            b0 = BROW[l] + (B_V if a == SELF else B_XV)
                            for c in range(KC):
                                ins = nc.scalar.activation(oT[:, c, :], src[:, c * T:(c + 1) * T], ACT.Identity,
                                                           bias=biasT[:, b0 + c:b0 + c + 1])
                        else:
                            ins = nc.scalar.activation(oT[:, :, :].rearrange("p c t -> p (c t)"), src[:, 0:KC * T], ACT.Copy)
                        ins.then_inc(s_tact, 1)

            def modulate(l, it):
                m = quad_of(l, it)
                act.wait_ge(s_mcur, done(m))
                for c in range(KC):
                    act.wait_ge(s_mT, done(m * KC + c))
                    for s in range(4):
                        ins = nc.scalar.activation(fT[:, c, s, :], bank[6 + c][:, s * T:(s + 1) * T], ACT.Identity,
                                                   bias=mcur[:, 0, c, s:s + 1], scale=mcur[:, 1, c, s:s + 1])
                ins.then_inc(s_mh, 1)

            def mlp_step(l, it, last):
                cfg = LAYER[l]
                b0 = BROW[l] + (B_F if l < 3 else 0)
                for f in range(FC):
                    if cfg["swiglu"]:
                        act.wait_ge(s_up, done(it * ups(l) + (up0(l) + 2 * f)))
                        act.wait_ge(s_upmul, freed(it * FC + f, 2))
                        nc.scalar.activation(act_a[:, f % 2, :], bank[2 * (f % 2)][:, :], cfg["act"],
                                             bias=biasT[:, b0 + f:b0 + f + 1]).then_inc(s_upact, 1)
                    else:
                        act.wait_ge(s_up, done(it * ups(l) + (up0(l) + f)))
                        nc.scalar.activation(hid[:, f, :], bank[f % 4][:, :], cfg["act"],
                                             bias=biasT[:, b0 + f:b0 + f + 1]).then_inc(s_upact, 1)
                if not last:
                    modulate(l, it + 1)

            act.wait_ge(s_bTs, 1)
            for l in range(LAYERS):
                nc.scalar.preload_act_table(ACT.Exp)
                for j in (-1, 0):
                    attention_step(l, j)
                with act.Fori(1, PAIRS - 1) as j:
                    attention_step(l, j)
                for j in (PAIRS - 1, PAIRS):
                    attention_step(l, j)
                modulate(l, 0)
                nc.scalar.preload_act_table(LAYER[l]["act"])
                with act.Fori(0, QUADS - 1) as it:
                    mlp_step(l, it, False)
                mlp_step(l, QUADS - 1, True)

        @block.vector
        def _(dve):
            for s in STARTED["dve"]:
                dve.sem_inc(s, START)
            chain = dict(base=0, per=0, n=0, it=0)

            def link(ins):
                chain["n"] += 1
                ins.then_inc(s_link, 1)
                dve.wait_ge(s_link, chain["it"] * chain["per"] + (chain["base"] + chain["n"]))

            def enter(it, per):
                chain.update(it=it, per=per, n=0)

            def settle():
                chain.update(base=chain["base"] + chain["n"], n=0)

            def leave(times):
                assert chain["n"] == chain["per"], chain
                chain.update(base=chain["base"] + times * chain["per"], n=0, it=0, per=0)

            dve.wait_ge(s_bT, 1)
            nc.vector.tensor_copy(biasT[:, :], bank[1][:, 0:NBROW]).then_inc(s_bTs, 1)

            def group_out(n):
                kind, c, j = GROUPS[n]
                dve.wait_ge(s_grp, n + 1)
                if kind == "ln":
                    dst = lnT[:, c, 512 * j:512 * (j + 1)]
                else:
                    if n >= 8:
                        dve.wait_ge(s_w3st[n % 2], 16 * ((n - 6) // 2))
                    dst = turned[:, n % 2, :]
                nc.vector.tensor_copy(dst, bank[6 + n % 2][:, :]).then_inc(s_grpout, 1)

            def chunk_out(n):
                l, at, w = MCHUNKS[n]
                dve.wait_ge(s_mchunk, n + 1)
                dve.wait_ge(s_mbias, 16 * (l + 1 if l < 3 else 6))
                if n >= 2:
                    dve.wait_ge(s_modst[n % 2], 16 * (n // 2))
                    dve.wait_ge(s_mturn, n - 1)
                nc.vector.tensor_tensor(mrow[:, n % 2, 0:w], bank[2 + n % 2][0:B, 0:w], mbias[:, at:at + w], ALU.add)\
                    .then_inc(s_mchout, 1)

            for n in range(6):
                group_out(n)
            for n in range(len(MCHUNKS)):
                chunk_out(n)
            for n in range(6, len(GROUPS)):
                group_out(n)
            dve.wait_ge(s_grp, len(GROUPS))
            link(nc.vector.memset(kflat[:, :], 0.0))
            link(nc.vector.memset(vflat[:, :], 0.0))
            for a in range(2):
                for s in range(2):
                    for g in range(G):
                        ones = vaug[:, a, s, g, :].rearrange("p (h x) -> p h x", h=HG)[:, :, D:D + 1]
                        ins = nc.vector.memset(ones, 1.0)
            ins.then_inc(s_zero, 1)
            dve.wait_ge(s_zero, 1)
            settle()
            dve.wait_ge(s_mturned, len(MCHUNKS))

            def apart():
                dve.sem_inc(s_apart, 1)

            def normalise(k, x, dst, n):
                apart()
                for s in range(n):
                    ins = nc.vector.bn_stats(stats[:, s, :], x[:, s, :])
                link(ins)
                apart()
                for s in range(n):
                    ins = nc.vector.bn_aggr(mv[:, s, :], stats[:, s, :])
                ins.then_inc(s_var, 1)
                dve.wait_ge(s_var, done(k))
                dve.wait_ge(s_rstd, done(k))
                for s in range(n):
                    ins = nc.vector.tensor_scalar(dst[:, s, :], x[:, s, :], mv[:, s, 0:1], rstd[:, s:s + 1],
                                                  ALU.subtract, ALU.mult)
                return ins

            def take(l, j, kind, a, i):
                dve.wait_ge(s_work, done(number(is_use, l, j, kind, a, i)))
                return bank[WB + work_bank(kind, a, i)]

            def fetch_mods(l, it, dst, mod, n):
                sh, sc = (2 * (MOD0[l] + m) for m in mod)
                nc.vector.tensor_copy(dst[:, 0, :, :], modT[:, sh:sh + 2, bass.ds(it * n, n)])
                return nc.vector.tensor_scalar(dst[:, 1, :, :], modT[:, sc:sc + 2, bass.ds(it * n, n)], 1.0, None, ALU.add)

            def residual(src, bias, g, x, dst, i):
                r = res[:, i % 2, :]
                if bias is not None:
                    link(nc.vector.tensor_tensor(r, src, bias, ALU.add))
                    src = r
                if g is not None:
                    link(nc.vector.tensor_tensor(r, src, g, ALU.mult))
                    src = r
                return nc.vector.tensor_tensor(dst, src, x, ALU.add)

            def rotate(l, j, kind, a, i):
                cos = rope_cos.unsqueeze(1).to_broadcast([P, 4, T])
                sin = rope_sin.unsqueeze(1).to_broadcast([P, 4, T])
                dst = (qT if kind == "q" else kT)[:, a, :, :, :].rearrange("p c s t -> p (c s) t")
                v = raw[:, :, :, :].rearrange("p c s t -> p (c s) t")
                w = swapped[:, :, :, :].rearrange("p c s t -> p (c s) t")
                dve.wait_ge(s_tact, done(number(is_taken_by("act"), l, j, kind, a, i)))
                apart()
                link(nc.vector.stream_shuffle(w, v, [(p // D) * D + (p + D // 2) % D for p in range(32)]))
                link(nc.vector.tensor_tensor(w, w, sin, ALU.mult))
                link(nc.vector.tensor_tensor(dst, v, cos, ALU.mult))
                nc.vector.tensor_tensor(dst, dst, w, ALU.add).then_inc(s_rope, 1)

            def top_k(l, j, a, i):
                t = number(is_topk_chunk, l, j, "scores", a, i)
                sc = bank[SC + i % 2]
                apart()
                for h in range(HG):
                    ins = nc.vector.max(top[:, 0, h, :], sc[:, h * T:(h + 1) * T])
                link(ins)
                nc.vector.tensor_scalar(negm[:, :], top[:, 0, :, 0], -(D ** -0.5), None, ALU.mult)
                for h in range(HG):
                    ins = nc.vector.match_replace(left[:, h, :], top[:, 0, h, :], sc[:, h * T:(h + 1) * T], NEG)
                ins.then_inc(s_negm, 1)
                dve.wait_ge(s_negm, done(t))
                apart()
                for h in range(HG):
                    ins = nc.vector.max(top[:, 1, h, :], left[:, h, :])
                link(ins)
                apart()
                for h in range(HG):
                    ins = nc.vector.match_replace(left[:, h, :], top[:, 1, h, :], left[:, h, :], NEG)
                link(ins)
                dve.wait_ge(s_texp, done(t))
                p = prob[:, i % 2, :, :].rearrange("p h t -> p (h t)")
                nc.vector.scalar_tensor_tensor(p, left[:, :, :].rearrange("p h t -> p (h t)"), NEG, p,
                                               ALU.is_equal, ALU.mult).then_inc(s_shift, 1)

            def attention_step(l, it):
                cfg = LAYER[l]
                for kind, a, i, off in steps_of(it):
                    j = it + off
                    if kind == "norm":
                        act_takes = is_taken_by("act")
                        mod = cfg["self_mod"] if a == SELF else cfg["cross_mod"]
                        if mod is not None:
                            dve.wait_ge(s_tact, freed(number(act_takes, l, j, "x_turn", a, 0), N_ACT))
                            fetch_mods(l, j, cur[:, a, :, :, :], mod, 2).then_inc(s_cur[a], 1)
                        if a == SELF:
                            dve.wait_ge(s_x, (pair_of(l, j) + 1) * 16)
                        else:
                            dve.wait_ge(s_res, done(number(is_taken_by("res"), l, j, "out_proj", SELF, 1)))
                        dve.wait_ge(s_work, freed(number(is_use, l, j, "x_turn", a, 0), N_USE))
                        normalise(vars_of(l, j, kind, a), xin if a == SELF else x1, xn[:, a, :, :], 2).then_inc(s_xn, 1)
                        if a == SELF:
                            nc.vector.tensor_copy(xself[:, :, :], xin[:, :, :]).then_inc(s_kept, 1)
                    elif kind == "norm_ctx" and cfg["ctx_norm"]:
                        dve.wait_ge(s_ctx, (pair_of(l, j) + 1) * 16)
                        dve.wait_ge(s_work, freed(number(is_use, l, j, "ctx_turn", CROSS, 0), N_USE))
                        normalise(vars_of(l, j, kind, a), cin, cn, 2).then_inc(s_cn, 1)
                    elif kind == "keep":
                        dve.wait_ge(s_res, START + 4 * PAIRS * l if isinstance(j, int) and j == 0 else
                                    done(number(is_taken_by("res"), l, j - 1, "out_proj", CROSS, 1)))
                        nc.vector.tensor_copy(x1cross[:, :, :], x1[:, :, :]).then_inc(s_kept, 1)
                    elif kind in ("q", "k") and cfg["rope"]:
                        rotate(l, j, kind, a, i)
                    elif kind == "v":
                        src = take(l, j, kind, a, i)
                        for s in range(2):
                            ins = nc.vector.tensor_copy(
                                vaug[:, a, s, :, :].rearrange("p g (h x) -> p g h x", h=HG)[:, :, :, 0:D],
                                src[:, s * C:(s + 1) * C].rearrange("p (g h d) -> p g h d", g=G, h=HG))
                        ins.then_inc(s_tdve, 1)
                    elif kind == "scores":
                        k = number(is_chunk, l, j, kind, a, i)
                        dve.wait_ge(s_score, done(k))
                        if cfg["topk"] and a == CROSS:
                            top_k(l, j, a, i)
                            continue
                        sc = bank[SC + i % 2][:, :].rearrange("p (h t) -> p h t", h=HG)
                        link(nc.vector.tensor_reduce(mx[:, i % 2, :], sc, AX.X, ALU.max))
                        dve.wait_ge(s_turn, freed(k, 2))
                        nc.vector.tensor_tensor(prob[:, i % 2, :, :], sc,
                                                mx[:, i % 2, :].unsqueeze(2).to_broadcast([P, HG, T]),
                                                ALU.subtract).then_inc(s_shift, 1)
                    elif kind == "out_turn":
                        src = take(l, j, kind, a, i)[:, 0:G * GW].rearrange("p (h x) -> p h x", x=DA)
                        link(nc.vector.reciprocal(rsum[:, :], src[:, :, D]))
                        nc.vector.tensor_tensor(on[:, :, :], src[:, :, 0:D], rsum[:, :].unsqueeze(2).to_broadcast([P, H, D]),
                                                ALU.mult).then_inc(s_tdve, 1)
                    elif kind == "out_proj":
                        src = take(l, j, kind, a, i)[:, 0:C]
                        gt = cfg["self_gate"] if a == SELF else cfg["cross_gate"]
                        if gt is not None and i == 0:
                            gates_before = sum(PAIRS * (LAYER[m]["self_gate" if a == SELF else "cross_gate"] is not None)
                                               for m in range(l))
                            dve.wait_ge(s_gate[a], (j + (gates_before + 1)) * 16)
                        if i == 0:
                            if a == CROSS:
                                dve.wait_ge(s_xast, (pair_of(l, j) + 1) * 16)
                            dve.wait_ge(s_kept, kept(l, j, a))
                        residual(src, bo[:, a, :] if cfg["bias"] else None, gate[:, a, i, :] if gt is not None else None,
                                 (xself if a == SELF else x1cross)[:, i, :], (x1 if a == SELF else x2)[:, i, :], i)\
                            .then_inc(s_res, 1)

            def front(l, it):
                cfg = LAYER[l]
                m = quad_of(l, it)
                dve.wait_ge(s_mh, freed(m, 1))
                fetch_mods(l, it, mcur, cfg["mlp_mod"], 4).then_inc(s_mcur, 1)
                dve.wait_ge(s_mx, (m + 1) * 16)
                dve.wait_ge(s_mT, freed(m * KC + 1, KC))
                normalise(vars_mlp(l, it), mx_in, mxn, 4).then_inc(s_mxn, 1)

            def mlp_step(l, it, last):
                cfg = LAYER[l]
                m = quad_of(l, it)
                b0 = BROW[l] + (B_F if l < 3 else 0)
                if cfg["swiglu"]:
                    for f in range(FC):
                        dve.wait_ge(s_up, done(it * ups(l) + (up0(l) + 2 * f + 1)))
                        dve.wait_ge(s_upact, done(it * FC + f))
                        nc.vector.scalar_tensor_tensor(hid[:, f, :], bank[2 * (f % 2) + 1][:, :],
                                                       biasT[:, b0 + FC + f:b0 + FC + f + 1], act_a[:, f % 2, :],
                                                       ALU.add, ALU.mult).then_inc(s_upmul, 1)
                if not last:
                    front(l, it + 1)
                dve.wait_ge(s_mres, (m + 1) * 16)
                if cfg["mlp_gate"] is not None:
                    dve.wait_ge(s_mgate, (m + 1) * 16)
                dve.wait_ge(s_wm, 48 * (l + 1))
                dve.wait_ge(s_mst, (m + 1) * 16)
                for s in range(4):
                    dve.wait_ge(s_down, done(m * 4 + s))
                    residual(bank[4 + s % 2][:, 0:C], bm[:, :], mgate[:, s, :] if cfg["mlp_gate"] is not None else None,
                             mres[:, s, :], mout[:, s, :], s).then_inc(s_mo, 1)

            LINKS = DVE_LINKS
            for l in range(LAYERS):
                dve.wait_ge(s_wa, 16 * sum(WA_N[:l + 1]))
                for j in (-1, 0):
                    attention_step(l, j)
                settle()
                with dve.Fori(0, PAIRS - 2) as it:
                    enter(it, LINKS[l][0])
                    attention_step(l, it + 1)
                leave(PAIRS - 2)
                for j in (PAIRS - 1, PAIRS):
                    attention_step(l, j)
                settle()
                front(l, 0)
                settle()
                with dve.Fori(0, QUADS - 1) as it:
                    enter(it, LINKS[l][1])
                    mlp_step(l, it, False)
                leave(QUADS - 1)
                mlp_step(l, QUADS - 1, True)
                settle()

        @block.tensor
        def _(pe):
            for s in STARTED["pe"]:
                pe.sem_inc(s, START)
            mm, turn = nc.tensor.matmul, nc.tensor.transpose

            pe.wait_ge(s_const, 16)
            pe.wait_ge(s_silu, 1)
            for a in range(2):
                for c in range(KC):
                    ins = turn(bank[0][:, (2 * a + c) * B:(2 * a + c + 1) * B], cond[:, a, c * P:(c + 1) * P],
                               ident[0:B, 0:B])
            ins.then_inc(s_condT, 1)
            pe.wait_ge(s_brow, 16 * 13)
            turn(bank[1][:, 0:NBROW], brows[:, :], ident[0:NBROW, 0:NBROW]).then_inc(s_bT, 1)

            def group(n):
                kind, c, j = GROUPS[n]
                if n >= 2:
                    pe.wait_ge(s_grpout, n - 1)
                dst = bank[6 + n % 2]
                if kind == "w2":
                    for f in range(2):
                        for r in range(2):
                            ins = turn(dst[:, f * C + r * P:f * C + (r + 1) * P], raw_w2[:, r, (c + f) * P:(c + f + 1) * P], ident)
                else:
                    src = {"ln": raw_ln, "attn": raw_attn, "w1": raw_w1}[kind]
                    for b in range(4):
                        ins = turn(dst[:, b * P:(b + 1) * P], src[:, 4 * j + b, c * P:(c + 1) * P], ident)
                ins.then_inc(s_grp, 1)

            pe.wait_ge(s_rawln, 48)
            for n in range(6):
                group(n)
            pe.wait_ge(s_condTs, 1)

            def mod_chunk(n):
                l, at, w = MCHUNKS[n]
                if l < 3:
                    pe.wait_ge(s_ada[l], 16)
                else:
                    pe.wait_ge(s_grpout, 6)
                if n >= 2:
                    pe.wait_ge(s_mchout, n - 1)
                src = (ada[l % 2] if l < 3 else lnT)
                for c in range(KC):
                    ins = mm(bank[2 + n % 2][0:B, 0:w], condT[:, 0 if l == 3 else 1, c, :], src[:, c, at:at + w],
                             start=c == 0, stop=c == KC - 1)
                ins.then_inc(s_mchunk, 1)

            def mod_turn(n):
                l, at, w = MCHUNKS[n]
                pe.wait_ge(s_mchout, n + 1)
                if n >= 2:
                    pe.wait_ge(s_mturned, n - 1)
                for b in range(w // P):
                    ins = turn(bank[4 + n % 2][:, b * B:(b + 1) * B], mrow[:, n % 2, b * P:(b + 1) * P], ident[0:B, 0:B])
                ins.then_inc(s_mturn, 1)

            for n in range(len(MCHUNKS)):
                mod_chunk(n)
                if n >= 1:
                    mod_turn(n - 1)
            mod_turn(len(MCHUNKS) - 1)
            pe.wait_ge(s_rawattn, 96)
            pe.wait_ge(s_raww1, 16)
            pe.wait_ge(s_raww2, 16)
            for n in range(6, len(GROUPS)):
                group(n)
            pe.wait_ge(s_bTs, 1)
            pe.wait_ge(s_grpout, len(GROUPS))
            pe.wait_ge(s_mturned, len(MCHUNKS))
            pe.wait_ge(s_zero, 1)

            def attention_step(l, it):
                cfg = LAYER[l]
                act_takes, dve_takes = is_taken_by("act"), is_taken_by("dve")
                for step in steps_of(it):
                    kind, a, i, off = step
                    j = it + off
                    if kind in TAKER:
                        dst = bank[WB + work_bank(kind, a, i)]
                        before = use_before(it, step)
                        if before is not None:
                            back, (kind0, a0, i0, off0) = before
                            who = TAKER[kind0]
                            pe.wait_ge(dict(act=s_tact, dve=s_tdve, res=s_res)[who],
                                       done(number(is_taken_by(who), l, it + (back + off0), kind0, a0, i0)))
                    if kind == "x_turn":
                        pe.wait_ge(s_xn, done(number(is_token_norm, l, j, "norm", a, 0)))
                        for c in range(KC):
                            for s in range(2):
                                ins = turn(dst[:, (2 * c + s) * T:(2 * c + s + 1) * T], xn[:, a, s, c * P:(c + 1) * P], ident)
                        ins.then_inc(s_work, 1)
                    elif kind == "ctx_turn":
                        if cfg["ctx_norm"]:
                            pe.wait_ge(s_cn, done(j))
                        else:
                            pe.wait_ge(s_ctx, (pair_of(l, j) + 1) * 16)
                        src = cn if cfg["ctx_norm"] else cin
                        for c in range(KC):
                            for s in range(2):
                                ins = turn(dst[:, (2 * c + s) * T:(2 * c + s + 1) * T], src[:, s, c * P:(c + 1) * P], ident)
                        ins.then_inc(s_work, 1)
                    elif kind in ("q", "k", "v"):
                        turned_by = ("x_turn", a, 0) if a == SELF or kind == "q" else ("ctx_turn", a, 0)
                        pe.wait_ge(s_tact, done(number(act_takes, l, j, *turned_by)))
                        src = hT if turned_by[0] == "x_turn" else cT
                        at = {("q", 0): W_Q, ("k", 0): W_K, ("v", 0): W_V, ("q", 1): W_XQ, ("k", 1): W_XK, ("v", 1): W_XV}[kind, a]
                        for m in range(2):
                            for c in range(KC):
                                if kind == "v":
                                    ins = mm(dst[:, m * C:(m + 1) * C], src[:, c, m, :], wa[:, c, at:at + C],
                                             start=c == 0, stop=c == KC - 1)
                                else:
                                    ins = mm(dst[:, m * 2 * T:(m + 1) * 2 * T], wa[:, c, at + m * P:at + (m + 1) * P],
                                             src[:, c, :, :].rearrange("p s t -> p (s t)"), start=c == 0, stop=c == KC - 1)
                        ins.then_inc(s_work, 1)
                    elif kind == "scores":
                        k = number(is_chunk, l, j, kind, a, i)
                        s, grp = divmod(i, G)
                        c, half = divmod(grp, 2)
                        if i == 0:
                            pe.wait_ge(s_spread[a], (pair_of(l, j) + 1) * (16 * (P // D)))
                            if cfg["rope"]:
                                pe.wait_ge(s_rope, done(number(is_rotated, l, j, "q", a, 0)))
                            else:
                                pe.wait_ge(s_tact, done(number(act_takes, l, j, "q", a, 0)))
                        pe.wait_ge(s_shift, freed(k, 2))
                        mm(bank[SC + i % 2][:, :], qT[:, a, c, s, :],
                           kblk[:, a, c, s, HG * half:HG * (half + 1), :].rearrange("p h t -> p (h t)"),
                           start=True, stop=True).then_inc(s_score, 1)
                    elif kind == "turn":
                        k = number(is_chunk, l, j, "scores", a, i)
                        if cfg["topk"] and a == CROSS:
                            pe.wait_ge(s_shift, done(k))
                        else:
                            pe.wait_ge(s_exp, done(number(is_plain_chunk, l, j, "scores", a, i)))
                        pe.wait_ge(s_probT, freed(k, 2))
                        for h in range(HG):
                            ins = turn(bank[PT + i % 2][:, h * T:(h + 1) * T], prob[:, i % 2, h, :], ident)
                        ins.then_inc(s_turn, 1)
                    elif kind == "values":
                        k = number(is_chunk, l, j, "scores", a, i)
                        s, grp = divmod(i, G)
                        if i == 0:
                            pe.wait_ge(s_tdve, done(number(dve_takes, l, j, "v", a, 0)))
                        if grp == 0:
                            pe.wait_ge(s_out, freed(number(is_output, l, j, "values", a, i + G - 1), 1))
                        pe.wait_ge(s_probT, done(k))
                        for h in range(HG):
                            ins = mm(bank[OB][0:GW, grp * T:(grp + 1) * T], vaug[:, a, s, grp, h * GW:(h + 1) * GW],
                                     probT[:, i % 2, h, :], start=h == 0, stop=h == HG - 1)
                        ins.then_inc(s_val, 1)
                    elif kind == "out_turn":
                        pe.wait_ge(s_out, done(number(is_output, l, j, "values", a, i * G + G - 1)))
                        for grp in range(G):
                            ins = turn(dst[:, grp * GW:(grp + 1) * GW], outT[:, grp, :], ident[0:GW, 0:GW])
                        ins.then_inc(s_work, 1)
                    elif kind == "out_back":
                        pe.wait_ge(s_tdve, done(number(dve_takes, l, j, "out_turn", a, i)))
                        for c in range(KC):
                            ins = turn(dst[:, c * T:(c + 1) * T],
                                       on[:, :, :].rearrange("p h d -> p (h d)")[:, c * P:(c + 1) * P], ident)
                        ins.then_inc(s_work, 1)
                    elif kind == "out_proj":
                        pe.wait_ge(s_tact, done(number(act_takes, l, j, "out_back", a, i)))
                        at = W_SO if a == SELF else W_XO
                        for c in range(KC):
                            ins = mm(dst[:, 0:C], oT[:, c, :], wa[:, c, at:at + C], start=c == 0, stop=c == KC - 1)
                        ins.then_inc(s_work, 1)

            def quad_turn(l, it):
                m = quad_of(l, it)
                pe.wait_ge(s_mxn, done(m))
                pe.wait_ge(s_mh, freed(m, 1))
                for c in range(KC):
                    for s in range(4):
                        ins = turn(bank[6 + c][:, s * T:(s + 1) * T], mxn[:, s, c * P:(c + 1) * P], ident)
                    ins.then_inc(s_mT, 1)

            def mlp_step(l, it, last):
                cfg = LAYER[l]
                m = quad_of(l, it)
                n = ups(l)
                w1 = wm[:, 0:KC * n * P].rearrange("p (c n) -> p c n", c=KC)
                w2 = wm[:, 4096:6144].rearrange("p (c n) -> p c n", c=FC)
                pe.wait_ge(s_mh, done(m))
                for j in range(n):
                    if cfg["swiglu"]:
                        f, lin = divmod(j, 2)
                        col = (f + lin * FC) * P
                        b = 2 * (f % 2) + lin
                        if lin:
                            pe.wait_ge(s_upmul, freed(it * FC + f, 2))
                        else:
                            pe.wait_ge(s_upact, freed(it * FC + f, 2))
                    else:
                        col = j * P
                        b = j % 4
                        pe.wait_ge(s_upact, freed(it * FC + (l * QUADS * FC + j), 4))
                    for c in range(KC):
                        ins = mm(bank[b][:, :], w1[:, c, col:col + P], fT[:, c, :, :].rearrange("p s t -> p (s t)"),
                                 start=c == 0, stop=c == KC - 1)
                    ins.then_inc(s_up, 1)
                if not last:
                    quad_turn(l, it + 1)
                if cfg["swiglu"]:
                    pe.wait_ge(s_upmul, done(it * FC + (FC - 1)))
                else:
                    pe.wait_ge(s_upact, done(it * FC + (l * QUADS * FC + FC - 1)))
                for s in range(4):
                    pe.wait_ge(s_mo, freed(m * 4 + s, 2))
                    for f in range(FC):
                        ins = mm(bank[4 + s % 2][:, 0:C], hid[:, f, s * T:(s + 1) * T], w2[:, f, :],
                                 start=f == 0, stop=f == FC - 1)
                    ins.then_inc(s_down, 1)

            for l in range(LAYERS):
                pe.wait_ge(s_wa, 16 * sum(WA_N[:l + 1]))
                pe.wait_ge(s_mo, START + 4 * QUADS * l)
                for j in (-1, 0):
                    attention_step(l, j)
                with pe.Fori(1, PAIRS - 1) as j:
                    attention_step(l, j)
                for j in (PAIRS - 1, PAIRS):
                    attention_step(l, j)
                pe.wait_ge(s_out, START + 4 * PAIRS * (l + 1))
                pe.wait_ge(s_res, START + 4 * PAIRS * (l + 1))
                quad_turn(l, 0)
                pe.wait_ge(s_wm, 48 * (l + 1))
                with pe.Fori(0, QUADS - 1) as it:
                    mlp_step(l, it, False)
                mlp_step(l, QUADS - 1, True)


DVE_LINKS = ((46, 9), (29, 9), (28, 9), (34, 5))


_INS = (
    ["x", "cond_1024", "ctx_1024"]
    + ["L0_xcond_" + n for n in ("w_ada b_ada w_qkv b_qkv w_so b_so w_q b_q w_kv b_kv w_co b_co w_m1 b_m1 w_m2 b_m2".split())]
    + ["L1_xcond_" + n for n in ("W_mod b_mod W_qkv b_qkv W_proj b_proj W_qc b_qc W_kvc b_kvc W_cproj b_cproj W_mlp1 b_mlp1 "
                                 "W_mlp2 b_mlp2".split())]
    + ["L2_xcond_" + n for n in ("adaln_w adaln_b qkv_w qkv_b sa_proj_w sa_proj_b q_w q_b kv_w kv_b ca_proj_w ca_proj_b "
                                 "fc1_w fc1_b fc2_w fc2_b".split())]
    + ["L3_xcond_" + n for n in ("ln1_w ln1_b ln2_w ln2_b ln3_w ln3_b qkv_w sa_out_w q_w k_w v_w ca_out_w ffn_w1 ffn_b1 "
                                 "ffn_w2 ffn_b2".split())]
)


def tables():
    import numpy as np

    half = D // 2
    inv_freq = (1.0 / np.float32(10000.0) ** (np.arange(half, dtype=np.float32) / np.float32(half))).astype(np.float32)
    ang = (np.arange(T, dtype=np.float32)[:, None] * inv_freq[None, :]).astype(np.float32)
    comp = np.arange(P) % D
    cos = np.cos(ang)[:, comp % half].T
    sin = np.sin(ang)[:, comp % half].T * np.where(comp < half, -1.0, 1.0)[:, None]
    eps = np.tile(np.array([[1e-6, 1e-5]]), (P, 1))
    return np.ascontiguousarray(np.concatenate([np.eye(P), cos, sin, eps], axis=1).astype(np.float32))


def kernel(**inputs):
    import numpy as _np
    import concourse.bacc as _bacc
    from concourse import mybir as _mybir
    from concourse.bass_utils import run_bass_kernel_spmd as _run

    nc = _bacc.Bacc("TRN2", target_bir_lowering=False, num_devices=1)
    arrays, dram = {}, {}
    for name in _INS:
        a = _np.ascontiguousarray(inputs[name])
        arrays[f"in_{name}_dram"] = a
        dram[name] = nc.dram_tensor(f"in_{name}_dram", a.shape, _mybir.dt.from_np(a.dtype), kind="ExternalInput").ap()
    t = tables()
    arrays["tables_dram"] = t
    dram["tables"] = nc.dram_tensor("tables_dram", t.shape, _mybir.dt.from_np(t.dtype), kind="ExternalInput").ap()
    out = nc.dram_tensor("out_dram", (B, T, C), F32, kind="ExternalOutput").ap()
    build(nc, dram, out)
    r = _run(nc, [arrays], core_ids=[0])
    return r.results[0]["out_dram"]
```

```python
import concourse.bass as bass
from concourse import mybir
from contextlib import ExitStack

F32 = mybir.dt.float32
ALU = mybir.AluOpType
ACT = mybir.ActivationFunctionType
AX = mybir.AxisListType

P = 128
B = 16
T = 128
C = 256
KC = C // P
H = 16
D = C // H
G = 4
HG = H // G
DA = D + 1
GW = HG * DA
HID = 1024
FC = HID // P
TOPK = 16
LAYERS = 4
PAIRS = B // 2
QUADS = B // 4
START = 32
NEG = -3.0e38

W_Q, W_K, W_V, W_SO, W_XQ, W_XK, W_XV, W_XO = range(0, 8 * C, C)
WA = 8 * C

MOD0 = (0, 9, 15, 21)
NMOD = 27
LAYER = (
    dict(eps=1e-6, self_mod=(0, 1), self_gate=2, cross_mod=(3, 4), cross_gate=5, mlp_mod=(6, 7), mlp_gate=8,
         ctx_norm=False, topk=True, rope=False, swiglu=True, act=ACT.Silu, bias=True),
    dict(eps=1e-6, self_mod=(0, 1), self_gate=2, cross_mod=None, cross_gate=None, mlp_mod=(3, 4), mlp_gate=5,
         ctx_norm=True, topk=False, rope=False, swiglu=False, act=ACT.Gelu_apprx_tanh, bias=True),
    dict(eps=1e-6, self_mod=(0, 1), self_gate=2, cross_mod=None, cross_gate=None, mlp_mod=(3, 4), mlp_gate=5,
         ctx_norm=False, topk=False, rope=False, swiglu=False, act=ACT.Gelu_apprx_tanh, bias=True),
    dict(eps=1e-5, self_mod=(1, 0), self_gate=None, cross_mod=(3, 2), cross_gate=None, mlp_mod=(5, 4), mlp_gate=None,
         ctx_norm=False, topk=False, rope=True, swiglu=False, act=ACT.Gelu, bias=False),
)
EPS_COL = (0, 0, 0, 1)

BROW = (0, 28, 48, 68)
NBROW = 76
B_Q, B_K, B_V, B_XQ, B_XK, B_XV, B_F = 0, 2, 4, 6, 8, 10, 12

SELF, CROSS = 0, 1
CHUNKS = ((SELF, 0, 1), (CROSS, 6, -1), (SELF, 1, 1), (CROSS, 7, -1), (SELF, 2, 1), (SELF, 3, 1), (SELF, 4, 1),
          (CROSS, 0, 0), (SELF, 5, 1), (CROSS, 1, 0), (SELF, 6, 1), (CROSS, 2, 0), (SELF, 7, 1), (CROSS, 3, 0),
          (CROSS, 4, 0), (CROSS, 5, 0))

AMONG = {
    0: [("v", SELF, 0, 1), ("out_turn", SELF, 1, 0)],
    1: [("out_back", SELF, 1, 0)],
    2: [("out_proj", SELF, 1, 0), ("stats", CROSS, 0, 0)],
    3: [("out_back", CROSS, 0, -1), ("norm", CROSS, 0, 0), ("rotate_k", CROSS, 0, 0)],
    4: [("x_turn", CROSS, 0, 0), ("out_proj", CROSS, 0, -1)],
    5: [("rotate_q", CROSS, 0, 0), ("keep", SELF, 0, 1)],
    7: [("v", CROSS, 0, 0)],
    8: [("stats_ctx", CROSS, 0, 1)],
    9: [("out_back", CROSS, 1, -1), ("norm_ctx", CROSS, 0, 1), ("stats", SELF, 0, 2)],
    10: [("norm", SELF, 0, 2), ("out_proj", CROSS, 1, -1), ("keep", CROSS, 0, 0), ("ctx_turn", CROSS, 0, 1)],
    12: [("out_back", SELF, 0, 1), ("rotate_k", SELF, 0, 2)],
    13: [("q", SELF, 0, 2), ("out_proj", SELF, 0, 1)],
}
AFTER_SCORES = {
    2: [("out_turn", CROSS, 0, -1)],
    3: [("k", CROSS, 0, 0)],
    5: [("q", CROSS, 0, 0)],
    8: [("out_turn", CROSS, 1, -1)],
    11: [("x_turn", SELF, 0, 2), ("out_turn", SELF, 0, 1)],
    12: [("k", SELF, 0, 2)],
    14: [("rotate_q", SELF, 0, 2)],
}
TURN_LAG, VALUES_LAG = 3, 4


def chunk_steps():
    def behind(kind, t):
        a, i, off = CHUNKS[t]
        return (kind, a, i, off if t >= 0 else off - 1)

    steps = []
    for t in range(len(CHUNKS)):
        steps += [behind("scores", t)] + AFTER_SCORES.get(t, [])
        steps += [behind("turn", t - TURN_LAG), behind("values", t - VALUES_LAG)]
        if CHUNKS[t - 1][0] == CROSS:
            steps.append(behind("mark", t - 1))
        steps += [behind("rest", t)] + AMONG.get(t, []) + [behind("exp", t)]
    return steps


STEPS = chunk_steps()
for _kind in ("scores", "turn", "values"):
    assert len([s for s in STEPS if s[0] == _kind]) == len({s[:3] for s in STEPS if s[0] == _kind}) == len(CHUNKS)
OFFSET = {s[:3]: s[3] for s in STEPS}
FIRST, LAST = -2, PAIRS


def steps_of(j):
    return [s for s in STEPS if not isinstance(j, int) or 0 <= j + s[3] < PAIRS]


def number(sel, l, pair, kind, a, i):
    off = OFFSET[kind, a, i]
    picked = [s for s in STEPS if sel(l, s)]

    def before(layer, j):
        all_before = sum(0 <= jj + s[3] < PAIRS for m in range(layer) for jj in range(FIRST, LAST + 1)
                         for s in STEPS if sel(m, s))
        return all_before + sum(0 <= jj + s[3] < PAIRS for jj in range(FIRST, j) for s in picked)

    step = (kind, a, i, off)
    if isinstance(pair, int):
        j = pair - off
        return before(l, j) + [s for s in picked if 0 <= j + s[3] < PAIRS].index(step)
    return pair * len(picked) + (before(l, 1) + picked.index(step) - (off + 1) * len(picked))


TAKER = dict(x_turn="act", ctx_turn="act", k="act", q="act", out_back="act", v="dve", out_turn="dve", out_proj="res")
USES = [s for s in STEPS if s[0] in TAKER]
WORK_BANKS = 3


def is_use(l, s):
    return s[0] in TAKER


def is_taken_by(who):
    return lambda l, s: TAKER.get(s[0]) == who


def is_chunk(l, s):
    return s[0] == "scores"


def is_plain_chunk(l, s):
    return s[0] == "scores" and not (LAYER[l]["topk"] and s[1] == CROSS)


def is_topk_chunk(l, s):
    return s[0] == "scores" and LAYER[l]["topk"] and s[1] == CROSS


def is_values(l, s):
    return s[0] == "values"


def is_output(l, s):
    return s[0] == "values" and s[2] % G == G - 1


def is_rotated(l, s):
    return s[0] in ("q", "k") and LAYER[l]["rope"]


def is_copy(l, s):
    return s[0] == "keep"


def is_gated_copy(l, s):
    return s[0] == "keep" and LAYER[l]["self_gate" if s[1] == SELF else "cross_gate"] is not None


def is_token_norm(l, s):
    return s[0] == "norm"


def is_norm(l, s):
    return s[0] == "norm" or (s[0] == "norm_ctx" and LAYER[l]["ctx_norm"])


def work_bank(kind, a, i):
    return [u[:3] for u in USES].index((kind, a, i)) % WORK_BANKS


def step_before(j, step, match, nth=1):
    todo = steps_of(j)
    todo = todo[:todo.index(step)]
    for back in range(3):
        for s in reversed(todo):
            if match(s):
                nth -= 1
                if nth == 0:
                    return -back, s
        if isinstance(j, int):
            todo = steps_of(j - back - 1) if j - back - 1 >= FIRST else []
        else:
            todo = STEPS
    return None


def use_before(j, step):
    mine = work_bank(*step[:3])
    return step_before(j, step, lambda s: s[0] in TAKER and work_bank(*s[:3]) == mine)


def topk_slot(l, pair, a, i):
    return i % 2


def slot(n, l, pair, a, i):
    if isinstance(pair, int):
        return number(is_chunk, l, pair, "scores", a, i) % n
    assert len(CHUNKS) % n == 0
    return number(is_chunk, l, 1 + OFFSET["scores", a, i], "scores", a, i) % n


def done(k):
    return k + (START + 1)


def freed(k, n):
    return k + (START + 1 - n)


def build(nc, dram, out):
    ctx = ExitStack()
    with ctx:
        def sb(name, shape, dt=F32):
            return ctx.enter_context(nc.sbuf_tensor(name, shape, dt))

        def sem(name):
            return ctx.enter_context(nc.semaphore(name))

        mods_dram = nc.dram_tensor("mods_dram", [B, NMOD * C], F32).ap()
        wa3_dram = nc.dram_tensor("wa3_dram", [C, WA], F32).ap()
        w13_dram = nc.dram_tensor("w13_dram", [C, HID], F32).ap()
        w23_dram = nc.dram_tensor("w23_dram", [HID, C], F32).ap()
        xa_dram = [nc.dram_tensor(f"xa{l}_dram", [B, T, C], F32).ap() for l in range(LAYERS)]
        xm_dram = [nc.dram_tensor(f"xm{l}_dram", [B, T, C], F32).ap() for l in range(LAYERS - 1)] + [out]
        x_src = [dram["x"]] + xm_dram[:-1]

        const = sb("const", [P, 3 * P + 2])
        ident = const[:, 0:P]
        rope_cos = const[:, P:2 * P]
        rope_sin = const[:, 2 * P:3 * P]
        eps = const[:, 3 * P:3 * P + 2]
        neghalf = sb("neghalf", [P, 4])
        wa = sb("wa", [P, KC, WA])
        wm = sb("wm", [P, 3 * 2048])
        bo = sb("bo", [P, 2, C])
        bm = sb("bm", [P, C])
        modT = sb("modT", [P, 2 * NMOD, B])
        brows = sb("brows", [NBROW, P])
        biasT = sb("biasT", [P, NBROW])
        cond = sb("cond", [B, 2, C])
        condT = sb("condT", [P, 2, KC, B])
        stats = sb("stats", [P, 4, 6])
        mv = sb("mv", [P, 4, 2])
        vare = sb("vare", [P, 4])
        rstd = sb("rstd", [P, 4])
        xin = sb("xin", [P, 2, C])
        xself = sb("xself", [P, 2, C])
        x1 = sb("x1", [P, 2, C])
        x1cross = sb("x1cross", [P, 2, C])
        x2 = sb("x2", [P, 2, C])
        cin = sb("cin", [P, 2, C])
        xn = sb("xn", [P, 2, 2, C])
        cn = sb("cn", [P, 2, C])
        gate = sb("gate", [P, 2, 2, C])
        cur = sb("cur", [P, 2, 2, KC, 2])
        hT = sb("hT", [P, KC, 2, T])
        cT = sb("cT", [P, KC, 2, T])
        qT = sb("qT", [P, 2, KC, 2, T])
        kT = sb("kT", [P, 2, KC, 2, T])
        kblk = sb("kblk", [P, 2, KC, 2, 8, T])
        vaug = sb("vaug", [P, 2, 2, G, HG * (GW + DA)])
        mx = sb("mx", [P, 2, HG])
        prob = sb("prob", [P, 4, HG, T])
        probT = sb("probT", [P, 2, HG, T])
        left = sb("left", [P, 2, HG, T])
        top = sb("top", [P, 2, HG, 8])
        negm = sb("negm", [P, 2, HG])
        outT = sb("outT", [GW, 2, G, T])
        rsum = sb("rsum", [P, H])
        on = sb("on", [P, H, D])
        oT = sb("oT", [P, KC, T])
        res = sb("res", [P, 2, C])
        quad = sb("quad", [P, 5, 4, C])
        mx_in, mres, mout, mxn, mgate = (quad[:, i, :, :] for i in range(5))
        mcur = sb("mcur", [P, 2, KC, 4])
        fT = sb("fT", [P, KC, 4, T])
        act_a = sb("act_a", [P, 2, 512])
        hid = sb("hid", [P, FC, 512])

        raw, swapped = (left[:, m, :, :].rearrange("p (c s) t -> p c s t", c=KC) for m in range(2))

        qflat = quad[:, :, :, :].rearrange("p i s n -> p (i s n)")
        mbias = qflat[0:B, 0:9 * C]
        mrow = qflat[0:B, 9 * C:13 * C].rearrange("p (i n) -> p i n", i=2)
        turned = [buf[:, 512 * i:512 * (i + 1)] for buf in (qflat[:, 13 * C:17 * C], fT[:, :, :, :].rearrange("p c s t -> p (c s t)"),
                                                            act_a[:, :, :].rearrange("p i n -> p (i n)")) for i in range(2)]
        kflat = kblk[:, :, :, :, :, :].rearrange("p e a b c d -> p (e a b c d)")
        ada = [kflat[:, 0:18 * C].rearrange("p (c n) -> p c n", c=KC),
               kflat[:, 18 * C:30 * C].rearrange("p (c n) -> p c n", c=KC)]
        raw_attn = hid[:, :, :].rearrange("p a b -> p (a b)").rearrange("p (r n) -> p r n", n=C)
        vflat = vaug[:, :, :, :, :].rearrange("p e a b c -> p (e a b c)")
        raw_w1 = prob[:, :, :, :].rearrange("p b h t -> p (b h t)")[:, 0:8 * C].rearrange("p (r n) -> p r n", n=C)
        raw_w2 = [probT[:, :, :, :].rearrange("p b h t -> p (b h t)"), left[:, :, :, :].rearrange("p b h t -> p (b h t)")]
        raw_ln = wm[:, 0:12 * C].rearrange("p (r n) -> p r n", n=C)
        lnT = wm[:, 12 * C:24 * C].rearrange("p (c n) -> p c n", c=KC)

        bank = [ctx.enter_context(nc.psum_tensor(f"bank{i}", [P, 512], F32)) for i in range(8)]
        SC, PT, OB, WB = 0, 2, 3, 5
        DOWN = (4, 3)

        s_const = sem("s_const")
        s_cond = sem("s_cond")
        s_brow = sem("s_brow")
        s_ada = [sem(f"s_ada{l}") for l in range(3)]
        s_rawln = sem("s_rawln")
        s_rawattn = sem("s_rawattn")
        s_raww1 = sem("s_raww1")
        s_raww2 = sem("s_raww2")
        s_mbias = sem("s_mbias")
        s_modst = [sem(f"s_modst{i}") for i in range(2)]
        s_w3st = [sem(f"s_w3st{i}") for i in range(len(turned))]
        s_wa = sem("s_wa")
        s_wm = sem("s_wm")
        s_x = sem("s_x")
        s_ctx = sem("s_ctx")
        s_gate = [sem("s_gate_self"), sem("s_gate_cross")]
        s_spread = [sem("s_spread_self"), sem("s_spread_cross")]
        s_xast = sem("s_xast")
        s_mx = sem("s_mx")
        s_mres = sem("s_mres")
        s_mgate = sem("s_mgate")
        s_mst = sem("s_mst")
        s_zero = sem("s_zero")
        s_half = sem("s_half")
        s_silu = sem("s_silu")
        s_condT = sem("s_condT")
        s_condTs = sem("s_condTs")
        s_bT = sem("s_bT")
        s_bTs = sem("s_bTs")
        s_grp = sem("s_grp")
        s_grpout = sem("s_grpout")
        s_mchunk = sem("s_mchunk")
        s_mchout = sem("s_mchout")
        s_mturn = sem("s_mturn")
        s_mturned = sem("s_mturned")
        s_cur = [sem("s_cur_self"), sem("s_cur_cross")]
        s_var = sem("s_var")
        s_rstd = sem("s_rstd")
        s_vare = sem("s_vare")
        s_xn = sem("s_xn")
        s_cn = sem("s_cn")
        s_work = sem("s_work")
        s_tact = sem("s_tact")
        s_tdve = sem("s_tdve")
        s_cosine = sem("s_cosine")
        s_rope = sem("s_rope")
        s_score = sem("s_score")
        s_shift = sem("s_shift")
        s_lexp = sem("s_lexp")
        s_mask = sem("s_mask")
        s_exp = sem("s_exp")
        s_negm = sem("s_negm")
        s_texp = sem("s_texp")
        s_turn = sem("s_turn")
        s_probT = sem("s_probT")
        s_val = sem("s_val")
        s_out = sem("s_out")
        s_gbias = sem("s_gbias")
        s_kept = sem("s_kept")
        s_res = sem("s_res")
        s_mxn = sem("s_mxn")
        s_mcur = sem("s_mcur")
        s_mT = sem("s_mT")
        s_mh = sem("s_mh")
        s_up = sem("s_up")
        s_upact = sem("s_upact")
        s_upmul = sem("s_upmul")
        s_down = sem("s_down")
        s_mo = sem("s_mo")
        s_link = sem("s_link")
        s_apart = sem("s_apart")
        s_apart_sp = sem("s_apart_sp")
        s_apart_pool = sem("s_apart_pool")

        STARTED = {
            "act": [s_tact, s_exp, s_texp, s_lexp, s_probT, s_out, s_mh, s_upact],
            "dve": [*s_cur, s_var, s_xn, s_cn, s_tdve, s_rope, s_shift, s_negm, s_res, s_mxn, s_mcur, s_upmul, s_mo],
            "pe": [s_work, s_score, s_turn, s_val, s_mT, s_up, s_down],
            "pool": [s_rstd, s_mask],
        }

        def ups(l):
            return 2 * FC if LAYER[l]["swiglu"] else FC

        def up0(l):
            return sum(ups(i) for i in range(l)) * QUADS

        def pair_of(l, it):
            return it + l * PAIRS

        def quad_of(l, it):
            return it + l * QUADS

        def kept(l, j, a):
            return number(is_copy, l, j, "keep", a, 0) + 1

        def wait_pair_before(engine, s, sel, l, pair, kind, a, i):
            if not isinstance(pair, int) or pair > 0:
                engine.wait_ge(s, done(number(sel, l, pair - 1, kind, a, i)))
            elif l > 0:
                engine.wait_ge(s, done(number(sel, l - 1, PAIRS - 1, kind, a, i)))

        def norms(l):
            return PAIRS * sum(is_norm(l, s) for s in STEPS)

        def vars_of(l, pair, kind, a):
            return number(is_norm, l, pair, kind, a, 0) + l * QUADS

        def vars_mlp(l, it):
            return it + (sum(norms(i) for i in range(l + 1)) + l * QUADS)

        def groups():
            out_rows = []
            for c in range(KC):
                for n in range(3):
                    out_rows.append(("ln", c, n))
            for c in range(KC):
                for n in range(4):
                    out_rows.append(("attn", c, n))
            for c in range(KC):
                for n in range(2):
                    out_rows.append(("w1", c, n))
            for f in range(0, FC, 2):
                out_rows.append(("w2", f, 0))
            return out_rows

        GROUPS = groups()
        N_LN = sum(g[0] == "ln" for g in GROUPS)

        def turned_buffer(n):
            return (n - N_LN) % len(turned)

        MCHUNKS = ([(0, 512 * n, 512) for n in range(4)] + [(0, 2048, 256)] + [(1, 512 * n, 512) for n in range(3)]
                   + [(2, 512 * n, 512) for n in range(3)] + [(3, 512 * n, 512) for n in range(3)])

        w_of = [
            dict(qkv="L0_xcond_w_qkv", so="L0_xcond_w_so", q="L0_xcond_w_q", kv="L0_xcond_w_kv", co="L0_xcond_w_co",
                 w1="L0_xcond_w_m1", w2="L0_xcond_w_m2", bo="L0_xcond_b_so", bco="L0_xcond_b_co", b2="L0_xcond_b_m2"),
            dict(qkv="L1_xcond_W_qkv", so="L1_xcond_W_proj", q="L1_xcond_W_qc", kv="L1_xcond_W_kvc", co="L1_xcond_W_cproj",
                 w1="L1_xcond_W_mlp1", w2="L1_xcond_W_mlp2", bo="L1_xcond_b_proj", bco="L1_xcond_b_cproj",
                 b2="L1_xcond_b_mlp2"),
            dict(qkv="L2_xcond_qkv_w", so="L2_xcond_sa_proj_w", q="L2_xcond_q_w", kv="L2_xcond_kv_w", co="L2_xcond_ca_proj_w",
                 w1="L2_xcond_fc1_w", w2="L2_xcond_fc2_w", bo="L2_xcond_sa_proj_b", bco="L2_xcond_ca_proj_b",
                 b2="L2_xcond_fc2_b"),
        ]
        WA_N = [7, 7, 7, 1]
        WM_N = [3, 3, 3, 3]

        def rows(ap):
            return ap.rearrange("(c p) n -> p c n", p=P)

        block = ctx.enter_context(nc.Block())

        @block.sync
        def _(sp):
            def load_attn_weights(l):
                if l == 3:
                    sp.dma_start(wa[:, :, :], rows(wa3_dram)).then_inc(s_wa, 16)
                    return
                w = w_of[l]
                for name, at, n in (("qkv", W_Q, 3 * C), ("so", W_SO, C), ("q", W_XQ, C), ("kv", W_XK, 2 * C),
                                    ("co", W_XO, C)):
                    sp.dma_start(wa[:, :, at:at + n], rows(dram[w[name]])).then_inc(s_wa, 16)
                for a, name in enumerate(("bo", "bco")):
                    sp.dma_start(bo[:, a, :], dram[w[name]].partition_broadcast(P)).then_inc(s_wa, 16)

            def load_mlp_weights(l):
                n = HID * 2 if LAYER[l]["swiglu"] else HID
                w1 = w13_dram if l == 3 else dram[w_of[l]["w1"]]
                w2 = w23_dram if l == 3 else dram[w_of[l]["w2"]]
                b2 = dram["L3_xcond_ffn_b2"] if l == 3 else dram[w_of[l]["b2"]]
                sp.dma_start(wm[:, 0:KC * n].rearrange("p (c n) -> p c n", c=KC), rows(w1)).then_inc(s_wm, 16)
                sp.dma_start(wm[:, 4096:6144].rearrange("p (c n) -> p c n", c=FC), rows(w2)).then_inc(s_wm, 16)
                sp.dma_start(bm[:, :], b2.partition_broadcast(P)).then_inc(s_wm, 16)

            sp.sem_inc(s_xast, 16)
            sp.sem_inc(s_mst, 16)

            sp.dma_start(const[:, :], dram["tables"]).then_inc(s_const, 16)
            sp.dma_start(cond[:, 0, :], dram["cond_1024"]).then_inc(s_cond, 16)
            sp.dma_start(ada[0][:, :, 0:9 * C], rows(dram["L0_xcond_w_ada"])).then_inc(s_ada[0], 16)
            sp.dma_start(mbias[:, 0:9 * C], dram["L0_xcond_b_ada"].partition_broadcast(B)).then_inc(s_mbias, 16)
            sp.dma_start(raw_ln[:, 0:4, :], dram["L3_xcond_ln1_w"].rearrange("(r p) n -> p r n", p=P)).then_inc(s_rawln, 16)
            sp.dma_start(raw_ln[:, 4:8, :], dram["L3_xcond_ln2_w"].rearrange("(r p) n -> p r n", p=P)).then_inc(s_rawln, 16)
            sp.dma_start(raw_ln[:, 8:12, :], dram["L3_xcond_ln3_w"].rearrange("(r p) n -> p r n", p=P)).then_inc(s_rawln, 16)
            r = 0
            for name in ("L0_xcond_b_qkv", "L0_xcond_b_q", "L0_xcond_b_kv", "L0_xcond_b_m1",
                         "L1_xcond_b_qkv", "L1_xcond_b_qc", "L1_xcond_b_kvc", "L1_xcond_b_mlp1",
                         "L2_xcond_qkv_b", "L2_xcond_q_b", "L2_xcond_kv_b", "L2_xcond_fc1_b", "L3_xcond_ffn_b1"):
                n = dram[name].shape[0] // P
                sp.dma_start(brows[r:r + n, :], dram[name].rearrange("(r p) -> r p", p=P)).then_inc(s_brow, 16)
                r += n
            sp.dma_start(ada[1], rows(dram["L1_xcond_W_mod"])).then_inc(s_ada[1], 16)
            r = 0
            for name in ("qkv_w", "sa_out_w", "q_w", "k_w", "v_w", "ca_out_w"):
                src = dram["L3_xcond_" + name]
                n = src.shape[0] // P
                sp.dma_start(raw_attn[:, r:r + n, :], src.rearrange("(r p) n -> p r n", p=P)).then_inc(s_rawattn, 16)
                r += n
            sp.dma_start(raw_w1, dram["L3_xcond_ffn_w1"].rearrange("(r p) n -> p r n", p=P)).then_inc(s_raww1, 16)
            for r in range(2):
                sp.dma_start(raw_w2[r], dram["L3_xcond_ffn_w2"][r * P:(r + 1) * P, :]).then_inc(s_raww2, 16)
            load_attn_weights(0)

            stored_w = [0] * len(turned)
            for n, (l, at, w) in enumerate(MCHUNKS):
                sp.wait_ge(s_mchout, n + 1)
                sp.dma_start(mods_dram[:, MOD0[l] * C + at:MOD0[l] * C + at + w], mrow[:, n % 2, 0:w]).then_inc(s_modst[n % 2], 16)
                last = n + 1 < len(MCHUNKS) and MCHUNKS[n + 1][0] != l
                if last and l == 0:
                    sp.dma_start(ada[0][:, :, 0:6 * C], rows(dram["L2_xcond_adaln_w"])).then_inc(s_ada[2], 16)
                    sp.dma_start(mbias[:, 0:6 * C], dram["L1_xcond_b_mod"].partition_broadcast(B)).then_inc(s_mbias, 16)
                if last and l == 1:
                    sp.dma_start(mbias[:, 0:6 * C], dram["L2_xcond_adaln_b"].partition_broadcast(B)).then_inc(s_mbias, 16)
                if last and l == 2:
                    for i in range(3):
                        sp.dma_start(mbias[:, 2 * C * i:2 * C * (i + 1)],
                                     dram[f"L3_xcond_ln{i + 1}_b"].partition_broadcast(B)).then_inc(s_mbias, 16)
            for n, (kind, c, j) in enumerate(GROUPS):
                if kind == "ln":
                    continue
                sp.wait_ge(s_grpout, n + 1)
                src = turned[turned_buffer(n)]
                if kind == "attn":
                    dst = wa3_dram[c * P:(c + 1) * P, 512 * j:512 * (j + 1)]
                elif kind == "w1":
                    dst = w13_dram[c * P:(c + 1) * P, 512 * j:512 * (j + 1)]
                else:
                    dst = w23_dram[c * P:(c + 2) * P, :].rearrange("(f p) n -> p f n", p=P)
                    src = src.rearrange("p (f n) -> p f n", f=2)
                sp.dma_start(dst, src).then_inc(s_w3st[turned_buffer(n)], 16)
                stored_w[turned_buffer(n)] += 1
            for i in range(2):
                sp.wait_ge(s_modst[i], 16 * (len(MCHUNKS) // 2))
            for i in range(len(turned)):
                sp.wait_ge(s_w3st[i], 16 * stored_w[i])

            def pair(x):
                return x.rearrange("b t n -> t b n")

            def apart():
                sp.sem_inc(s_apart_sp, 1)

            def load_x(l, j):
                wait_pair_before(sp, s_xn, is_token_norm, l, j, "norm", SELF, 0)
                apart()
                if not isinstance(j, int) or j > 0:
                    sp.wait_ge(s_kept, kept(l, j - 1, SELF))
                elif l > 0:
                    sp.wait_ge(s_kept, kept(l - 1, PAIRS - 1, SELF))
                apart()
                sp.dma_start(xin[:, :, :], pair(x_src[l][bass.ds(j * 2, 2), :, :])).then_inc(s_x, 16)

            def load_ctx(l, j):
                wait_pair_before(sp, s_work, is_use, l, j, "ctx_turn", CROSS, 0)
                if LAYER[l]["ctx_norm"]:
                    apart()
                    sp.wait_ge(s_cn, freed(j, 1))
                apart()
                sp.dma_start(cin[:, :, :], pair(dram["ctx_1024"][bass.ds(j * 2, 2), :, :])).then_inc(s_ctx, 16)

            def load_gate(l, j, a):
                mod = LAYER[l]["self_gate" if a == SELF else "cross_gate"]
                if mod is None:
                    return
                wait_pair_before(sp, s_res, is_taken_by("res"), l, j, "out_proj", a, 1)
                apart()
                at = (MOD0[l] + mod) * C
                sp.dma_start(gate[:, a, :, :], mods_dram[bass.ds(j * 2, 2), at:at + C].partition_broadcast(P))\
                    .then_inc(s_gate[a], 16)

            def spread(l, j, a):
                if LAYER[l]["rope"]:
                    sp.wait_ge(s_rope, done(number(is_rotated, l, j, "k", a, 0)))
                else:
                    sp.wait_ge(s_tact, done(number(is_taken_by("act"), l, j, "k", a, 0)))
                for h in range(P // D):
                    sp.dma_start(kblk[D * h:D * (h + 1), a, :, :, h, :].rearrange("p c s t -> p (c s) t"),
                                 kT[D * h:D * (h + 1), a, :, :, :].rearrange("p c s t -> p (c s) t")).then_inc(s_spread[a], 16)

            def attention_step(l, j):
                def has(off):
                    return not isinstance(j, int) or 0 <= j + off < PAIRS
                if has(1):
                    load_ctx(l, j + 1)
                if has(0):
                    spread(l, j, CROSS)
                if has(1):
                    load_gate(l, j + 1, SELF)
                if has(2) and has(1):
                    load_x(l, j + 2)
                if has(-1):
                    sp.wait_ge(s_res, done(number(is_taken_by("res"), l, j - 1, "out_proj", CROSS, 1)))
                    apart()
                    sp.dma_start(pair(xa_dram[l][bass.ds((j - 1) * 2, 2), :, :]), x2[:, :, :]).then_inc(s_xast, 16)
                if has(0):
                    load_gate(l, j, CROSS)
                if has(2):
                    spread(l, j + 2, SELF)

            def load_quad_x(l, it):
                sp.wait_ge(s_mxn, freed(quad_of(l, it), 1))
                sp.dma_start(mx_in[:, :, :], pair(xa_dram[l][bass.ds(it * 4, 4), :, :])).then_inc(s_mx, 16)

            def load_quad_res(l, it):
                sp.wait_ge(s_mo, freed(quad_of(l, it) * 4 + 3, 4))
                sp.dma_start(mres[:, :, :], pair(xa_dram[l][bass.ds(it * 4, 4), :, :])).then_inc(s_mres, 16)
                if LAYER[l]["mlp_gate"] is not None:
                    at = (MOD0[l] + LAYER[l]["mlp_gate"]) * C
                    sp.dma_start(mgate[:, :, :], mods_dram[bass.ds(it * 4, 4), at:at + C].partition_broadcast(P))\
                        .then_inc(s_mgate, 16)

            def mlp_step(l, it, last):
                load_quad_res(l, it)
                if not last:
                    load_quad_x(l, it + 1)
                elif l + 1 < LAYERS:
                    sp.wait_ge(s_mst, 16 * (QUADS * l + 2))
                    load_x(l + 1, 0)
                    attention_step(l + 1, FIRST)
                sp.wait_ge(s_mo, done(quad_of(l, it) * 4 + 3))
                sp.dma_start(pair(xm_dram[l][bass.ds(it * 4, 4), :, :]), mout[:, :, :]).then_inc(s_mst, 16)

            load_x(0, 0)
            sp.wait_ge(s_mchunk, len(MCHUNKS))
            load_mlp_weights(0)
            attention_step(0, FIRST)
            for l in range(LAYERS):
                if l > 0:
                    sp.wait_ge(s_mst, 16 * (QUADS * l + 1))
                    sp.wait_ge(s_down, done(4 * QUADS * l - 1))
                for j in (-1, 0):
                    attention_step(l, j)
                    if j < 0 and l > 0:
                        load_mlp_weights(l)
                with sp.Fori(1, PAIRS - 2) as j:
                    attention_step(l, j)
                attention_step(l, PAIRS - 2)
                sp.wait_ge(s_xast, 16 * (PAIRS * l + 3))
                load_quad_x(l, 0)
                for j in (PAIRS - 1, PAIRS):
                    attention_step(l, j)
                sp.wait_ge(s_xast, 16 * (PAIRS * (l + 1) + 1))
                if l + 1 < LAYERS:
                    load_attn_weights(l + 1)
                with sp.Fori(0, QUADS - 1) as it:
                    mlp_step(l, it, False)
                mlp_step(l, QUADS - 1, True)
            sp.wait_ge(s_mst, 16 * (QUADS * LAYERS + 1))

        @block.gpsimd
        def _(pool):
            for s in STARTED["pool"]:
                pool.sem_inc(s, START)
            nc.gpsimd.memset(vflat[:, :], 0.0).then_inc(s_zero, 1)
            pool.wait_ge(s_zero, 1)
            for a in range(2):
                for s in range(2):
                    for g in range(G):
                        ones = vaug[:, a, s, g, :].rearrange("p (h x) -> p h x", h=HG)[:, :, D:D + 1]
                        ins = nc.gpsimd.memset(ones, 1.0)
            ins.then_inc(s_zero, 1)
            chunks_of = [sum(m[0] == l for m in MCHUNKS) for l in range(3)]
            pool.wait_ge(s_mchunk, sum(chunks_of[0:2]))
            nc.gpsimd.memset(kflat[:, 15 * C:32 * C], 0.0).then_inc(s_zero, 1)
            pool.wait_ge(s_mchunk, sum(chunks_of))
            nc.gpsimd.memset(kflat[:, 0:15 * C], 0.0).then_inc(s_zero, 1)
            nc.gpsimd.memset(neghalf[:, :], -0.5).then_inc(s_half, 1)
            pool.wait_ge(s_half, 1)
            pool.wait_ge(s_const, 16)

            def one(k, n, l):
                pool.wait_ge(s_var, done(k))
                e = eps[:, EPS_COL[l]:EPS_COL[l] + 1].to_broadcast([P, n])
                nc.gpsimd.tensor_tensor(vare[:, 0:n], mv[:, 0:n, 1], e, ALU.add).then_inc(s_vare, 1)
                pool.wait_ge(s_vare, k + 1)
                nc.gpsimd.tensor_tensor(rstd[:, 0:n], vare[:, 0:n], neghalf[:, 0:n], ALU.pow).then_inc(s_rstd, 1)

            def attention_step(l, it):
                cfg = LAYER[l]
                for kind, a, i, off in steps_of(it):
                    j = it + off
                    if kind == "stats":
                        one(vars_of(l, j, "norm", a), 2, l)
                    elif kind == "stats_ctx" and cfg["ctx_norm"]:
                        one(vars_of(l, j, "norm_ctx", a), 2, l)
                    elif is_rotated(l, (kind, a, i, off)):
                        pool.wait_ge(s_tact, done(number(is_taken_by("act"), l, j, kind, a, i)))
                        dst = (qT if kind == "q" else kT)[:, a, :, :, :].rearrange("p c s t -> p (c s) t")
                        nc.gpsimd.tensor_tensor(dst, raw[:, :, :, :].rearrange("p c s t -> p (c s) t"),
                                                rope_cos.unsqueeze(1).to_broadcast([P, 4, T]), ALU.mult).then_inc(s_cosine, 1)
                    elif kind == "keep":
                        src, dst = (xin, xself) if a == SELF else (x1, x1cross)
                        if a == SELF:
                            pool.wait_ge(s_x, (pair_of(l, j) + 1) * 16)
                        if a == SELF or not isinstance(j, int) or j > 0:
                            wait_pair_before(pool, s_res, is_taken_by("res"), l, j, "out_proj", a, 1)
                        else:
                            pool.wait_ge(s_res, done(number(is_taken_by("res"), l, j, "out_proj", SELF, 1)))
                        if not cfg["bias"]:
                            pool.sem_inc(s_apart_pool, 1)
                            nc.gpsimd.tensor_copy(dst[:, :, :], src[:, :, :]).then_inc(s_kept, 1)
                            continue
                        bias = bo[:, a, :].unsqueeze(1).to_broadcast([P, 2, C])
                        if is_gated_copy(l, (kind, a, i, off)):
                            gates_before = sum(PAIRS * is_gated_copy(m, (kind, a, i, off)) for m in range(l))
                            pool.wait_ge(s_gate[a], (j + (gates_before + 1)) * 16)
                            nc.gpsimd.tensor_tensor(dst[:, :, :], gate[:, a, :, :], bias, ALU.mult).then_inc(s_gbias, 1)
                            pool.wait_ge(s_gbias, number(is_gated_copy, l, j, kind, a, i) + 1)
                            bias = dst[:, :, :]
                        nc.gpsimd.tensor_tensor(dst[:, :, :], src[:, :, :], bias, ALU.add).then_inc(s_kept, 1)
                    elif kind == "mark" and cfg["topk"]:
                        t = number(is_topk_chunk, l, j, "scores", a, i)
                        pool.wait_ge(s_lexp, done(t))
                        p = prob[:, slot(4, l, j, a, i), :, :].rearrange("p h t -> p (h t)")
                        rest = left[:, topk_slot(l, j, a, i), :, :].rearrange("p h t -> p (h t)")
                        nc.gpsimd.tensor_tensor(p, p, rest, ALU.subtract).then_inc(s_mask, 1)

            for l in range(LAYERS):
                attention_step(l, FIRST)
                pool.wait_ge(s_wa, 16 * sum(WA_N[:l + 1]))
                for j in (-1, 0):
                    attention_step(l, j)
                with pool.Fori(1, PAIRS - 2) as j:
                    attention_step(l, j)
                for j in (PAIRS - 2, PAIRS - 1):
                    attention_step(l, j)
                first = vars_mlp(l, 0)
                one(first, 4, l)
                attention_step(l, PAIRS)
                with pool.Fori(1, QUADS) as it:
                    one(it + first, 4, l)

        @block.scalar
        def _(act):
            for s in STARTED["act"]:
                act.sem_inc(s, START)
            act.wait_ge(s_cond, 16)
            nc.scalar.activation(cond[:, 1, :], cond[:, 0, :], ACT.Silu).then_inc(s_silu, 1)
            act.wait_ge(s_condT, 1)
            nc.scalar.activation(condT[:, :, :, :].rearrange("p a c b -> p (a c b)"), bank[0][:, 0:4 * B], ACT.Copy)\
                .then_inc(s_condTs, 1)
            blk = 0
            for n, (l, at, w) in enumerate(MCHUNKS):
                act.wait_ge(s_mturn, n + 1)
                k = w // P
                nc.scalar.activation(modT[:, blk:blk + k, :].rearrange("p k b -> p (k b)"),
                                     bank[4 + n % 2][:, 0:k * B], ACT.Copy).then_inc(s_mturned, 1)
                blk += k

            def take(l, j, kind, a, i):
                act.wait_ge(s_work, done(number(is_use, l, j, kind, a, i)))
                return bank[WB + work_bank(kind, a, i)]

            def attention_step(l, it):
                cfg = LAYER[l]
                for kind, a, i, off in steps_of(it):
                    j = it + off
                    if kind == "x_turn":
                        src = take(l, j, kind, a, i)
                        mod = cfg["self_mod"] if a == SELF else cfg["cross_mod"]
                        if mod is None:
                            nc.scalar.activation(hT[:, :, :, :].rearrange("p c s t -> p (c s t)"), src[:, :], ACT.Copy)\
                                .then_inc(s_tact, 1)
                        else:
                            layers_before = sum(LAYER[m]["self_mod" if a == SELF else "cross_mod"] is not None for m in range(l))
                            act.wait_ge(s_cur[a], done(j + PAIRS * layers_before))
                            for c in range(KC):
                                for s in range(2):
                                    ins = nc.scalar.activation(
                                        hT[:, c, s, :], src[:, (2 * c + s) * T:(2 * c + s + 1) * T], ACT.Identity,
                                        bias=cur[:, a, 0, c, s:s + 1], scale=cur[:, a, 1, c, s:s + 1])
                            ins.then_inc(s_tact, 1)
                    elif kind == "ctx_turn":
                        src = take(l, j, kind, a, i)
                        nc.scalar.activation(cT[:, :, :, :].rearrange("p c s t -> p (c s t)"), src[:, :], ACT.Copy)\
                            .then_inc(s_tact, 1)
                    elif kind in ("q", "k"):
                        src = take(l, j, kind, a, i)
                        if cfg["rope"]:
                            act.wait_ge(s_rope, freed(number(is_rotated, l, j, kind, a, i), 1))
                            nc.scalar.activation(raw[:, :, :, :].rearrange("p c s t -> p (c s t)"), src[:, :], ACT.Copy)\
                                .then_inc(s_tact, 1)
                            continue
                        dst = qT if kind == "q" else kT
                        b0 = BROW[l] + {("q", SELF): B_Q, ("k", SELF): B_K, ("q", CROSS): B_XQ, ("k", CROSS): B_XK}[kind, a]
                        for c in range(KC):
                            ins = nc.scalar.activation(
                                dst[:, a, c, :, :].rearrange("p s t -> p (s t)"), src[:, c * 2 * T:(c + 1) * 2 * T],
                                ACT.Identity, bias=biasT[:, b0 + c:b0 + c + 1])
                        ins.then_inc(s_tact, 1)
                    elif kind == "exp":
                        k = number(is_chunk, l, j, "scores", a, i)
                        if cfg["topk"] and a == CROSS:
                            t = number(is_topk_chunk, l, j, "scores", a, i)
                            act.wait_ge(s_negm, done(t))
                            act.wait_ge(s_turn, freed(k, 4))
                            b, pb, m = slot(2, l, j, a, i), slot(4, l, j, a, i), topk_slot(l, j, a, i)
                            for h in range(HG):
                                ins = nc.scalar.activation(prob[:, pb, h, :], bank[SC + b][:, h * T:(h + 1) * T],
                                                           ACT.Exp, bias=negm[:, m, h:h + 1], scale=D ** -0.5)
                            ins.then_inc(s_texp, 1)
                        else:
                            act.wait_ge(s_shift, done(k))
                            p = prob[:, slot(4, l, j, a, i), :, :].rearrange("p h t -> p (h t)")
                            nc.scalar.activation(p, p, ACT.Exp, scale=D ** -0.5).then_inc(s_exp, 1)
                    elif kind == "mark" and cfg["topk"]:
                        act.wait_ge(s_shift, done(number(is_chunk, l, j, "scores", a, i)))
                        m = topk_slot(l, j, a, i)
                        for h in range(HG):
                            ins = nc.scalar.activation(left[:, m, h, :], left[:, m, h, :], ACT.Exp, bias=negm[:, m, h:h + 1],
                                                       scale=D ** -0.5)
                        ins.then_inc(s_lexp, 1)
                    elif kind == "turn":
                        k = number(is_chunk, l, j, "scores", a, i)
                        act.wait_ge(s_turn, done(k))
                        act.wait_ge(s_val, freed(number(is_values, l, j, "values", a, i), 2))
                        b = slot(2, l, j, a, i)
                        nc.scalar.activation(probT[:, b, :, :].rearrange("p h t -> p (h t)"), bank[PT][:, :],
                                             ACT.Copy).then_inc(s_probT, 1)
                    elif kind == "values" and i % G == G - 1:
                        act.wait_ge(s_val, done(number(is_values, l, j, kind, a, i)))
                        nc.scalar.activation(outT[:, a, :, :].rearrange("p g t -> p (g t)"), bank[OB + a][0:GW, :], ACT.Copy)\
                            .then_inc(s_out, 1)
                    elif kind == "out_back":
                        src = take(l, j, kind, a, i)
                        if cfg["bias"]:
                            b0 = BROW[l] + (B_V if a == SELF else B_XV)
                            for c in range(KC):
                                ins = nc.scalar.activation(oT[:, c, :], src[:, c * T:(c + 1) * T], ACT.Identity,
                                                           bias=biasT[:, b0 + c:b0 + c + 1])
                        else:
                            ins = nc.scalar.activation(oT[:, :, :].rearrange("p c t -> p (c t)"), src[:, 0:KC * T], ACT.Copy)
                        ins.then_inc(s_tact, 1)

            def modulate(l, it):
                m = quad_of(l, it)
                act.wait_ge(s_mcur, done(m))
                for c in range(KC):
                    act.wait_ge(s_mT, done(m * KC + c))
                    for s in range(4):
                        ins = nc.scalar.activation(fT[:, c, s, :], bank[6 + c][:, s * T:(s + 1) * T], ACT.Identity,
                                                   bias=mcur[:, 0, c, s:s + 1], scale=mcur[:, 1, c, s:s + 1])
                ins.then_inc(s_mh, 1)

            def mlp_step(l, it, last):
                cfg = LAYER[l]
                b0 = BROW[l] + (B_F if l < 3 else 0)
                for f in range(FC):
                    if cfg["swiglu"]:
                        act.wait_ge(s_up, done(it * ups(l) + (up0(l) + 2 * f)))
                        act.wait_ge(s_upmul, freed(it * FC + f, 2))
                        nc.scalar.activation(act_a[:, f % 2, :], bank[2 * (f % 2)][:, :], cfg["act"],
                                             bias=biasT[:, b0 + f:b0 + f + 1]).then_inc(s_upact, 1)
                    else:
                        act.wait_ge(s_up, done(it * ups(l) + (up0(l) + f)))
                        nc.scalar.activation(hid[:, f, :], bank[f % 4][:, :], cfg["act"],
                                             bias=biasT[:, b0 + f:b0 + f + 1]).then_inc(s_upact, 1)
                if not last:
                    modulate(l, it + 1)

            act.wait_ge(s_bTs, 1)
            for l in range(LAYERS):
                attention_step(l, FIRST)
                nc.scalar.preload_act_table(ACT.Exp)
                for j in (-1, 0):
                    attention_step(l, j)
                with act.Fori(1, PAIRS - 2) as j:
                    attention_step(l, j)
                for j in (PAIRS - 2, PAIRS - 1, PAIRS):
                    attention_step(l, j)
                modulate(l, 0)
                nc.scalar.preload_act_table(LAYER[l]["act"])
                with act.Fori(0, QUADS - 1) as it:
                    mlp_step(l, it, False)
                mlp_step(l, QUADS - 1, True)

        @block.vector
        def _(dve):
            for s in STARTED["dve"]:
                dve.sem_inc(s, START)
            chain = dict(base=0, per=0, n=0, it=0)

            def link(ins):
                chain["n"] += 1
                ins.then_inc(s_link, 1)
                dve.wait_ge(s_link, chain["it"] * chain["per"] + (chain["base"] + chain["n"]))

            def enter(it, per):
                chain.update(it=it, per=per, n=0)

            def settle():
                chain.update(base=chain["base"] + chain["n"], n=0)

            def leave(times):
                assert chain["n"] == chain["per"], chain
                chain.update(base=chain["base"] + times * chain["per"], n=0, it=0, per=0)

            dve.wait_ge(s_bT, 1)
            nc.vector.tensor_copy(biasT[:, :], bank[1][:, 0:NBROW]).then_inc(s_bTs, 1)

            def group_out(n):
                kind, c, j = GROUPS[n]
                dve.wait_ge(s_grp, n + 1)
                if kind == "ln":
                    dst = lnT[:, c, 512 * j:512 * (j + 1)]
                else:
                    b = turned_buffer(n)
                    if n >= N_LN + len(turned):
                        dve.wait_ge(s_w3st[b], 16 * ((n - N_LN) // len(turned)))
                    dst = turned[b]
                nc.vector.tensor_copy(dst, bank[6 + n % 2][:, :]).then_inc(s_grpout, 1)

            def chunk_out(n):
                l, at, w = MCHUNKS[n]
                dve.wait_ge(s_mchunk, n + 1)
                dve.wait_ge(s_mbias, 16 * (l + 1 if l < 3 else 6))
                if n >= 2:
                    dve.wait_ge(s_modst[n % 2], 16 * (n // 2))
                    dve.wait_ge(s_mturn, n - 1)
                nc.vector.tensor_tensor(mrow[:, n % 2, 0:w], bank[2 + n % 2][0:B, 0:w], mbias[:, at:at + w], ALU.add)\
                    .then_inc(s_mchout, 1)

            for n in range(6):
                group_out(n)
            for n in range(len(MCHUNKS)):
                chunk_out(n)
            for n in range(6, len(GROUPS)):
                group_out(n)
            dve.wait_ge(s_mturned, len(MCHUNKS))

            def apart():
                dve.sem_inc(s_apart, 1)

            def statistics(k, x, n):
                apart()
                for s in range(n):
                    ins = nc.vector.bn_stats(stats[:, s, :], x[:, s, :])
                link(ins)
                apart()
                for s in range(n):
                    ins = nc.vector.bn_aggr(mv[:, s, :], stats[:, s, :])
                ins.then_inc(s_var, 1)

            def normalise(k, x, dst, n):
                dve.wait_ge(s_var, done(k))
                dve.wait_ge(s_rstd, done(k))
                for s in range(n):
                    ins = nc.vector.tensor_scalar(dst[:, s, :], x[:, s, :], mv[:, s, 0:1], rstd[:, s:s + 1],
                                                  ALU.subtract, ALU.mult)
                return ins

            def take(l, j, kind, a, i):
                dve.wait_ge(s_work, done(number(is_use, l, j, kind, a, i)))
                return bank[WB + work_bank(kind, a, i)]

            def fetch_mods(l, it, dst, mod, n):
                sh, sc = (2 * (MOD0[l] + m) for m in mod)
                nc.vector.tensor_copy(dst[:, 0, :, :], modT[:, sh:sh + 2, bass.ds(it * n, n)])
                return nc.vector.tensor_scalar(dst[:, 1, :, :], modT[:, sc:sc + 2, bass.ds(it * n, n)], 1.0, None, ALU.add)

            def residual(src, bias, g, x, dst, i):
                r = res[:, i % 2, :]
                if bias is not None:
                    link(nc.vector.tensor_tensor(r, src, bias, ALU.add))
                    src = r
                if g is not None:
                    link(nc.vector.tensor_tensor(r, src, g, ALU.mult))
                    src = r
                return nc.vector.tensor_tensor(dst, src, x, ALU.add)

            def rotate(l, j, kind, a, i):
                sin = rope_sin.unsqueeze(1).to_broadcast([P, 4, T])
                dst = (qT if kind == "q" else kT)[:, a, :, :, :].rearrange("p c s t -> p (c s) t")
                v = raw[:, :, :, :].rearrange("p c s t -> p (c s) t")
                w = swapped[:, :, :, :].rearrange("p c s t -> p (c s) t")
                dve.wait_ge(s_tact, done(number(is_taken_by("act"), l, j, kind, a, i)))
                apart()
                link(nc.vector.stream_shuffle(w, v, [(p // D) * D + (p + D // 2) % D for p in range(32)]))
                link(nc.vector.tensor_tensor(w, w, sin, ALU.mult))
                dve.wait_ge(s_cosine, number(is_rotated, l, j, kind, a, i) + 1)
                nc.vector.tensor_tensor(dst, dst, w, ALU.add).then_inc(s_rope, 1)

            def top_k(l, j, a, i):
                t = number(is_topk_chunk, l, j, "scores", a, i)
                sc, m = bank[SC + slot(2, l, j, a, i)], topk_slot(l, j, a, i)
                dve.wait_ge(s_mask, freed(t, 2))
                apart()
                for h in range(HG):
                    ins = nc.vector.max(top[:, 0, h, :], sc[:, h * T:(h + 1) * T])
                link(ins)
                nc.vector.tensor_scalar(negm[:, m, :], top[:, 0, :, 0], -(D ** -0.5), None, ALU.mult)
                for h in range(HG):
                    ins = nc.vector.match_replace(left[:, m, h, :], top[:, 0, h, :], sc[:, h * T:(h + 1) * T], NEG)
                ins.then_inc(s_negm, 1)

            def top_k_rest(l, j, a, i):
                m = topk_slot(l, j, a, i)
                dve.wait_ge(s_negm, done(number(is_topk_chunk, l, j, "scores", a, i)))
                apart()
                for h in range(HG):
                    ins = nc.vector.max(top[:, 1, h, :], left[:, m, h, :])
                link(ins)
                apart()
                for h in range(HG):
                    ins = nc.vector.match_replace(left[:, m, h, :], top[:, 1, h, :], left[:, m, h, :], NEG)
                ins.then_inc(s_shift, 1)
                dve.wait_ge(s_shift, done(number(is_chunk, l, j, "scores", a, i)))

            def attention_step(l, it):
                cfg = LAYER[l]
                for kind, a, i, off in steps_of(it):
                    j = it + off
                    if kind == "stats":
                        if a == SELF:
                            dve.wait_ge(s_x, (pair_of(l, j) + 1) * 16)
                        else:
                            dve.wait_ge(s_res, done(number(is_taken_by("res"), l, j, "out_proj", SELF, 1)))
                        statistics(vars_of(l, j, "norm", a), xin if a == SELF else x1, 2)
                    elif kind == "norm":
                        mod = cfg["self_mod"] if a == SELF else cfg["cross_mod"]
                        if a == SELF:
                            wait_pair_before(dve, s_tact, is_taken_by("act"), l, j, "x_turn", SELF, 0)
                            wait_pair_before(dve, s_work, is_use, l, j, "x_turn", SELF, 0)
                        else:
                            wait_pair_before(dve, s_score, is_chunk, l, j, "scores", CROSS, 0)
                        if mod is not None:
                            fetch_mods(l, j, cur[:, a, :, :, :], mod, 2).then_inc(s_cur[a], 1)
                        normalise(vars_of(l, j, kind, a), xin if a == SELF else x1, xn[:, a, :, :], 2).then_inc(s_xn, 1)
                    elif kind == "stats_ctx" and cfg["ctx_norm"]:
                        dve.wait_ge(s_ctx, (pair_of(l, j) + 1) * 16)
                        statistics(vars_of(l, j, "norm_ctx", a), cin, 2)
                    elif kind == "norm_ctx" and cfg["ctx_norm"]:
                        wait_pair_before(dve, s_work, is_use, l, j, "ctx_turn", CROSS, 0)
                        normalise(vars_of(l, j, kind, a), cin, cn, 2).then_inc(s_cn, 1)
                    elif kind in ("rotate_q", "rotate_k") and cfg["rope"]:
                        rotate(l, j, kind[-1], a, i)
                    elif kind == "v":
                        src = take(l, j, kind, a, i)
                        for s in range(2):
                            ins = nc.vector.tensor_copy(
                                vaug[:, a, s, :, :].rearrange("p g (h x) -> p g h x", h=HG)[:, :, :, 0:D],
                                src[:, s * C:(s + 1) * C].rearrange("p (g h d) -> p g h d", g=G, h=HG))
                        ins.then_inc(s_tdve, 1)
                    elif kind == "scores":
                        k = number(is_chunk, l, j, kind, a, i)
                        dve.wait_ge(s_score, done(k))
                        if cfg["topk"] and a == CROSS:
                            top_k(l, j, a, i)
                            continue
                        b = slot(2, l, j, a, i)
                        sc = bank[SC + b][:, :].rearrange("p (h t) -> p h t", h=HG)
                        link(nc.vector.tensor_reduce(mx[:, b, :], sc, AX.X, ALU.max))
                        dve.wait_ge(s_turn, freed(k, 4))
                        nc.vector.tensor_tensor(prob[:, slot(4, l, j, a, i), :, :], sc,
                                                mx[:, b, :].unsqueeze(2).to_broadcast([P, HG, T]),
                                                ALU.subtract).then_inc(s_shift, 1)
                    elif kind == "rest" and is_topk_chunk(l, ("scores", a, i, off)):
                        top_k_rest(l, j, a, i)
                    elif kind == "out_turn":
                        src = take(l, j, kind, a, i)[:, 0:G * GW].rearrange("p (h x) -> p h x", x=DA)
                        link(nc.vector.reciprocal(rsum[:, :], src[:, :, D]))
                        nc.vector.tensor_tensor(on[:, :, :], src[:, :, 0:D], rsum[:, :].unsqueeze(2).to_broadcast([P, H, D]),
                                                ALU.mult).then_inc(s_tdve, 1)
                    elif kind == "out_proj":
                        src = take(l, j, kind, a, i)[:, 0:C]
                        gt = cfg["self_gate"] if a == SELF else cfg["cross_gate"]
                        if i == 0:
                            if a == CROSS:
                                dve.wait_ge(s_xast, (pair_of(l, j) + 1) * 16)
                            if a == SELF and (not isinstance(j, int) or j > 0):
                                dve.wait_ge(s_kept, kept(l, j - 1, CROSS))
                            else:
                                dve.wait_ge(s_kept, kept(l, j, a))
                        residual(src, None, gate[:, a, i, :] if gt is not None else None,
                                 (xself if a == SELF else x1cross)[:, i, :], (x1 if a == SELF else x2)[:, i, :], i)\
                            .then_inc(s_res, 1)

            def front(l, it):
                cfg = LAYER[l]
                m = quad_of(l, it)
                dve.wait_ge(s_mh, freed(m, 1))
                fetch_mods(l, it, mcur, cfg["mlp_mod"], 4).then_inc(s_mcur, 1)
                dve.wait_ge(s_mx, (m + 1) * 16)
                dve.wait_ge(s_mT, freed(m * KC + 1, KC))
                statistics(vars_mlp(l, it), mx_in, 4)
                normalise(vars_mlp(l, it), mx_in, mxn, 4).then_inc(s_mxn, 1)

            def mlp_step(l, it, last):
                cfg = LAYER[l]
                m = quad_of(l, it)
                b0 = BROW[l] + (B_F if l < 3 else 0)
                if cfg["swiglu"]:
                    for f in range(FC):
                        dve.wait_ge(s_up, done(it * ups(l) + (up0(l) + 2 * f + 1)))
                        dve.wait_ge(s_upact, done(it * FC + f))
                        nc.vector.scalar_tensor_tensor(hid[:, f, :], bank[2 * (f % 2) + 1][:, :],
                                                       biasT[:, b0 + FC + f:b0 + FC + f + 1], act_a[:, f % 2, :],
                                                       ALU.add, ALU.mult).then_inc(s_upmul, 1)
                if not last:
                    front(l, it + 1)
                elif l + 1 < LAYERS:
                    attention_step(l + 1, FIRST)
                dve.wait_ge(s_mres, (m + 1) * 16)
                if cfg["mlp_gate"] is not None:
                    dve.wait_ge(s_mgate, (m + 1) * 16)
                dve.wait_ge(s_wm, 48 * (l + 1))
                dve.wait_ge(s_mst, (m + 1) * 16)
                for s in range(4):
                    dve.wait_ge(s_down, done(m * 4 + s))
                    residual(bank[DOWN[s % 2]][:, 0:C], bm[:, :], mgate[:, s, :] if cfg["mlp_gate"] is not None else None,
                             mres[:, s, :], mout[:, s, :], s).then_inc(s_mo, 1)

            LINKS = DVE_LINKS
            attention_step(0, FIRST)
            for l in range(LAYERS):
                for j in (-1, 0):
                    attention_step(l, j)
                settle()
                with dve.Fori(0, PAIRS - 3) as it:
                    enter(it, LINKS[l][0])
                    attention_step(l, it + 1)
                leave(PAIRS - 3)
                for j in (PAIRS - 2, PAIRS - 1):
                    attention_step(l, j)
                front(l, 0)
                attention_step(l, PAIRS)
                settle()
                with dve.Fori(0, QUADS - 1) as it:
                    enter(it, LINKS[l][1])
                    mlp_step(l, it, False)
                leave(QUADS - 1)
                mlp_step(l, QUADS - 1, True)
                settle()

        @block.tensor
        def _(pe):
            for s in STARTED["pe"]:
                pe.sem_inc(s, START)
            mm, turn = nc.tensor.matmul, nc.tensor.transpose

            pe.wait_ge(s_const, 16)
            pe.wait_ge(s_silu, 1)
            for a in range(2):
                for c in range(KC):
                    ins = turn(bank[0][:, (2 * a + c) * B:(2 * a + c + 1) * B], cond[:, a, c * P:(c + 1) * P],
                               ident[0:B, 0:B])
            ins.then_inc(s_condT, 1)
            pe.wait_ge(s_brow, 16 * 13)
            turn(bank[1][:, 0:NBROW], brows[:, :], ident[0:NBROW, 0:NBROW]).then_inc(s_bT, 1)

            def group(n):
                kind, c, j = GROUPS[n]
                if n >= 2:
                    pe.wait_ge(s_grpout, n - 1)
                dst = bank[6 + n % 2]
                if kind == "w2":
                    for f in range(2):
                        for r in range(2):
                            ins = turn(dst[:, f * C + r * P:f * C + (r + 1) * P], raw_w2[r][:, (c + f) * P:(c + f + 1) * P], ident)
                else:
                    src = {"ln": raw_ln, "attn": raw_attn, "w1": raw_w1}[kind]
                    for b in range(4):
                        ins = turn(dst[:, b * P:(b + 1) * P], src[:, 4 * j + b, c * P:(c + 1) * P], ident)
                ins.then_inc(s_grp, 1)

            pe.wait_ge(s_rawln, 48)
            for n in range(6):
                group(n)
            pe.wait_ge(s_condTs, 1)

            def mod_chunk(n):
                l, at, w = MCHUNKS[n]
                if l < 3:
                    pe.wait_ge(s_ada[l], 16)
                else:
                    pe.wait_ge(s_grpout, 6)
                if n >= 2:
                    pe.wait_ge(s_mchout, n - 1)
                src = (ada[l % 2] if l < 3 else lnT)
                for c in range(KC):
                    ins = mm(bank[2 + n % 2][0:B, 0:w], condT[:, 0 if l == 3 else 1, c, :], src[:, c, at:at + w],
                             start=c == 0, stop=c == KC - 1)
                ins.then_inc(s_mchunk, 1)

            def mod_turn(n):
                l, at, w = MCHUNKS[n]
                pe.wait_ge(s_mchout, n + 1)
                if n >= 2:
                    pe.wait_ge(s_mturned, n - 1)
                for b in range(w // P):
                    ins = turn(bank[4 + n % 2][:, b * B:(b + 1) * B], mrow[:, n % 2, b * P:(b + 1) * P], ident[0:B, 0:B])
                ins.then_inc(s_mturn, 1)

            for n in range(len(MCHUNKS)):
                mod_chunk(n)
                if n >= 2:
                    mod_turn(n - 2)
            for n in (2, 1):
                mod_turn(len(MCHUNKS) - n)
            pe.wait_ge(s_rawattn, 96)
            pe.wait_ge(s_raww1, 16)
            pe.wait_ge(s_raww2, 32)
            for n in range(6, len(GROUPS)):
                group(n)
            pe.wait_ge(s_bTs, 1)
            pe.wait_ge(s_grpout, len(GROUPS))
            pe.wait_ge(s_mturned, len(MCHUNKS))
            pe.wait_ge(s_zero, 4)

            def attention_step(l, it):
                cfg = LAYER[l]
                act_takes, dve_takes = is_taken_by("act"), is_taken_by("dve")
                for step in steps_of(it):
                    kind, a, i, off = step
                    j = it + off
                    if kind in TAKER:
                        dst = bank[WB + work_bank(kind, a, i)]
                        before = use_before(it, step)
                        if before is not None:
                            back, (kind0, a0, i0, off0) = before
                            who = TAKER[kind0]
                            pe.wait_ge(dict(act=s_tact, dve=s_tdve, res=s_res)[who],
                                       done(number(is_taken_by(who), l, it + (back + off0), kind0, a0, i0)))
                    if kind == "x_turn":
                        pe.wait_ge(s_xn, done(number(is_token_norm, l, j, "norm", a, 0)))
                        for c in range(KC):
                            for s in range(2):
                                ins = turn(dst[:, (2 * c + s) * T:(2 * c + s + 1) * T], xn[:, a, s, c * P:(c + 1) * P], ident)
                        ins.then_inc(s_work, 1)
                    elif kind == "ctx_turn":
                        if cfg["ctx_norm"]:
                            pe.wait_ge(s_cn, done(j))
                        else:
                            pe.wait_ge(s_ctx, (pair_of(l, j) + 1) * 16)
                        src = cn if cfg["ctx_norm"] else cin
                        for c in range(KC):
                            for s in range(2):
                                ins = turn(dst[:, (2 * c + s) * T:(2 * c + s + 1) * T], src[:, s, c * P:(c + 1) * P], ident)
                        ins.then_inc(s_work, 1)
                    elif kind in ("q", "k", "v"):
                        turned_by = ("x_turn", a, 0) if a == SELF or kind == "q" else ("ctx_turn", a, 0)
                        pe.wait_ge(s_tact, done(number(act_takes, l, j, *turned_by)))
                        src = hT if turned_by[0] == "x_turn" else cT
                        at = {("q", 0): W_Q, ("k", 0): W_K, ("v", 0): W_V, ("q", 1): W_XQ, ("k", 1): W_XK, ("v", 1): W_XV}[kind, a]
                        for m in range(2):
                            for c in range(KC):
                                if kind == "v":
                                    ins = mm(dst[:, m * C:(m + 1) * C], src[:, c, m, :], wa[:, c, at:at + C],
                                             start=c == 0, stop=c == KC - 1)
                                else:
                                    ins = mm(dst[:, m * 2 * T:(m + 1) * 2 * T], wa[:, c, at + m * P:at + (m + 1) * P],
                                             src[:, c, :, :].rearrange("p s t -> p (s t)"), start=c == 0, stop=c == KC - 1)
                        ins.then_inc(s_work, 1)
                    elif kind == "scores":
                        k = number(is_chunk, l, j, kind, a, i)
                        s, grp = divmod(i, G)
                        c, half = divmod(grp, 2)
                        if i == 0:
                            pe.wait_ge(s_spread[a], (pair_of(l, j) + 1) * (16 * (P // D)))
                            if cfg["rope"]:
                                pe.wait_ge(s_rope, done(number(is_rotated, l, j, "q", a, 0)))
                            else:
                                pe.wait_ge(s_tact, done(number(act_takes, l, j, "q", a, 0)))
                        before = step_before(it, step, lambda x: x[0] == "scores", 2)
                        if before is not None and is_topk_chunk(l, before[1]):
                            back, (_, a0, i0, off0) = before
                            pe.wait_ge(s_texp, done(number(is_topk_chunk, l, it + (back + off0), "scores", a0, i0)))
                        else:
                            pe.wait_ge(s_shift, freed(k, 2))
                        mm(bank[SC + slot(2, l, j, a, i)][:, :], qT[:, a, c, s, :],
                           kblk[:, a, c, s, HG * half:HG * (half + 1), :].rearrange("p h t -> p (h t)"),
                           start=True, stop=True).then_inc(s_score, 1)
                    elif kind == "turn":
                        k = number(is_chunk, l, j, "scores", a, i)
                        if cfg["topk"] and a == CROSS:
                            pe.wait_ge(s_mask, done(number(is_topk_chunk, l, j, "scores", a, i)))
                        else:
                            pe.wait_ge(s_exp, done(number(is_plain_chunk, l, j, "scores", a, i)))
                        pe.wait_ge(s_probT, freed(k, 1))
                        b = slot(4, l, j, a, i)
                        for h in range(HG):
                            ins = turn(bank[PT][:, h * T:(h + 1) * T], prob[:, b, h, :], ident)
                        ins.then_inc(s_turn, 1)
                    elif kind == "values":
                        k = number(is_chunk, l, j, "scores", a, i)
                        s, grp = divmod(i, G)
                        if i == 0:
                            pe.wait_ge(s_tdve, done(number(dve_takes, l, j, "v", a, 0)))
                        if grp == 0:
                            if s == 0:
                                wait_pair_before(pe, s_out, is_output, l, j, "values", a, 2 * G - 1)
                            else:
                                pe.wait_ge(s_out, done(number(is_output, l, j, "values", a, G - 1)))
                        b = slot(2, l, j, a, i)
                        pe.wait_ge(s_probT, done(k))
                        for h in range(HG):
                            ins = mm(bank[OB + a][0:GW, grp * T:(grp + 1) * T], vaug[:, a, s, grp, h * GW:(h + 1) * GW], probT[:, b, h, :],
                                     start=h == 0, stop=h == HG - 1)
                        ins.then_inc(s_val, 1)
                    elif kind == "out_turn":
                        pe.wait_ge(s_out, done(number(is_output, l, j, "values", a, i * G + G - 1)))
                        for grp in range(G):
                            ins = turn(dst[:, grp * GW:(grp + 1) * GW], outT[:, a, grp, :], ident[0:GW, 0:GW])
                        ins.then_inc(s_work, 1)
                    elif kind == "out_back":
                        pe.wait_ge(s_tdve, done(number(dve_takes, l, j, "out_turn", a, i)))
                        for c in range(KC):
                            ins = turn(dst[:, c * T:(c + 1) * T],
                                       on[:, :, :].rearrange("p h d -> p (h d)")[:, c * P:(c + 1) * P], ident)
                        ins.then_inc(s_work, 1)
                    elif kind == "out_proj":
                        pe.wait_ge(s_tact, done(number(act_takes, l, j, "out_back", a, i)))
                        at = W_SO if a == SELF else W_XO
                        for c in range(KC):
                            ins = mm(dst[:, 0:C], oT[:, c, :], wa[:, c, at:at + C], start=c == 0, stop=c == KC - 1)
                        ins.then_inc(s_work, 1)

            def quad_turn(l, it):
                m = quad_of(l, it)
                pe.wait_ge(s_mxn, done(m))
                pe.wait_ge(s_mh, freed(m, 1))
                for c in range(KC):
                    for s in range(4):
                        ins = turn(bank[6 + c][:, s * T:(s + 1) * T], mxn[:, s, c * P:(c + 1) * P], ident)
                    ins.then_inc(s_mT, 1)

            def mlp_step(l, it, last):
                cfg = LAYER[l]
                m = quad_of(l, it)
                n = ups(l)
                w1 = wm[:, 0:KC * n * P].rearrange("p (c n) -> p c n", c=KC)
                w2 = wm[:, 4096:6144].rearrange("p (c n) -> p c n", c=FC)
                pe.wait_ge(s_mh, done(m))
                for j in range(n):
                    if cfg["swiglu"]:
                        f, lin = divmod(j, 2)
                        col = (f + lin * FC) * P
                        b = 2 * (f % 2) + lin
                        if lin:
                            pe.wait_ge(s_upmul, freed(it * FC + f, 2))
                        else:
                            pe.wait_ge(s_upact, freed(it * FC + f, 2))
                    else:
                        col = j * P
                        b = j % 4
                        pe.wait_ge(s_upact, freed(it * FC + (l * QUADS * FC + j), 4))
                    if j == 3:
                        pe.wait_ge(s_mo, freed(m * 4 + 3, 4))
                    for c in range(KC):
                        ins = mm(bank[b][:, :], w1[:, c, col:col + P], fT[:, c, :, :].rearrange("p s t -> p (s t)"),
                                 start=c == 0, stop=c == KC - 1)
                    ins.then_inc(s_up, 1)
                if last and l + 1 < LAYERS:
                    pe.wait_ge(s_wa, 16 * sum(WA_N[:l + 2]))
                    attention_step(l + 1, FIRST)
                if cfg["swiglu"]:
                    pe.wait_ge(s_upmul, done(it * FC + (FC - 1)))
                else:
                    pe.wait_ge(s_upact, done(it * FC + (l * QUADS * FC + FC - 1)))
                for s in range(4):
                    if s == 2 and not last:
                        quad_turn(l, it + 1)
                    pe.wait_ge(s_mo, freed(m * 4 + s, 2))
                    for f in range(FC):
                        ins = mm(bank[DOWN[s % 2]][:, 0:C], hid[:, f, s * T:(s + 1) * T], w2[:, f, :],
                                 start=f == 0, stop=f == FC - 1)
                    ins.then_inc(s_down, 1)

            for l in range(LAYERS):
                pe.wait_ge(s_wa, 16 * sum(WA_N[:l + 1]))
                if l == 0:
                    attention_step(l, FIRST)
                pe.wait_ge(s_mo, START + 4 * QUADS * l)
                for j in (-1, 0):
                    attention_step(l, j)
                with pe.Fori(1, PAIRS - 2) as j:
                    attention_step(l, j)
                for j in (PAIRS - 2, PAIRS - 1, PAIRS):
                    attention_step(l, j)
                pe.wait_ge(s_out, START + 4 * PAIRS * (l + 1))
                pe.wait_ge(s_res, START + 4 * PAIRS * (l + 1))
                quad_turn(l, 0)
                pe.wait_ge(s_wm, 48 * (l + 1))
                with pe.Fori(0, QUADS - 1) as it:
                    mlp_step(l, it, False)
                mlp_step(l, QUADS - 1, True)


DVE_LINKS = ((34, 9), (25, 9), (24, 9), (30, 5))


_INS = (
    ["x", "cond_1024", "ctx_1024"]
    + ["L0_xcond_" + n for n in ("w_ada b_ada w_qkv b_qkv w_so b_so w_q b_q w_kv b_kv w_co b_co w_m1 b_m1 w_m2 b_m2".split())]
    + ["L1_xcond_" + n for n in ("W_mod b_mod W_qkv b_qkv W_proj b_proj W_qc b_qc W_kvc b_kvc W_cproj b_cproj W_mlp1 b_mlp1 "
                                 "W_mlp2 b_mlp2".split())]
    + ["L2_xcond_" + n for n in ("adaln_w adaln_b qkv_w qkv_b sa_proj_w sa_proj_b q_w q_b kv_w kv_b ca_proj_w ca_proj_b "
                                 "fc1_w fc1_b fc2_w fc2_b".split())]
    + ["L3_xcond_" + n for n in ("ln1_w ln1_b ln2_w ln2_b ln3_w ln3_b qkv_w sa_out_w q_w k_w v_w ca_out_w ffn_w1 ffn_b1 "
                                 "ffn_w2 ffn_b2".split())]
)


def tables():
    import numpy as np

    half = D // 2
    inv_freq = (1.0 / np.float32(10000.0) ** (np.arange(half, dtype=np.float32) / np.float32(half))).astype(np.float32)
    ang = (np.arange(T, dtype=np.float32)[:, None] * inv_freq[None, :]).astype(np.float32)
    comp = np.arange(P) % D
    cos = np.cos(ang)[:, comp % half].T
    sin = np.sin(ang)[:, comp % half].T * np.where(comp < half, -1.0, 1.0)[:, None]
    eps = np.tile(np.array([[1e-6, 1e-5]]), (P, 1))
    return np.ascontiguousarray(np.concatenate([np.eye(P), cos, sin, eps], axis=1).astype(np.float32))


def kernel(**inputs):
    import numpy as _np
    import concourse.bacc as _bacc
    from concourse import mybir as _mybir
    from concourse.bass_utils import run_bass_kernel_spmd as _run

    nc = _bacc.Bacc("TRN2", target_bir_lowering=False, num_devices=1)
    arrays, dram = {}, {}
    for name in _INS:
        a = _np.ascontiguousarray(inputs[name])
        arrays[f"in_{name}_dram"] = a
        dram[name] = nc.dram_tensor(f"in_{name}_dram", a.shape, _mybir.dt.from_np(a.dtype), kind="ExternalInput").ap()
    t = tables()
    arrays["tables_dram"] = t
    dram["tables"] = nc.dram_tensor("tables_dram", t.shape, _mybir.dt.from_np(t.dtype), kind="ExternalInput").ap()
    out = nc.dram_tensor("out_dram", (B, T, C), F32, kind="ExternalOutput").ap()
    build(nc, dram, out)
    r = _run(nc, [arrays], core_ids=[0])
    return r.results[0]["out_dram"]
```
